# Optimizing a Trainium2 kernel written in Bass

```python
import numpy as np
import jax
import jax.numpy as jnp

def _softmax(x, axis=-1):
    return jax.nn.softmax(x, axis=axis)

def _gelu(x):
    return jax.nn.gelu(x, approximate=True)

def _silu(x):
    return jax.nn.silu(x)

def _sigmoid(x):
    return jax.nn.sigmoid(x)

def _layernorm(x, axis=-1, eps=1e-05):
    m = jnp.mean(x, axis=axis, keepdims=True)
    v = jnp.var(x, axis=axis, keepdims=True)
    return (x - m) / jnp.sqrt(v + eps)

def _scatter_add(tgt, idx, src, axis=0):
    return tgt.at[idx].add(src)

def _segment_sum(src, seg, n):
    return jax.ops.segment_sum(src, seg, n)
kernel_name = 'mk_conv_seq_d4_conv_nhwc96_r2_2deded'

def setup_inputs(seed: int=0):
    np.random.seed(seed)
    _w = jnp.asarray

    def _rec_inputs():
        import jax
        import jax.numpy as jnp
        _gk = jax.random.key(seed)
        x = -0.0004039 + 1 * jax.random.normal(jax.random.fold_in(_gk, 1), (8, 64, 64, 48), jnp.float32)
        return x
    x = _rec_inputs()

    def _L0_conv_setup():
        import jax, jax.numpy as jnp
        import numpy as np
        import math
        DIM = 48
        B, H, W = (8, 64, 64)
        BN_EPS = 0.001

        def _l2n(x, axis):
            s = jnp.sum(x * x, axis=axis, keepdims=True)
            return x * jax.lax.rsqrt(jnp.maximum(s, 1e-12))

        def _conv(x, w, padding):
            return jax.lax.conv_general_dilated(x, w, window_strides=(1, 1), padding=padding, dimension_numbers=('NHWC', 'HWIO', 'NHWC'))
        key = jax.random.key(seed)
        ks = jax.random.split(key, 16)
        C = DIM
        sd = lambda fan_in: 1.0 / np.sqrt(fan_in)
        inp = {'x': jax.random.normal(ks[0], (B, H, W, C), jnp.float32), 'w_qkv': jax.random.normal(ks[1], (C, 3 * C), jnp.float32) * sd(C), 'b_qkv': jnp.zeros((3 * C,), jnp.float32), 'w_ln': jax.random.normal(ks[2], (C, C), jnp.float32) * sd(C), 'b_ln': jnp.zeros((C,), jnp.float32), 'bn_gamma': jnp.ones((C,), jnp.float32), 'bn_beta': jnp.zeros((C,), jnp.float32), 'bn_mean': jax.random.normal(ks[3], (C,), jnp.float32) * 0.1, 'bn_var': jax.random.uniform(ks[4], (C,), jnp.float32, 0.5, 1.5), 'w1': jax.random.normal(ks[5], (1, 1, 2 * C, 2 * C), jnp.float32) * sd(2 * C), 'b1': jnp.zeros((2 * C,), jnp.float32), 'w2': jax.random.normal(ks[6], (3, 3, 2 * C, 2 * C), jnp.float32) * sd(9 * 2 * C), 'b2': jnp.zeros((2 * C,), jnp.float32), 'w3': jax.random.normal(ks[7], (1, 1, 2 * C, C), jnp.float32) * sd(2 * C), 'b3': jnp.zeros((C,), jnp.float32)}
        return inp
    _L0_conv_all = _L0_conv_setup()
    _L0_conv_in = {k: v for k, v in _L0_conv_all.items() if k in ('w_qkv', 'b_qkv', 'w_ln', 'b_ln', 'bn_gamma', 'bn_beta', 'bn_mean', 'bn_var', 'w1', 'b1', 'w2', 'b2', 'w3', 'b3')}
    del _L0_conv_all

    def _L1_conv_setup():
        import jax, jax.numpy as jnp
        import numpy as np
        from jax import lax
        BN_EPS = 0.001
        DN = ('NHWC', 'HWIO', 'NHWC')
        key = jax.random.key(seed)
        ks = jax.random.split(key, 8)
        B, H, W, C = (16, 112, 112, 48)
        K = 3
        x = jax.random.normal(ks[0], (B, H, W, C), dtype=jnp.float32)
        dw_kernel = jax.random.normal(ks[1], (K, K, 1, C), dtype=jnp.float32) * 0.1
        dw_bias = jnp.zeros((C,), dtype=jnp.float32)
        pw_kernel = jax.random.normal(ks[2], (1, 1, C, C), dtype=jnp.float32) * 0.1
        pw_bias = jnp.zeros((C,), dtype=jnp.float32)
        gamma = jax.random.uniform(ks[3], (C,), dtype=jnp.float32, minval=0.5, maxval=1.5)
        beta = jax.random.normal(ks[4], (C,), dtype=jnp.float32) * 0.1
        moving_mean = jax.random.normal(ks[5], (C,), dtype=jnp.float32) * 0.1
        moving_var = jax.random.uniform(ks[6], (C,), dtype=jnp.float32, minval=0.5, maxval=1.5)
        return {'x': x, 'dw_kernel': dw_kernel, 'dw_bias': dw_bias, 'pw_kernel': pw_kernel, 'pw_bias': pw_bias, 'gamma': gamma, 'beta': beta, 'moving_mean': moving_mean, 'moving_var': moving_var}
    _L1_conv_all = _L1_conv_setup()
    _L1_conv_in = {k: v for k, v in _L1_conv_all.items() if k in ('dw_kernel', 'dw_bias', 'pw_kernel', 'pw_bias', 'gamma', 'beta', 'moving_mean', 'moving_var')}
    del _L1_conv_all

    def _L2_conv_setup():
        import jax, jax.numpy as jnp
        import numpy as np
        from jax import lax
        EPS = 0.001

        def _bn(x, g, b, m, v):
            return (x - m) * (g * lax.rsqrt(v + EPS)) + b

        def _cond_dw(h, Wdw, bdw, rw):
            E, M = (Wdw.shape[0], Wdw.shape[-1])
            out = jnp.zeros_like(h)
            for i in range(E):
                k = Wdw[i].reshape(3, 3, 1, M)
                y = lax.conv_general_dilated(h, k, window_strides=(1, 1), padding='SAME', dimension_numbers=('NHWC', 'HWIO', 'NHWC'), feature_group_count=M) + bdw[i]
                out = out + y * rw[:, i, None, None, None]
            return out
        key = jax.random.key(seed)
        ks = jax.random.split(key, 24)
        B, H, W, C = (32, 56, 56, 48)
        E, M, F = (4, 192, 48)
        d = {}
        d['x'] = jax.random.normal(ks[0], (B, H, W, C), jnp.float32)
        d['Wr'] = jax.random.normal(ks[1], (C, E), jnp.float32) * 0.1
        d['br'] = jax.random.normal(ks[2], (E,), jnp.float32) * 0.1
        d['Wpw'] = jax.random.normal(ks[3], (E, C, M), jnp.float32) * (2.0 / C) ** 0.5
        d['bpw'] = jax.random.normal(ks[4], (E, M), jnp.float32) * 0.01
        d['Wdw'] = jax.random.normal(ks[5], (E, 3, 3, M), jnp.float32) * 0.1
        d['bdw'] = jax.random.normal(ks[6], (E, M), jnp.float32) * 0.01
        d['Wpwl'] = jax.random.normal(ks[7], (E, M, F), jnp.float32) * (2.0 / M) ** 0.5
        d['bpwl'] = jax.random.normal(ks[8], (E, F), jnp.float32) * 0.01
        d['g1'] = jax.random.uniform(ks[9], (M,), jnp.float32, 0.5, 1.5)
        d['b1'] = jax.random.normal(ks[10], (M,), jnp.float32) * 0.1
        d['m1'] = jax.random.normal(ks[11], (M,), jnp.float32) * 0.1
        d['v1'] = jax.random.uniform(ks[12], (M,), jnp.float32, 0.5, 1.5)
        d['g2'] = jax.random.uniform(ks[13], (M,), jnp.float32, 0.5, 1.5)
        d['b2'] = jax.random.normal(ks[14], (M,), jnp.float32) * 0.1
        d['m2'] = jax.random.normal(ks[15], (M,), jnp.float32) * 0.1
        d['v2'] = jax.random.uniform(ks[16], (M,), jnp.float32, 0.5, 1.5)
        d['g3'] = jax.random.uniform(ks[17], (F,), jnp.float32, 0.5, 1.5)
        d['b3'] = jax.random.normal(ks[18], (F,), jnp.float32) * 0.1
        d['m3'] = jax.random.normal(ks[19], (F,), jnp.float32) * 0.1
        d['v3'] = jax.random.uniform(ks[20], (F,), jnp.float32, 0.5, 1.5)
        return d
    _L2_conv_all = _L2_conv_setup()
    _L2_conv_in = {k: v for k, v in _L2_conv_all.items() if k in ('Wr', 'br', 'Wpw', 'bpw', 'Wdw', 'bdw', 'Wpwl', 'bpwl', 'g1', 'b1', 'm1', 'v1', 'g2', 'b2', 'm2', 'v2', 'g3', 'b3', 'm3', 'v3')}
    del _L2_conv_all

    def _L3_conv_setup():
        import jax, jax.numpy as jnp
        import numpy as np
        from jax import lax
        BN_EPS = 0.001
        DN = ('NHWC', 'HWIO', 'NHWC')
        key = jax.random.key(seed)
        ks = jax.random.split(key, 8)
        B, H, W, C = (16, 112, 112, 48)
        K = 3
        x = jax.random.normal(ks[0], (B, H, W, C), dtype=jnp.float32)
        dw_kernel = jax.random.normal(ks[1], (K, K, 1, C), dtype=jnp.float32) * 0.1
        dw_bias = jnp.zeros((C,), dtype=jnp.float32)
        pw_kernel = jax.random.normal(ks[2], (1, 1, C, C), dtype=jnp.float32) * 0.1
        pw_bias = jnp.zeros((C,), dtype=jnp.float32)
        gamma = jax.random.uniform(ks[3], (C,), dtype=jnp.float32, minval=0.5, maxval=1.5)
        beta = jax.random.normal(ks[4], (C,), dtype=jnp.float32) * 0.1
        moving_mean = jax.random.normal(ks[5], (C,), dtype=jnp.float32) * 0.1
        moving_var = jax.random.uniform(ks[6], (C,), dtype=jnp.float32, minval=0.5, maxval=1.5)
        return {'x': x, 'dw_kernel': dw_kernel, 'dw_bias': dw_bias, 'pw_kernel': pw_kernel, 'pw_bias': pw_bias, 'gamma': gamma, 'beta': beta, 'moving_mean': moving_mean, 'moving_var': moving_var}
    _L3_conv_all = _L3_conv_setup()
    _L3_conv_in = {k: v for k, v in _L3_conv_all.items() if k in ('dw_kernel', 'dw_bias', 'pw_kernel', 'pw_bias', 'gamma', 'beta', 'moving_mean', 'moving_var')}
    del _L3_conv_all
    return {'x': x, 'L0_conv_w_qkv': _L0_conv_in['w_qkv'], 'L0_conv_b_qkv': _L0_conv_in['b_qkv'], 'L0_conv_w_ln': _L0_conv_in['w_ln'], 'L0_conv_b_ln': _L0_conv_in['b_ln'], 'L0_conv_bn_gamma': _L0_conv_in['bn_gamma'], 'L0_conv_bn_beta': _L0_conv_in['bn_beta'], 'L0_conv_bn_mean': _L0_conv_in['bn_mean'], 'L0_conv_bn_var': _L0_conv_in['bn_var'], 'L0_conv_w1': _L0_conv_in['w1'], 'L0_conv_b1': _L0_conv_in['b1'], 'L0_conv_w2': _L0_conv_in['w2'], 'L0_conv_b2': _L0_conv_in['b2'], 'L0_conv_w3': _L0_conv_in['w3'], 'L0_conv_b3': _L0_conv_in['b3'], 'L1_conv_dw_kernel': _L1_conv_in['dw_kernel'], 'L1_conv_dw_bias': _L1_conv_in['dw_bias'], 'L1_conv_pw_kernel': _L1_conv_in['pw_kernel'], 'L1_conv_pw_bias': _L1_conv_in['pw_bias'], 'L1_conv_gamma': _L1_conv_in['gamma'], 'L1_conv_beta': _L1_conv_in['beta'], 'L1_conv_moving_mean': _L1_conv_in['moving_mean'], 'L1_conv_moving_var': _L1_conv_in['moving_var'], 'L2_conv_Wr': _L2_conv_in['Wr'], 'L2_conv_br': _L2_conv_in['br'], 'L2_conv_Wpw': _L2_conv_in['Wpw'], 'L2_conv_bpw': _L2_conv_in['bpw'], 'L2_conv_Wdw': _L2_conv_in['Wdw'], 'L2_conv_bdw': _L2_conv_in['bdw'], 'L2_conv_Wpwl': _L2_conv_in['Wpwl'], 'L2_conv_bpwl': _L2_conv_in['bpwl'], 'L2_conv_g1': _L2_conv_in['g1'], 'L2_conv_b1': _L2_conv_in['b1'], 'L2_conv_m1': _L2_conv_in['m1'], 'L2_conv_v1': _L2_conv_in['v1'], 'L2_conv_g2': _L2_conv_in['g2'], 'L2_conv_b2': _L2_conv_in['b2'], 'L2_conv_m2': _L2_conv_in['m2'], 'L2_conv_v2': _L2_conv_in['v2'], 'L2_conv_g3': _L2_conv_in['g3'], 'L2_conv_b3': _L2_conv_in['b3'], 'L2_conv_m3': _L2_conv_in['m3'], 'L2_conv_v3': _L2_conv_in['v3'], 'L3_conv_dw_kernel': _L3_conv_in['dw_kernel'], 'L3_conv_dw_bias': _L3_conv_in['dw_bias'], 'L3_conv_pw_kernel': _L3_conv_in['pw_kernel'], 'L3_conv_pw_bias': _L3_conv_in['pw_bias'], 'L3_conv_gamma': _L3_conv_in['gamma'], 'L3_conv_beta': _L3_conv_in['beta'], 'L3_conv_moving_mean': _L3_conv_in['moving_mean'], 'L3_conv_moving_var': _L3_conv_in['moving_var']}

def reference(x, L0_conv_w_qkv, L0_conv_b_qkv, L0_conv_w_ln, L0_conv_b_ln, L0_conv_bn_gamma, L0_conv_bn_beta, L0_conv_bn_mean, L0_conv_bn_var, L0_conv_w1, L0_conv_b1, L0_conv_w2, L0_conv_b2, L0_conv_w3, L0_conv_b3, L1_conv_dw_kernel, L1_conv_dw_bias, L1_conv_pw_kernel, L1_conv_pw_bias, L1_conv_gamma, L1_conv_beta, L1_conv_moving_mean, L1_conv_moving_var, L2_conv_Wr, L2_conv_br, L2_conv_Wpw, L2_conv_bpw, L2_conv_Wdw, L2_conv_bdw, L2_conv_Wpwl, L2_conv_bpwl, L2_conv_g1, L2_conv_b1, L2_conv_m1, L2_conv_v1, L2_conv_g2, L2_conv_b2, L2_conv_m2, L2_conv_v2, L2_conv_g3, L2_conv_b3, L2_conv_m3, L2_conv_v3, L3_conv_dw_kernel, L3_conv_dw_bias, L3_conv_pw_kernel, L3_conv_pw_bias, L3_conv_gamma, L3_conv_beta, L3_conv_moving_mean, L3_conv_moving_var):
    import jax
    import jax.numpy as jnp

    def _L0_conv_ref(x, w_qkv, b_qkv, w_ln, b_ln, bn_gamma, bn_beta, bn_mean, bn_var, w1, b1, w2, b2, w3, b3):
        import jax, jax.numpy as jnp
        import numpy as np
        import math
        DIM = 48
        B, H, W = (8, 64, 64)
        BN_EPS = 0.001

        def _l2n(x, axis):
            s = jnp.sum(x * x, axis=axis, keepdims=True)
            return x * jax.lax.rsqrt(jnp.maximum(s, 1e-12))

        def _conv(x, w, padding):
            return jax.lax.conv_general_dilated(x, w, window_strides=(1, 1), padding=padding, dimension_numbers=('NHWC', 'HWIO', 'NHWC'))
        b, h, w, C = x.shape
        N = h * w
        shortcut = x
        xe = x.reshape(b, N, C)
        xn = (xe - bn_mean) * (bn_gamma * jax.lax.rsqrt(bn_var + BN_EPS)) + bn_beta
        qkv = xn @ w_qkv + b_qkv
        q, k, v = jnp.split(qkv, 3, axis=2)
        q = q - jnp.mean(q, axis=2, keepdims=True)
        k = k - jnp.mean(k, axis=2, keepdims=True)
        q2 = q * q
        k2 = k * k
        q2 = _l2n(q2 / (jnp.sum(q2, axis=2, keepdims=True) + 1e-07), axis=2)
        k2 = _l2n(k2 / (jnp.sum(k2, axis=2, keepdims=True) + 1e-07), axis=1)
        kv = jnp.einsum('bnc,bnd->bcd', k2, v)
        t2 = jnp.einsum('bnc,bcd->bnd', q2, kv) / math.sqrt(N)
        attn = (v + t2) @ w_ln + b_ln
        xr = attn.reshape(b, h, w, C)
        y = jnp.concatenate([xr, shortcut], axis=-1)
        y = jax.nn.leaky_relu(_conv(y, w1, 'VALID') + b1, 0.2)
        y = jax.nn.leaky_relu(_conv(y, w2, 'SAME') + b2, 0.2)
        y = _conv(y, w3, 'VALID') + b3
        return y + shortcut

    def _L1_conv_ref(x, dw_kernel, dw_bias, pw_kernel, pw_bias, gamma, beta, moving_mean, moving_var):
        import jax, jax.numpy as jnp
        import numpy as np
        from jax import lax
        BN_EPS = 0.001
        DN = ('NHWC', 'HWIO', 'NHWC')
        C = x.shape[-1]
        stride = 1
        y = jax.nn.relu(x)
        y = lax.conv_general_dilated(y, dw_kernel, window_strides=(stride, stride), padding='SAME', dimension_numbers=DN, feature_group_count=C)
        y = y + dw_bias
        y = lax.conv_general_dilated(y, pw_kernel, window_strides=(1, 1), padding='SAME', dimension_numbers=DN)
        y = y + pw_bias
        inv = gamma * lax.rsqrt(moving_var + BN_EPS)
        y = y * inv + (beta - moving_mean * inv)
        return y

    def _L2_conv_ref(x, Wr, br, Wpw, bpw, Wdw, bdw, Wpwl, bpwl, g1, b1, m1, v1, g2, b2, m2, v2, g3, b3, m3, v3):
        import jax, jax.numpy as jnp
        import numpy as np
        from jax import lax
        EPS = 0.001

        def _bn(x, g, b, m, v):
            return (x - m) * (g * lax.rsqrt(v + EPS)) + b

        def _cond_dw(h, Wdw, bdw, rw):
            E, M = (Wdw.shape[0], Wdw.shape[-1])
            out = jnp.zeros_like(h)
            for i in range(E):
                k = Wdw[i].reshape(3, 3, 1, M)
                y = lax.conv_general_dilated(h, k, window_strides=(1, 1), padding='SAME', dimension_numbers=('NHWC', 'HWIO', 'NHWC'), feature_group_count=M) + bdw[i]
                out = out + y * rw[:, i, None, None, None]
            return out
        shortcut = x
        pooled = jnp.mean(x, axis=(1, 2))
        rw = jax.nn.sigmoid(pooled @ Wr + br)
        Wk = jnp.einsum('be,ecm->bcm', rw, Wpw)
        h = jnp.einsum('bhwc,bcm->bhwm', x, Wk) + (rw @ bpw)[:, None, None, :]
        h = jax.nn.relu(_bn(h, g1, b1, m1, v1))
        h = _cond_dw(h, Wdw, bdw, rw)
        h = jax.nn.relu(_bn(h, g2, b2, m2, v2))
        Wk2 = jnp.einsum('be,emf->bmf', rw, Wpwl)
        h = jnp.einsum('bhwm,bmf->bhwf', h, Wk2) + (rw @ bpwl)[:, None, None, :]
        h = _bn(h, g3, b3, m3, v3)
        return h + shortcut

    def _L3_conv_ref(x, dw_kernel, dw_bias, pw_kernel, pw_bias, gamma, beta, moving_mean, moving_var):
        import jax, jax.numpy as jnp
        import numpy as np
        from jax import lax
        BN_EPS = 0.001
        DN = ('NHWC', 'HWIO', 'NHWC')
        C = x.shape[-1]
        stride = 1
        y = jax.nn.relu(x)
        y = lax.conv_general_dilated(y, dw_kernel, window_strides=(stride, stride), padding='SAME', dimension_numbers=DN, feature_group_count=C)
        y = y + dw_bias
        y = lax.conv_general_dilated(y, pw_kernel, window_strides=(1, 1), padding='SAME', dimension_numbers=DN)
        y = y + pw_bias
        inv = gamma * lax.rsqrt(moving_var + BN_EPS)
        y = y * inv + (beta - moving_mean * inv)
        return y

    def _gn(v, G=32, eps=1e-05):
        B_, H_, W_, C_ = v.shape
        g = v.reshape(B_, H_, W_, G, C_ // G)
        m = jnp.mean(g, axis=(1, 2, 4), keepdims=True)
        s = jnp.var(g, axis=(1, 2, 4), keepdims=True)
        return ((g - m) / jnp.sqrt(s + eps)).reshape(v.shape)

    def _ln_c(v, eps=1e-06):
        m = jnp.mean(v, axis=-1, keepdims=True)
        s = jnp.var(v, axis=-1, keepdims=True)
        return (v - m) / jnp.sqrt(s + eps)

    def _ln_t(v, eps=1e-05):
        m = jnp.mean(v, axis=-1, keepdims=True)
        s = jnp.var(v, axis=-1, keepdims=True)
        return (v - m) / jnp.sqrt(s + eps)

    def _to_tokens(v):
        B_, H_, W_, C_ = v.shape
        return v.reshape(B_, H_ * W_, C_)

    def _from_tokens(t, like):
        return t.reshape(like.shape)
    x = _L0_conv_ref(x, L0_conv_w_qkv, L0_conv_b_qkv, L0_conv_w_ln, L0_conv_b_ln, L0_conv_bn_gamma, L0_conv_bn_beta, L0_conv_bn_mean, L0_conv_bn_var, L0_conv_w1, L0_conv_b1, L0_conv_w2, L0_conv_b2, L0_conv_w3, L0_conv_b3)
    x = _L1_conv_ref(x, L1_conv_dw_kernel, L1_conv_dw_bias, L1_conv_pw_kernel, L1_conv_pw_bias, L1_conv_gamma, L1_conv_beta, L1_conv_moving_mean, L1_conv_moving_var)
    x = _L2_conv_ref(x, L2_conv_Wr, L2_conv_br, L2_conv_Wpw, L2_conv_bpw, L2_conv_Wdw, L2_conv_bdw, L2_conv_Wpwl, L2_conv_bpwl, L2_conv_g1, L2_conv_b1, L2_conv_m1, L2_conv_v1, L2_conv_g2, L2_conv_b2, L2_conv_m2, L2_conv_v2, L2_conv_g3, L2_conv_b3, L2_conv_m3, L2_conv_v3)
    x = _L3_conv_ref(x, L3_conv_dw_kernel, L3_conv_dw_bias, L3_conv_pw_kernel, L3_conv_pw_bias, L3_conv_gamma, L3_conv_beta, L3_conv_moving_mean, L3_conv_moving_var)
    return x

_drawn_inputs = setup_inputs


def setup_inputs(seed=0):
    import zlib

    import numpy as np

    out = dict(_drawn_inputs(seed))
    spreads = {'L0_conv_b_qkv': (0.0, 0.1),
     'L0_conv_b_ln': (0.0, 0.7),
     'L0_conv_bn_gamma': (1.0, 0.6),
     'L0_conv_bn_beta': (0.0, 0.571),
     'L0_conv_b1': (0.0, 0.676),
     'L0_conv_b2': (0.0, 0.778),
     'L0_conv_b3': (0.0, 0.408),
     'L1_conv_dw_bias': (0.0, 0.1),
     'L1_conv_pw_bias': (0.0, 0.1),
     'L3_conv_dw_bias': (0.0, 0.1),
     'L3_conv_pw_bias': (0.0, 0.1)}
    factors = {'L0_conv_bn_mean': 2.849,
     'L0_conv_bn_var': 5.316,
     'L2_conv_bpw': 8.0,
     'L2_conv_bdw': 7.328,
     'L2_conv_bpwl': 6.569,
     'L2_conv_g1': 2.806}
    for name, (base, spread) in spreads.items():
        noise = np.random.default_rng([zlib.crc32(name.encode()), seed]).standard_normal(out[name].shape)
        drawn = base * np.exp(spread * noise) if base else spread * noise
        out[name] = jnp.asarray(drawn.astype(out[name].dtype))
    for name, factor in factors.items():
        out[name] = (out[name] * factor).astype(out[name].dtype)
    return out
```

```python
from contextlib import ExitStack

import concourse.bass as bass
from concourse import mybir

F32 = mybir.dt.float32
F32R = mybir.dt.float32r
ALU = mybir.AluOpType
ACT = mybir.ActivationFunctionType
AX = mybir.AxisListType

IMAGES, H, W, C = 8, 64, 64, 48
C2 = 2 * C
TOKENS = H * W
PAIRS = H // 2
HALF = TOKENS // 2
WQ = 4
RUN = W // WQ
EXPERTS = 4
M = 192
M1 = 128
M2 = M - M1
TAPS = 9
WP = W + 2
BANK = 512
CHUNKS = TOKENS // BANK
PCHUNKS = HALF // BANK
ROWS = BANK // W
Q_AT, X_AT, K_AT, TOK = 0, C, 2 * C, 3 * C + 1
SUMS = 2 * C + 1
BN_EPS = 1e-3
SLOPE = 0.2

T_VAR, T_GAMMA, T_MEAN, T_BETA = 0, 4, 8, 12
L0, L1, L3, L2 = 0, 1, 2, 3
T_BLN, T_B3, T_B2, T_DWB1, T_PWB1, T_DWB3, T_PWB3 = 16, 17, 18, 19, 20, 21, 22
T_S1, T_S3, T_BPWL = 23, 35, 47
T_ROWS = 51
U_VAR, U_GAMMA, U_MEAN, U_BETA, U_BPW, U_BDW, U_WDW = 0, 2, 4, 6, 8, 12, 16
U_ROWS = U_WDW + EXPERTS * TAPS
Y_DW, Y_DWB, Y_B1, Y_B3 = 0, 2 * TAPS, 2 * TAPS + 2, 2 * TAPS + 4
Y_ALL = Y_B3 + 1
E_BOTTOM, E_OTHER, E_ALL = M1, M1 + M2, M1 + 3 * M2


class Ring:

    def __init__(self, banks, readers):
        assert len(readers) % 2 == 0
        self.banks, self.readers = banks, readers

    def bank(self, k):
        return self.banks[k % 2]

    def take(self, pe, image, k):
        sem, each, nth = self.readers[k - 2]
        if k >= 2:
            pe.wait_ge(sem, image * each + nth)
        elif not isinstance(image, int) or image > 0:
            pe.wait_ge(sem, image * each)
        return self.banks[k % 2]


class Chain:

    def __init__(self, sem, each):
        self.sem, self.each = sem, each

    def begin(self, engine, image):
        self.engine, self.image, self.k = engine, image, 0

    def __call__(self, instruction):
        instruction.then_inc(self.sem, 1)
        self.k += 1
        self.engine.wait_ge(self.sem, self.image * self.each + self.k)

    def end(self):
        assert self.k == self.each, self.k


def columns(ap, offset, dims):
    return bass.AP(ap.tensor, ap.offset + offset, [list(ap.ap[0])] + [list(d) for d in dims])


def twice(row_ap):
    (rs, rn), (es, en) = row_ap.ap
    return bass.AP(row_ap.tensor, row_ap.offset, [[rs, rn], [0, 2], [es, en]])


def conv_chain_kernel(nc, a, out):
    ctx = ExitStack()
    with ctx:
        def sb(name, shape, dt=F32):
            return ctx.enter_context(nc.sbuf_tensor(name, shape, dt))

        def sem(name):
            return ctx.enter_context(nc.semaphore(name))

        def row(name):
            return a[name].rearrange("(o n) -> o n", o=1)

        tab96 = sb("tab96", [T_ROWS, C2])
        tab192 = sb("tab192", [U_ROWS, 2 * M1])
        col96 = sb("col96", [C2, T_ROWS])
        colm = sb("colm", [128, 2, U_ROWS])
        ident = sb("ident", [128, 128])
        ones = sb("ones", [128, 128])
        gram_mask = sb("gram_mask", [SUMS, C])
        mask_par = sb("mask_par", [C2, 2])
        mask_half = sb("mask_half", [128, 2])
        inv96, shift96 = sb("inv96", [C2, 4]), sb("shift96", [C2, 4])
        invm, shiftm = sb("invm", [128, 2, 2]), sb("shiftm", [128, 2, 2])
        inv0 = sb("inv0", [C + 1, 1])
        bn_fold = sb("bn_fold", [C + 1, C + 1])
        wqkv = sb("wqkv", [C + 1, 3 * C])
        wln, w1a, w1b = sb("wln", [C, C]), sb("w1a", [C, C2]), sb("w1b", [C + 1, C2])
        wqk = sb("wqk", [C + 1, C2])
        qk_mean = sb("qk_mean", [C + 1, 2])
        wv_t, p1, p1b = sb("wv_t", [C, C + 1]), sb("p1", [C, C + 1]), sb("p1b", [C, C + 1])
        wva, m1w = sb("wva", [C + 1, C2]), sb("m1w", [C + 1, C2])
        qkw = sb("qkw", [C2 + 1, 2 * C2])
        wva_aug = sb("wva_aug", [SUMS, C2])
        w1_cur = sb("w1_cur", [C2 + 1, C2])
        w2_h, w2_l = sb("w2_h", [C2, TAPS, C2], F32R), sb("w2_l", [C2, TAPS, C2], F32R)
        w3eo = sb("w3eo", [C2, 2, C2])
        b2s = sb("b2s", [C2, 1])
        pw = {L1: sb("pw1", [C2, 2, C]), L3: sb("pw3", [C2, 2, C])}
        wt_h = {n: sb(f"wt_h{n}", [C2, 3, 2, C2], F32R) for n in (L1, L3)}
        wt_l = {n: sb(f"wt_l{n}", [C2, 3, 2, C2], F32R) for n in (L1, L3)}
        conv_bias = sb("conv_bias", [C2, 2])
        wpw = sb("wpw", [C2, EXPERTS, E_ALL])
        wr, br = sb("wr", [C2, EXPERTS]), sb("br", [128, EXPERTS])
        wpl = sb("wpl", [128, EXPERTS, 2, C])
        lin, lin_const = sb("lin", [128, Y_ALL, EXPERTS]), sb("lin_const", [128, Y_ALL])
        s1, s2, u, r = (sb(n, [128, k, 2 * RUN]) for n, k in (("s1", 2), ("s2", 1), ("u", 2), ("r", 1)))
        gt, gm = sb("gt", [SUMS, C]), sb("gm", [SUMS, C])
        rk = sb("rk", [C, 1])
        msum, mean, mean_b = sb("msum", [C2, PCHUNKS]), sb("mean", [C2, 1]), sb("mean_b", [C2, 128])
        rwz, rw = sb("rwz", [128, EXPERTS]), sb("rw", [128, EXPERTS])
        prod, dyn = sb("prod", [128, Y_ALL, EXPERTS]), sb("dyn", [128, Y_ALL])
        wk, ew = sb("wk", [C2, E_ALL]), sb("ew", [C2, 2, E_ALL])
        pk = sb("pk", [128, 2, C])
        pc = sb("pc", [128, 3, 3 * C])
        tok = sb("tok", [128, 2, RUN, TOK])
        xcm = sb("xcm", [C2 + 1, RUN * 128])
        xq = sb("xq", [C2 + 1, 2, BANK])
        y1 = sb("y1", [C2, 2, BANK])
        y1_h, y1_l = sb("y1_h", [C2, H + 2, WP], F32R), sb("y1_l", [C2, H + 2, WP], F32R)
        y2 = [t[0:C2, :, :].rearrange("p a n -> p (a n)") for t in (xq, y1)]
        v = sb("v", [C2, 2, BANK])
        a_h = {n: sb(f"a_h{n}", [C2, PAIRS + 2, WP], F32R) for n in (L1, L3)}
        a_l = {n: sb(f"a_l{n}", [C2, PAIRS + 2, WP], F32R) for n in (L1, L3)}
        b_h, b_l = y1_h[:, 1:PAIRS + 1, :], y1_l[:, 1:PAIRS + 1, :]
        x2 = sb("x2", [C2, HALF])
        h1a = sb("h1a", [128, H + 2, WP])
        h1b = sb("h1b", [128, PAIRS + 2, WP])
        dwa = sb("dwa", [128, H, W])
        dwb = sb("dwb", [128, PAIRS, W])
        dwa_flat, dwb_flat = dwa[:, :, :].rearrange("p h w -> p (h w)"), dwb[:, :, :].rearrange("p h w -> p (h w)")
        outc = dwa_flat[0:C2, 0:HALF]
        q4 = dwa_flat[:, HALF:HALF + 2 * RUN * C]
        xa = q4
        ot = dwb_flat[:, 0:2 * RUN * C]
        h1a_flat = h1a[:, :, :].rearrange("p h w -> p (h w)")
        w2_f = h1a_flat[0:C2, 0:TAPS * C2]
        wt_f = h1a_flat[0:C2, TAPS * C2:(TAPS + 6) * C2]

        banks = [ctx.enter_context(nc.psum_tensor(f"bank{n}", [128, BANK], F32)) for n in range(8)]
        loaded, cleared, masks_ready = sem("loaded"), sem("cleared"), sem("masks_ready")
        prep_pe, prep_dve, prep_act, prep_dma = (sem(n) for n in ("prep_pe", "prep_dve", "prep_act", "prep_dma"))
        xa_loaded, x_loaded = sem("xa_loaded"), sem("x_loaded")
        xt_done, qk_done, g_done, m2_done, xqt_done = (sem(n) for n in ("xt_done", "qk_done", "g_done", "m2_done", "xqt_done"))
        conv1_done, conv2_done, w3_done, l1_done = (sem(n) for n in ("conv1_done", "conv2_done", "w3_done", "l1_done"))
        rw_done, expand_done, project_done, l3_done, outt_done = (sem(n) for n in ("rw_done", "expand_done", "project_done", "l3_done", "outt_done"))
        xcm_ready, squared, q4_ready, root_q, root_k = (sem(n) for n in ("xcm_ready", "squared", "q4_ready", "root_q", "root_k"))
        norm_q, norm_k = sem("norm_q"), sem("norm_k")
        u_ready, q_scaled, k_scaled = sem("u_ready"), sem("q_scaled"), sem("k_scaled")
        gt_ready, w1_ready = sem("gt_ready"), sem("w1_ready")
        xq_ready, y1_slope, y1_max, y1h_ready, y1l_ready = (sem(n) for n in ("xq_ready", "y1_slope", "y1_max", "y1h_ready", "y1l_ready"))
        y2_slope, y2_ready, v_ready, ah1_ready, al1_ready = (sem(n) for n in ("y2_slope", "y2_ready", "v_ready", "ah1_ready", "al1_ready"))
        b1_copied, b3_copied = sem("b1_copied"), sem("b3_copied")
        x2_ready, mean_ready, rwz_ready, rw_ready = (sem(n) for n in ("x2_ready", "mean_ready", "rwz_ready", "rw_ready"))
        h1_ready, tap1_ready, dw_ready, h2_ready = (sem(n) for n in ("h1_ready", "tap1_ready", "dw_ready", "h2_ready"))
        v3_affine, v3_ready, ah3_ready, al3_ready = (sem(n) for n in ("v3_affine", "v3_ready", "ah3_ready", "al3_ready"))
        sync_waits = sem("sync_waits")
        outc_ready, ot_ready, stored = sem("outc_ready"), sem("ot_ready"), sem("stored")
        attn_chain, attn2_chain = Chain(sem("attn_chain"), 5), Chain(sem("attn2_chain"), 2)
        weight_chain = Chain(sem("weight_chain"), 8)
        rk_ready, mean_sum, pc_ready = sem("rk_ready"), sem("mean_sum"), sem("pc_ready")
        project_weight_chain = Chain(sem("project_weight_chain"), 4)
        tap_step = sem("tap_step")

        A_XT, A_QK, A_G, A_M2, A_XQ = 0, 4, 12, 13, 14
        ring_a = Ring(banks[0:2], [(xcm_ready, 4, n + 1) for n in range(4)]
                      + [(squared, 16, 2 * n + 2) for n in range(8)]
                      + [(gt_ready, 2, 2), (w1_ready, 1, 1)]
                      + [(xq_ready, CHUNKS, n + 1) for n in range(CHUNKS)])
        B_W3, B_L1, B_RW, B_HALO, B_E = 0, 4, 8, 9, 10
        ring_b = Ring(banks[2:4], [(v_ready, PCHUNKS, n + 1) for n in range(PCHUNKS)]
                      + [(x2_ready, PCHUNKS, n + 1) for n in range(PCHUNKS)]
                      + [(rwz_ready, 1, 1), (h1_ready, 14, 2)]
                      + [(h1_ready, 14, n + 3) for n in range(12)])
        C_1, C_2 = 0, 8
        ring_c = Ring(banks[4:6], [(y1_max, CHUNKS, n + 1) for n in range(CHUNKS)]
                      + [(y2_ready, CHUNKS, n + 1) for n in range(CHUNKS)])
        D_P, D_L3, D_OUT = 0, 4, 8
        ring_d = Ring(banks[6:8], [(v3_affine, PCHUNKS, n + 1) for n in range(PCHUNKS)]
                      + [(outc_ready, PCHUNKS, n + 1) for n in range(PCHUNKS)]
                      + [(ot_ready, 4, n + 1) for n in range(4)])

        UNITS = CHUNKS + PCHUNKS

        def unit(n):
            if n < PCHUNKS:
                return h1b, dwb[:, n * ROWS:(n + 1) * ROWS, :], 1, n * ROWS
            n -= PCHUNKS
            return h1a, dwa[:, n * ROWS:(n + 1) * ROWS, :], 0, n * ROWS

        def tap_input(n, t):
            src, _, _, r0 = unit(n)
            return src[:, r0 + t // 3:r0 + t // 3 + ROWS, t % 3:t % 3 + W]

        def units_for(k):
            left = UNITS - EARLY
            return range(EARLY + left * k // CHUNKS, EARLY + left * (k + 1) // CHUNKS)

        loads = []

        def load(dst, src):
            loads.append((dst, src))

        def flat2(name):
            return a[name]

        bn_names = {L0: ("L0_conv_bn_var", "L0_conv_bn_gamma", "L0_conv_bn_mean", "L0_conv_bn_beta"),
                    L1: ("L1_conv_moving_var", "L1_conv_gamma", "L1_conv_moving_mean", "L1_conv_beta"),
                    L3: ("L3_conv_moving_var", "L3_conv_gamma", "L3_conv_moving_mean", "L3_conv_beta"),
                    L2: ("L2_conv_v3", "L2_conv_g3", "L2_conv_m3", "L2_conv_b3")}

        def both(r0, rows, src):
            load(tab96[r0:r0 + rows, :].rearrange("r (a c) -> r a c", a=2), twice(src))

        load(wqkv[0:C, :], a["L0_conv_w_qkv"])
        load(wqkv[C:C + 1, :], row("L0_conv_b_qkv"))
        load(wln[:, :], a["L0_conv_w_ln"])
        w1_rows = a["L0_conv_w1"].rearrange("a b i o -> (a b i) o")
        load(w1a[:, :], w1_rows[0:C, :])
        load(w1b[0:C, :], w1_rows[C:C2, :])
        load(w1b[C:C + 1, :], row("L0_conv_b1"))
        for n, names in bn_names.items():
            for r0, name in zip((T_VAR, T_GAMMA, T_MEAN, T_BETA), names):
                both(r0 + n, 1, row(name))
        for r0, name in ((T_BLN, "L0_conv_b_ln"), (T_B3, "L0_conv_b3"), (T_DWB1, "L1_conv_dw_bias"),
                         (T_PWB1, "L1_conv_pw_bias"), (T_DWB3, "L3_conv_dw_bias"), (T_PWB3, "L3_conv_pw_bias")):
            both(r0, 1, row(name))
        load(tab96[T_B2:T_B2 + 1, :], row("L0_conv_b2"))
        both(T_BPWL, EXPERTS, a["L2_conv_bpwl"])
        for r0, name in ((T_S1, "L1_conv_dw_kernel"), (T_S3, "L3_conv_dw_kernel")):
            dw = a[name].rearrange("h w o c -> h (w o) c")
            for g, (even, odd) in enumerate(((1, 2), (0, 1), (None, 0), (2, None))):
                for par, kh in enumerate((even, odd)):
                    if kh is not None:
                        load(tab96[r0 + 3 * g:r0 + 3 * g + 3, par * C:(par + 1) * C], dw[kh])
        for r0, name in ((U_VAR, "L2_conv_v1"), (U_VAR + 1, "L2_conv_v2"), (U_GAMMA, "L2_conv_g1"),
                         (U_GAMMA + 1, "L2_conv_g2"), (U_MEAN, "L2_conv_m1"), (U_MEAN + 1, "L2_conv_m2"),
                         (U_BETA, "L2_conv_b1"), (U_BETA + 1, "L2_conv_b2")):
            load(tab192[r0:r0 + 1, 0:M], row(name))
            load(tab192[r0:r0 + 1, M:M + M2], row(name)[:, M1:M])
        for r0, rows, src in ((U_BPW, EXPERTS, a["L2_conv_bpw"]), (U_BDW, EXPERTS, a["L2_conv_bdw"]),
                              (U_WDW, EXPERTS * TAPS, a["L2_conv_Wdw"].rearrange("e h w m -> (e h w) m"))):
            load(tab192[r0:r0 + rows, 0:M], src)
            load(tab192[r0:r0 + rows, M:M + M2], src[:, M1:M])
        load(w2_f.rearrange("p (t o) -> p t o", t=TAPS), a["L0_conv_w2"].rearrange("h w i o -> i (h w) o"))
        w3_rows = a["L0_conv_w3"].rearrange("a b i o -> (a b i) o")
        for par in range(2):
            load(w3eo[:, par, par * C:(par + 1) * C], w3_rows)
            half = slice(par * C, (par + 1) * C)
            for n, name in ((L1, "L1_conv_pw_kernel"), (L3, "L3_conv_pw_kernel")):
                load(pw[n][half, :, :], twice(a[name].rearrange("a b i o -> (a b i) o")))
            wpw_src = a["L2_conv_Wpw"].rearrange("e c m -> c e m")
            load(wpw[half, :, 0:M1], wpw_src[:, :, 0:M1])
            load(wpw[half, :, E_OTHER:E_OTHER + M2], wpw_src[:, :, M1:M])
            load(wr[half, :], a["L2_conv_Wr"])
            wpl_src = a["L2_conv_Wpwl"].rearrange("e m f -> m e f")
            load(wpl[par * M2:(par + 1) * M2, :, 1, :], wpl_src[M1:M])
        load(wpl[:, :, 0, :], wpl_src[0:M1])
        br_row = row("L2_conv_br")
        load(br[:, :], bass.AP(br_row.tensor, br_row.offset, [[0, 128], [1, EXPERTS]]))

        cleared_tiles = [tab96, qkw, wva_aug, w3eo, wpw]
        placements = [
            (qkw[0:C, 0:C2], wqk[0:C, :]), (qkw[C:C2, C2:2 * C2], wqk[0:C, :]),
            (qkw[C2:C2 + 1, 0:C2], wqk[C:C + 1, :]), (qkw[C2:C2 + 1, C2:2 * C2], wqk[C:C + 1, :]),
            (wva_aug[0:C, :], wva[0:C, :]), (wva_aug[C2:C2 + 1, :], wva[C:C + 1, :]),
            (w1_cur[C:C2 + 1, :], m1w[:, :]),
        ]

        def y1_tokens(k):
            return columns(y1[:, :, :], (k % 2) * BANK, [[WQ, PAIRS], [1, WQ], [128, 4]])

        def y1_view(tile, k):
            par, i0 = k // 4, 4 * (k % 4)
            return columns(tile[:, :, :], (1 + par) * WP + 1 + i0, [[2 * WP, PAIRS], [RUN, WQ], [1, 4]])

        def tokens(at, outer=()):
            return columns(tok[:, :, :, :], at, [*outer, [TOK, 2 * RUN], [1, C]])

        def token(par, i, at, n):
            return tok[:, par, i, at:at + n]

        def after(engine, semaphore, value):
            if not isinstance(value, int) or value > 0:
                engine.wait_ge(semaphore, value)

        marks = {}
        EARLY = 2

        block = ctx.enter_context(nc.Block())

        @block.vector
        def _(dve):
            for n, tile in enumerate(cleared_tiles):
                nc.vector.memset(tile[:], 0.0).then_inc(cleared, 1)
            steps = [0]

            def step(instruction, name=None):
                instruction.then_inc(prep_dve, 1)
                steps[0] += 1
                dve.wait_ge(prep_dve, steps[0])
                if name is not None:
                    marks[name] = steps[0]

            for tile in (pc, lin, lin_const):
                step(nc.vector.memset(tile[:], 0.0))
            for tile in (inv0, ones):
                step(nc.vector.memset(tile[:], 1.0))
            step(nc.vector.memset(tok[:, :, :, TOK - 1], 1.0))
            step(nc.vector.memset(xcm[C2:C2 + 1, :], 1.0))
            step(nc.vector.memset(xq[C2:C2 + 1, :, :], 1.0))
            step(nc.vector.memset(mask_par[:, 0:1], 0.0))
            step(nc.vector.memset(mask_par[0:C, 0:1], 1.0))
            step(nc.vector.tensor_scalar(mask_par[:, 1:2], mask_par[:, 0:1], -1.0, 1.0, ALU.mult, ALU.add))
            step(nc.vector.memset(mask_half[:, :], 0.0))
            for half in range(2):
                step(nc.vector.memset(mask_half[half * M2:(half + 1) * M2, half:half + 1], 1.0))
            for tile in (y1_h, y1_l, a_h[L1], a_l[L1], a_h[L3], a_l[L3], h1b):
                rows = tile.shape[1]
                edge = tile[:, :, :] if tile is h1b else tile[:, :, :].bitcast(F32)
                step(nc.vector.memset(edge[:, 0:rows:rows - 1, :], 0.0))
                step(nc.vector.memset(edge[:, :, 0:WP:WP - 1], 0.0))
            dve.wait_ge(prep_pe, 1)
            step(nc.vector.tensor_copy(col96[:, :], banks[0][0:C2, 0:T_ROWS]))
            dve.wait_ge(prep_pe, 3)
            step(nc.vector.tensor_copy(colm[:, :, :], banks[1][:, 0:2 * 64].rearrange("p (c u) -> p c u", c=2)[:, :, 0:U_ROWS]))
            step(nc.vector.tensor_scalar_add(inv96[:, :], col96[:, T_VAR:T_VAR + 4], BN_EPS))
            step(nc.vector.tensor_scalar_add(invm[:, :, :], colm[:, :, U_VAR:U_VAR + 2], BN_EPS), "variances")
            dve.wait_ge(prep_act, 2)
            step(nc.vector.reciprocal(inv96[:, :], inv96[:, :]))
            step(nc.vector.reciprocal(invm[:, :, :], invm[:, :, :]))
            for inv, shift, tab, g, m, b, n in ((inv96[:, :], shift96[:, :], col96[:, :], T_GAMMA, T_MEAN, T_BETA, 4),
                                                (invm[:, :, :], shiftm[:, :, :], colm[:, :, :], U_GAMMA, U_MEAN, U_BETA, 2)):
                step(nc.vector.tensor_tensor(inv, inv, tab[..., g:g + n], ALU.mult))
                step(nc.vector.tensor_tensor(shift, inv, tab[..., m:m + n], ALU.mult))
                step(nc.vector.tensor_tensor(shift, tab[..., b:b + n], shift, ALU.subtract))
            step(nc.vector.tensor_copy(inv0[0:C, :], inv96[0:C, L0:L0 + 1]))
            step(nc.vector.tensor_scalar(bn_fold[:, :], ident[0:C + 1, 0:C + 1], inv0[:, 0:1], None, ALU.mult))
            step(nc.vector.tensor_copy(bn_fold[0:C, C:C + 1], shift96[0:C, L0:L0 + 1]), "bn_fold")
            dve.wait_ge(prep_pe, 5)
            step(nc.vector.tensor_copy(wv_t[:, :], banks[3][0:C, 0:C + 1]), "wv_t")
            qk = banks[2][0:C + 1, 0:C2].rearrange("p (s c) -> p s c", s=2)
            step(nc.vector.tensor_reduce(qk_mean[:, :], qk, axis=AX.X, op=ALU.add))
            step(nc.vector.tensor_scalar(qk_mean[:, :], qk_mean[:, :], -1.0 / C, None, ALU.mult))
            step(nc.vector.tensor_tensor(wqk[:, :].rearrange("p (s c) -> p s c", s=2), qk,
                                         columns(qk_mean[:, :], 0, [[1, 2], [0, C]]), ALU.add))
            dve.wait_ge(prep_pe, 6)
            step(nc.vector.tensor_copy(p1[:, :], banks[4][0:C, 0:C + 1]))
            step(nc.vector.tensor_copy(p1b[:, :], p1[:, :]))
            step(nc.vector.tensor_tensor(p1b[:, C:C + 1], p1[:, C:C + 1], col96[0:C, T_BLN:T_BLN + 1], ALU.add), "p1")
            dve.wait_ge(prep_pe, 8)
            step(nc.vector.tensor_copy(wva[:, :], banks[5][0:C + 1, 0:C2]))
            step(nc.vector.tensor_copy(m1w[:, :], banks[6][0:C + 1, 0:C2]), "placed")
            step(nc.vector.tensor_scalar(b2s[:, :], col96[:, T_B2:T_B2 + 1], SLOPE, None, ALU.mult), "attention")
            w2_src = w2_f.rearrange("p (t o) -> p t o", t=TAPS)
            step(nc.vector.tensor_copy(w2_h[:, :, :], w2_src))
            step(nc.vector.tensor_tensor(w2_l[:, :, :], w2_src, w2_h[:, :, :].bitcast(F32), ALU.subtract))
            dve.wait_ge(prep_pe, 10)
            for n, (layer, s0, pwb) in enumerate(((L1, T_S1, T_PWB1), (L3, T_S3, T_PWB3))):
                step(nc.vector.scalar_tensor_tensor(out=conv_bias[:, n:n + 1], in0=banks[7][0:C2, n:n + 1],
                                                    scalar=col96[:, pwb:pwb + 1], in1=inv96[:, layer:layer + 1],
                                                    op0=ALU.add, op1=ALU.mult))
                step(nc.vector.tensor_tensor(conv_bias[:, n:n + 1], conv_bias[:, n:n + 1], shift96[:, layer:layer + 1], ALU.add))
                step(nc.vector.tensor_tensor(wt_f.rearrange("p (k g o) -> p k g o", k=3, g=4),
                                             columns(col96[:, :], s0, [[1, 3], [3, 4], [0, C]]),
                                             columns(pw[layer][:, :, :], 0, [[0, 3], [0, 4], [1, C]]), ALU.mult))
                flat = [t[layer][:, :, :, :].rearrange("p k b o -> p (k b o)") for t in (wt_h, wt_l)]
                step(nc.vector.tensor_copy(flat[0], wt_f))
                step(nc.vector.tensor_tensor(flat[1], wt_f, flat[0].bitcast(F32), ALU.subtract))
            for c in range(2):
                w_in = colm[:, c, U_WDW:U_ROWS].rearrange("p (e t) -> p t e", e=EXPERTS)
                step(nc.vector.tensor_scalar(lin[:, Y_DW + c * TAPS:Y_DW + (c + 1) * TAPS, :], w_in,
                                             invm[:, c, 1:2], None, ALU.mult))
                step(nc.vector.tensor_scalar(lin[:, Y_DWB + c, :], colm[:, c, U_BDW:U_BDW + EXPERTS], invm[:, c, 1:2], None, ALU.mult))
                step(nc.vector.tensor_scalar(lin[:, Y_B1 + c, :], colm[:, c, U_BPW:U_BPW + EXPERTS], invm[:, c, 0:1], None, ALU.mult))
                step(nc.vector.tensor_copy(lin_const[:, Y_DWB + c:Y_DWB + c + 1], shiftm[:, c, 1:2]))
                step(nc.vector.tensor_copy(lin_const[:, Y_B1 + c:Y_B1 + c + 1], shiftm[:, c, 0:1]))
            step(nc.vector.tensor_scalar(lin[0:C2, Y_B3, :], col96[:, T_BPWL:T_BPWL + EXPERTS], inv96[:, L2:L2 + 1], None, ALU.mult))
            step(nc.vector.tensor_copy(lin_const[0:C2, Y_B3:Y_B3 + 1], shift96[:, L2:L2 + 1]))
            step(nc.vector.memset(h1a[:, 0:H + 2:H + 1, :], 0.0))
            step(nc.vector.memset(h1a[:, :, 0:WP:WP - 1], 0.0), "all")

            def norms_begin(image):
                attn_chain.begin(dve, image)
                dve.wait_ge(squared, 16 * image + 16)
                attn_chain(nc.vector.tensor_reduce(s1[:, :, :], tokens(Q_AT, [[K_AT - Q_AT, 2]]), axis=AX.X, op=ALU.add))
                attn_chain(nc.vector.tensor_scalar_add(s1[:, :, :], s1[:, :, :], 1e-7))
                nc.vector.reciprocal(u[:, :, :], s1[:, :, :]).then_inc(u_ready, 1)
                dve.wait_ge(q4_ready, image + 1)
                dve.wait_ge(u_ready, image + 1)
                attn_chain(nc.vector.tensor_reduce(s2[:, 0, :], q4.rearrange("p (n c) -> p n c", c=C), axis=AX.X, op=ALU.add))
                attn_chain(nc.vector.tensor_tensor(s2[:, 0, :], s2[:, 0, :], u[:, 0, :], ALU.mult))
                attn_chain(nc.vector.tensor_tensor(s2[:, 0, :], s2[:, 0, :], u[:, 0, :], ALU.mult))
                nc.vector.tensor_scalar_max(s2[:, 0, :], s2[:, 0, :], 1e-12).then_inc(norm_q, 1)
                attn_chain.end()

            def norms_end(image):
                attn2_chain.begin(dve, image)
                dve.wait_ge(root_q, image + 1)
                attn2_chain(nc.vector.reciprocal(r[:, 0, :], s2[:, 0, :]))
                attn2_chain(nc.vector.tensor_tensor(r[:, 0, :], r[:, 0, :], u[:, 0, :], ALU.mult))
                q = tokens(Q_AT)
                nc.vector.tensor_tensor(q, q, columns(r[:, :, :], 0, [[1, 2 * RUN], [0, C]]), ALU.mult).then_inc(q_scaled, 1)
                attn2_chain.end()

            def sums_out(image):
                bank = ring_a.bank(A_G)
                dve.wait_ge(g_done, image + 1)
                nc.vector.tensor_copy(gt[:, :], bank[0:SUMS, 0:C]).then_inc(gt_ready, 1)
                nc.vector.tensor_tensor(gm[:, :], bank[0:SUMS, 0:C], gram_mask[:, :], ALU.mult).then_inc(gt_ready, 1)

            def conv1_weights(image):
                bank = ring_a.bank(A_M2)
                dve.wait_ge(m2_done, image + 1)
                nc.vector.tensor_scalar_max(rk[:, :], bank[0:C, C2:C2 + 1], 1e-12).then_inc(norm_k, 1)
                dve.wait_ge(root_k, image + 1)
                nc.vector.reciprocal(rk[:, :], rk[:, :]).then_inc(rk_ready, 1)
                dve.wait_ge(rk_ready, image + 1)
                nc.vector.tensor_scalar(w1_cur[0:C, :], bank[0:C, 0:C2], rk[:, 0:1], None, ALU.mult).then_inc(w1_ready, 1)

            def conv1_out(image):
                after(dve, l3_done, PCHUNKS * (image - 1))
                for k in range(CHUNKS):
                    dve.wait_ge(y1_slope, CHUNKS * image + k + 1)
                    bank = ring_c.bank(C_1 + k)
                    nc.vector.tensor_tensor(y1[:, k % 2, :], bank[0:C2, :], y1[:, k % 2, :], ALU.max).then_inc(y1_max, 1)
                    dve.wait_ge(y1_max, CHUNKS * image + k + 1)
                    nc.vector.tensor_copy(y1_view(y1_h, k), y1_tokens(k)).then_inc(y1h_ready, 1)

            def depthwise(image, n):
                _, dst, c, _ = unit(n)
                dve.wait_ge(tap1_ready, UNITS * image + n + 1)
                for t in range(1, TAPS):
                    at = Y_DW + c * TAPS + t
                    last = nc.vector.scalar_tensor_tensor(out=dst, in0=tap_input(n, t), scalar=dyn[:, at:at + 1],
                                                          in1=dst, op0=ALU.mult, op1=ALU.add)
                    if t < TAPS - 1:
                        last.then_inc(tap_step, 1)
                        dve.wait_ge(tap_step, (TAPS - 2) * (UNITS * image + n) + t)
                last.then_inc(dw_ready, 1)

            def conv2_out(f, back):
                for k in range(CHUNKS + 1):
                    if k < CHUNKS:
                        dve.wait_ge(y2_slope, CHUNKS * f + k + 1)
                        dst = y2[(k // 2) % 2][:, (k % 2) * BANK:(k % 2 + 1) * BANK]
                        nc.vector.scalar_tensor_tensor(out=dst, in0=ring_c.bank(C_2 + k)[0:C2, :],
                                                       scalar=col96[:, T_B2:T_B2 + 1], in1=dst,
                                                       op0=ALU.add, op1=ALU.max).then_inc(y2_ready, 1)
                    m = k // 2 - 1
                    if k >= 2 and k % 2 == 0:
                        dve.wait_ge(w3_done, PCHUNKS * f + m + 1)
                        if m >= 2:
                            dve.wait_ge(ah1_ready, PCHUNKS * f + m - 1)
                        x_in = columns(xcm[0:C2, :], m * ROWS * WQ, [[1, ROWS * WQ], [128, RUN]])
                        nc.vector.scalar_tensor_tensor(
                            out=v[:, m % 2, :].rearrange("p (a b) -> p a b", b=RUN),
                            in0=ring_b.bank(B_W3 + m)[0:C2, :].rearrange("p (a b) -> p a b", b=RUN),
                            scalar=col96[:, T_B3:T_B3 + 1], in1=x_in, op0=ALU.add, op1=ALU.add).then_inc(v_ready, 1)
                    if back is not None and k < CHUNKS:
                        for n in units_for(k):
                            depthwise(back, n)
                    if k >= 2 and k % 2 == 0:
                        dve.wait_ge(ah1_ready, PCHUNKS * f + m + 1)
                        low_part(a_h[L1], a_l[L1], v, m).then_inc(al1_ready, 1)

            def low_part(hi, lo, src, m):
                rows = slice(m * ROWS + 1, (m + 1) * ROWS + 1)
                return nc.vector.scalar_tensor_tensor(
                    out=lo[:, rows, 1:W + 1], in0=src[:, m % 2, :].rearrange("p (j w) -> p j w", w=W), scalar=0.0,
                    in1=hi[:, rows, 1:W + 1].bitcast(F32), op0=ALU.max, op1=ALU.subtract)

            def project_out(b):
                for m in range(PCHUNKS):
                    dve.wait_ge(v3_affine, PCHUNKS * b + m + 1)
                    nc.vector.tensor_tensor(v[:, m % 2, :], v[:, m % 2, :], x2[:, m * BANK:(m + 1) * BANK], ALU.add)\
                        .then_inc(v3_ready, 1)
                    dve.wait_ge(ah3_ready, PCHUNKS * b + m + 1)
                    low_part(a_h[L3], a_l[L3], v, m).then_inc(al3_ready, 1)

            def mean_out(f):
                dve.wait_ge(x2_ready, PCHUNKS * f + PCHUNKS)
                nc.vector.tensor_reduce(mean[:, :], msum[:, :], axis=AX.X, op=ALU.add).then_inc(mean_sum, 1)
                dve.wait_ge(mean_sum, f + 1)
                nc.vector.tensor_scalar(mean_b[:, :], ones[0:C2, :], mean[:, 0:1], 1.0 / TOKENS, ALU.mult, ALU.mult)\
                    .then_inc(mean_ready, 1)

            def route(f):
                dve.wait_ge(rw_done, f + 1)
                nc.vector.tensor_tensor(rwz[:, :], ring_b.bank(B_RW)[:, 0:EXPERTS], br[:, :], ALU.add).then_inc(rwz_ready, 1)

            def mix(chain, dst, src):
                chain(nc.vector.tensor_scalar(dst, src[:, 0, :], rw[0:dst.shape[0], 0:1], None, ALU.mult))
                for e in range(1, EXPERTS):
                    chain(nc.vector.scalar_tensor_tensor(out=dst, in0=src[:, e, :], scalar=rw[0:dst.shape[0], e:e + 1],
                                                         in1=dst, op0=ALU.mult, op1=ALU.add))

            def mix_weights(f):
                weight_chain.begin(dve, f)
                dve.wait_ge(rw_ready, f + 1)
                weight_chain(nc.vector.tensor_tensor(prod[:, :, :], lin[:, :, :], columns(rw[:, :], 0, [[0, Y_ALL], [1, EXPERTS]]), ALU.mult))
                weight_chain(nc.vector.tensor_reduce(dyn[:, :], prod[:, :, :], axis=AX.X, op=ALU.add))
                weight_chain(nc.vector.tensor_tensor(dyn[:, :], dyn[:, :], lin_const[:, :], ALU.add))
                mix(weight_chain, wk[:, :], wpw[:, :, :])
                nc.vector.tensor_scalar(ew[:, 0, :], wk[:, :], mask_par[:, 0:1], None, ALU.mult)
                weight_chain(nc.vector.tensor_scalar(ew[:, 1, :], wk[:, :], mask_par[:, 1:2], None, ALU.mult))
                weight_chain.end()
                project_weight_chain.begin(dve, f)
                mix(project_weight_chain, pk[:, :, :].rearrange("p c f -> p (c f)"),
                    wpl[:, :, :, :].rearrange("p e c f -> p e (c f)"))
                project_weight_chain.end()
                nc.vector.tensor_copy(pc[:, 0, C:C2], pk[:, 0, :]).then_inc(pc_ready, 1)
                for half in range(2):
                    nc.vector.tensor_scalar(pc[:, 1 + half, C:C2], pk[:, 1, :], mask_half[:, half:half + 1], None, ALU.mult)\
                        .then_inc(pc_ready, 1)

            def iteration(f, attn, back):
                conv2_out(f, back)
                if back is not None:
                    project_out(back)
                mean_out(f)
                if attn is not None:
                    norms_begin(attn)
                route(f)
                mix_weights(f)
                if attn is not None:
                    norms_end(attn)
                    sums_out(attn)
                    conv1_weights(attn)
                for n in range(EARLY):
                    depthwise(f, n)
                if attn is not None:
                    conv1_out(attn)

            norms_begin(0)
            norms_end(0)
            sums_out(0)
            conv1_weights(0)
            conv1_out(0)
            iteration(0, 1, None)
            with dve.Fori(1, IMAGES - 1) as f:
                iteration(f, f + 1, f - 1)
            iteration(IMAGES - 1, None, IMAGES - 2)
            for n in range(EARLY, UNITS):
                depthwise(IMAGES - 1, n)
            project_out(IMAGES - 1)

        def wait(sp, semaphore, value):
            if not isinstance(value, int) or value > 0:
                sp.wait_ge(semaphore, value)
                sp.sem_inc(sync_waits, 1)

        def load_x(sp, image, transposed_images, projected_images):
            src = a["x"][image].rearrange("(j b) (q i) c -> b q j i c", b=2, q=WQ)
            wait(sp, project_done, PCHUNKS * projected_images)
            by_column = xa.rearrange("p (i b c) -> p b i c", b=2, c=C)
            for n in range(2 * WQ):
                par, q = n % 2, n // 2
                sp.dma_start(by_column[q::WQ, par], src[par, q]).then_inc(xa_loaded, 16)
            wait(sp, xqt_done, CHUNKS * transposed_images)
            for n in range(2 * WQ):
                par, q = n % 2, n // 2
                sp.dma_start(tok[q::WQ, par, :, X_AT:X_AT + C], src[par, q]).then_inc(x_loaded, 16)

        def copy_beside(sp, n, copied):
            for hi_or_lo in ((b_h, a_h[n]), (b_l, a_l[n])):
                dst, src = (t[:, :, :].bitcast(F32) for t in hi_or_lo)
                sp.dma_start(dst[0:C, :, :], src[0:C, 2:PAIRS + 2, :]).then_inc(copied, 16)
                sp.dma_start(dst[C:C2, :, :], src[C:C2, 0:PAIRS, :]).then_inc(copied, 16)

        def store(sp, image):
            wait(sp, ot_ready, 4 * image + 4)
            dst = out[image].rearrange("(j b) (q i) c -> q j b (i c)", b=2, q=WQ)
            for q in range(WQ):
                sp.dma_start(dst[q], ot[q::WQ, :].rearrange("p (b n) -> p b n", b=2)).then_inc(stored, 16)

        def beside_l1(sp, f):
            wait(sp, ah1_ready, PCHUNKS * f + PCHUNKS)
            wait(sp, al1_ready, PCHUNKS * f + PCHUNKS)
            wait(sp, conv2_done, CHUNKS * f + CHUNKS)
            wait(sp, l3_done, PCHUNKS * (f - 1))
            copy_beside(sp, L1, b1_copied)

        def beside_l3(sp, b, l1_images):
            wait(sp, ah3_ready, PCHUNKS * b + PCHUNKS)
            wait(sp, al3_ready, PCHUNKS * b + PCHUNKS)
            wait(sp, l1_done, PCHUNKS * l1_images)
            copy_beside(sp, L3, b3_copied)

        @block.sync
        def _(sp):
            load_x(sp, 0, 0, 0)
            for dst, src in loads[0:6]:
                sp.dma_start(dst, src).then_inc(loaded, 16)
            sp.wait_ge(cleared, len(cleared_tiles))
            for dst, src in loads[6::2]:
                sp.dma_start(dst, src).then_inc(loaded, 16)
            sp.wait_ge(prep_dve, marks["placed"])
            for dst, src in placements:
                sp.dma_start(dst, src).then_inc(prep_dma, 16)

            def iteration(f, attn, back):
                beside_l1(sp, f)
                if attn is not None:
                    load_x(sp, attn, attn, f)
                if back is not None:
                    beside_l3(sp, back, f + 1)
                    store(sp, back)

            iteration(0, 1, None)
            with sp.Fori(1, IMAGES - 1) as f:
                iteration(f, f + 1, f - 1)
            iteration(IMAGES - 1, None, IMAGES - 2)
            beside_l3(sp, IMAGES - 1, IMAGES)
            store(sp, IMAGES - 1)
            sp.wait_ge(stored, 16 * WQ * IMAGES)

        @block.gpsimd
        def _(pool):
            nc.gpsimd.memset(ident[:, :], 0.0).then_inc(masks_ready, 1)
            nc.gpsimd.memset(gram_mask[:, :], 0.0).then_inc(masks_ready, 1)
            pool.wait_ge(masks_ready, 2)
            nc.gpsimd.affine_select(out=ident[:, :], in_=ident[:, :], compare_op=ALU.not_equal, fill=1.0,
                                    base=0, pattern=[[-1, 128]], channel_multiplier=1).then_inc(masks_ready, 1)
            nc.gpsimd.affine_select(out=gram_mask[:, :], in_=gram_mask[:, :], compare_op=ALU.not_equal, fill=1.0,
                                    base=-C, pattern=[[-1, C]], channel_multiplier=1).then_inc(masks_ready, 1)

            def scale_k(image):
                pool.wait_ge(squared, 16 * image + 16)
                pool.wait_ge(u_ready, image + 1)
                k = tokens(K_AT)
                nc.gpsimd.tensor_tensor(k, k, columns(u[:, :, :], 2 * RUN, [[1, 2 * RUN], [0, C]]), ALU.mult).then_inc(k_scaled, 1)

            def split_y1(image):
                for k in range(CHUNKS):
                    pool.wait_ge(y1h_ready, CHUNKS * image + k + 1)
                    nc.gpsimd.tensor_tensor(y1_view(y1_l, k), y1_tokens(k), y1_view(y1_h, k).bitcast(F32),
                                            ALU.subtract).then_inc(y1l_ready, 1)

            scale_k(0)
            split_y1(0)
            with pool.Fori(1, IMAGES) as image:
                scale_k(image)
                split_y1(image)

        @block.tensor
        def _(pe):
            pe.wait_ge(loaded, 16 * len(loads))
            pe.wait_ge(masks_ready, 4)
            nc.tensor.transpose(banks[0][0:C2, 0:T_ROWS], tab96[:, :], ident[0:T_ROWS, 0:T_ROWS]).then_inc(prep_pe, 1)
            for c in range(2):
                nc.tensor.transpose(banks[1][:, c * 64:c * 64 + U_ROWS], tab192[:, c * M1:(c + 1) * M1],
                                    ident[0:U_ROWS, 0:U_ROWS]).then_inc(prep_pe, 1)
            pe.wait_ge(prep_dve, marks["bn_fold"])
            nc.tensor.matmul(banks[2][0:C + 1, 0:3 * C], bn_fold[:, :], wqkv[:, :], start=True, stop=True).then_inc(prep_pe, 1)
            nc.tensor.matmul(banks[3][0:C, 0:C + 1], wqkv[:, 2 * C:3 * C], bn_fold[:, :], start=True, stop=True).then_inc(prep_pe, 1)
            pe.wait_ge(prep_dve, marks["wv_t"])
            nc.tensor.matmul(banks[4][0:C, 0:C + 1], wln[:, :], wv_t[:, :], start=True, stop=True).then_inc(prep_pe, 1)
            pe.wait_ge(prep_dve, marks["p1"])
            nc.tensor.matmul(banks[5][0:C + 1, 0:C2], p1[:, :], w1a[:, :], start=True, stop=True).then_inc(prep_pe, 1)
            nc.tensor.matmul(banks[6][0:C + 1, 0:C2], p1b[:, :], w1a[:, :], start=True, stop=False)
            nc.tensor.matmul(banks[6][0:C + 1, 0:C2], ident[0:C + 1, 0:C + 1], w1b[:, :], start=False, stop=True).then_inc(prep_pe, 1)
            for n, (layer, t) in enumerate(((L1, T_DWB1), (L3, T_DWB3))):
                nc.tensor.matmul(banks[7][0:C2, n:n + 1], pw[layer][0:C, :, :].rearrange("p a c -> p (a c)"), col96[0:C, t:t + 1], start=True, stop=True).then_inc(prep_pe, 1)
            pe.wait_ge(prep_dve, marks["all"])
            pe.wait_ge(prep_dma, 16 * len(placements))

            def attention_scores(image):
                pe.wait_ge(xa_loaded, 32 * WQ * (image + 1))
                for n in range(4):
                    bank = ring_a.take(pe, image, A_XT + n)
                    for m in range(4):
                        i = 4 * n + m
                        last = nc.tensor.transpose(bank[0:C2, m * 128:(m + 1) * 128],
                                                   xa[:, i * C2:(i + 1) * C2], ident[:, :])
                    last.then_inc(xt_done, 1)
                for n in range(8):
                    bank = ring_a.take(pe, image, A_QK + n)
                    if n % 2 == 0:
                        pe.wait_ge(xcm_ready, 4 * image + n // 2 + 1)
                    for m in range(2):
                        i = 2 * n + m
                        last = nc.tensor.matmul(bank[:, m * 2 * C2:(m + 1) * 2 * C2], xcm[:, i * 128:(i + 1) * 128],
                                                qkw[:, :], start=True, stop=True)
                    last.then_inc(qk_done, 1)

            def attention_sums(image):
                bank = ring_a.take(pe, image, A_G)
                pe.wait_ge(x_loaded, 32 * WQ * (image + 1))
                pe.wait_ge(k_scaled, image + 1)
                for par in range(2):
                    for i in range(RUN):
                        first, final = par == 0 and i == 0, par == 1 and i == RUN - 1
                        last = nc.tensor.matmul(bank[0:SUMS, 0:C], token(par, i, X_AT, SUMS), token(par, i, K_AT, C),
                                                start=first, stop=final)
                last.then_inc(g_done, 1)

            def attention_weights(image):
                bank = ring_a.take(pe, image, A_M2)
                pe.wait_ge(gt_ready, 2 * image + 2)
                nc.tensor.matmul(bank[0:C, 0:C2], gt[:, :], wva_aug[:, :], start=True, stop=True)
                nc.tensor.matmul(bank[0:C, C2:C2 + 1], gm[:, :], ones[0:SUMS, 0:1], start=True, stop=True).then_inc(m2_done, 1)

            def conv1(image):
                pe.wait_ge(q_scaled, image + 1)
                for k in range(CHUNKS + 1):
                    if k < CHUNKS:
                        par, i0 = k // 4, 4 * (k % 4)
                        bank = ring_a.take(pe, image, A_XQ + k)
                        for m in range(4):
                            last = nc.tensor.transpose(bank[0:C2, m * 128:(m + 1) * 128],
                                                       token(par, i0 + m, Q_AT, C2), ident[:, :])
                        last.then_inc(xqt_done, 1)
                    if k > 0:
                        if k == 1:
                            pe.wait_ge(w1_ready, image + 1)
                        bank = ring_c.take(pe, image, C_1 + k - 1)
                        pe.wait_ge(xq_ready, CHUNKS * image + k)
                        nc.tensor.matmul(bank[0:C2, :], w1_cur[:, :], xq[:, (k - 1) % 2, :], start=True, stop=True)\
                            .then_inc(conv1_done, 1)

            def conv2(image):
                pe.wait_ge(y1h_ready, CHUNKS * image + CHUNKS)
                pe.wait_ge(y1l_ready, CHUNKS * image + CHUNKS)
                for k in range(CHUNKS + 1):
                    if k < CHUNKS:
                        bank = ring_c.take(pe, image, C_2 + k)
                        for t in range(TAPS):
                            rows, cols = slice(k * ROWS + t // 3, k * ROWS + t // 3 + ROWS), slice(t % 3, t % 3 + W)
                            for n, (wgt, src) in enumerate(((w2_h, y1_h), (w2_l, y1_h), (w2_h, y1_l))):
                                last = nc.tensor.matmul(bank[0:C2, :], wgt[:, t, :], src[:, rows, cols],
                                                        start=t + n == 0, stop=t == TAPS - 1 and n == 2)
                        last.then_inc(conv2_done, 1)
                    if k >= 2 and k % 2 == 0:
                        m = k // 2 - 1
                        bank = ring_b.take(pe, image, B_W3 + m)
                        pe.wait_ge(y2_ready, CHUNKS * image + 2 * m + 2)
                        rows = y2[m % 2].rearrange("p (j b w) -> p j b w", b=2, w=W)
                        for par in range(2):
                            last = nc.tensor.matmul(bank[0:C2, :], w3eo[:, par, :], rows[:, :, par, :],
                                                    start=par == 0, stop=par == 1)
                        last.then_inc(w3_done, 1)

            def pair_conv(image, layer, ring, first, copied, done):
                for m in range(PCHUNKS):
                    bank = ring.take(pe, image, first + m)
                    n = 0
                    for beside in range(2):
                        if beside == 1 and m == 0:
                            pe.wait_ge(copied, 64 * (image + 1))
                        hi, lo = ((a_h[layer], a_l[layer]), (b_h, b_l))[beside]
                        r0 = m * ROWS + 1 - beside
                        for kw in range(3):
                            for wgt, src in ((wt_h, hi), (wt_l, hi), (wt_h, lo)):
                                last = nc.tensor.matmul(bank[0:C2, :], wgt[layer][:, kw, beside, :],
                                                        src[:, r0:r0 + ROWS, kw:kw + W], start=n == 0, stop=n == 17)
                                n += 1
                    last.then_inc(done, 1)

            def routing(image):
                bank = ring_b.take(pe, image, B_RW)
                pe.wait_ge(mean_ready, image + 1)
                nc.tensor.matmul(bank[:, 0:EXPERTS], mean_b[:, :], wr[:, :], start=True, stop=True).then_inc(rw_done, 1)

            def expand(image):
                pe.wait_ge(weight_chain.sem, weight_chain.each * (image + 1))
                x2_rows = x2[:, :].rearrange("p (j w) -> p j w", w=W)
                bank = ring_b.take(pe, image, B_HALO)
                nc.tensor.matmul(bank[:, 0:W], ew[:, 0, E_OTHER:E_OTHER + M1], x2_rows[:, PAIRS // 2, :], start=True, stop=True)
                nc.tensor.matmul(bank[:, W:2 * W], ew[:, 1, E_BOTTOM:E_BOTTOM + M1], x2_rows[:, PAIRS // 2 - 1, :],
                                 start=True, stop=True).then_inc(expand_done, 1)
                for n in range(4):
                    par, g = n % 2, n // 2
                    bank = ring_b.take(pe, image, B_E + n)
                    nc.tensor.matmul(bank[:, :], ew[:, par, E_OTHER:E_OTHER + M1], x2_rows[:, g * ROWS:(g + 1) * ROWS, :],
                                     start=True, stop=False)
                    g += 2
                    nc.tensor.matmul(bank[:, :], ew[:, par, E_BOTTOM:E_BOTTOM + M1], x2_rows[:, g * ROWS:(g + 1) * ROWS, :],
                                     start=False, stop=True).then_inc(expand_done, 1)
                for n in range(8):
                    par, g = n % 2, n // 2
                    bank = ring_b.take(pe, image, B_E + 4 + n)
                    nc.tensor.matmul(bank[:, :], ew[:, par, 0:M1], x2_rows[:, g * ROWS:(g + 1) * ROWS, :],
                                     start=True, stop=True).then_inc(expand_done, 1)

            def project(image):
                for m in range(PCHUNKS):
                    bank = ring_d.take(pe, image, D_P + m)
                    if m == 0:
                        pe.wait_ge(pc_ready, 3 * image + 3)
                        pe.wait_ge(h2_ready, UNITS * image + UNITS)
                    first = dwa[:, :, :].rearrange("p (j b) w -> p j b w", b=2)[:, m * ROWS:(m + 1) * ROWS]
                    m2 = m % 2
                    other = dwb[:, :, :].rearrange("p (j b) w -> p j b w", b=2)[:, m2 * ROWS:(m2 + 1) * ROWS]
                    for par in range(2):
                        cols = slice(C - C * par, 3 * C - C * par)
                        nc.tensor.matmul(bank[0:C2, :], pc[:, 0, cols], first[:, :, par, :], start=par == 0, stop=False)
                        last = nc.tensor.matmul(bank[0:C2, :], pc[:, 1 + m // 2, cols], other[:, :, par, :],
                                                start=False, stop=par == 1)
                    last.then_inc(project_done, 1)

            def out_tokens(image):
                for n in range(4):
                    bank = ring_d.take(pe, image, D_OUT + n)
                    if n == 0:
                        pe.wait_ge(outc_ready, PCHUNKS * image + PCHUNKS)
                    for m in range(4):
                        i = 4 * n + m
                        last = nc.tensor.transpose(bank[:, m * C2:(m + 1) * C2], outc[:, i::RUN], ident[0:C2, 0:C2])
                    last.then_inc(outt_done, 1)

            def iteration(f, attn, back):
                conv2(f)
                if back is not None:
                    project(back)
                pair_conv(f, L1, ring_b, B_L1, b1_copied, l1_done)
                if attn is not None:
                    attention_scores(attn)
                routing(f)
                if back is not None:
                    pair_conv(back, L3, ring_d, D_L3, b3_copied, l3_done)
                if attn is not None:
                    attention_sums(attn)
                if back is not None:
                    out_tokens(back)
                if attn is not None:
                    attention_weights(attn)
                expand(f)
                if attn is not None:
                    conv1(attn)

            attention_scores(0)
            attention_sums(0)
            attention_weights(0)
            conv1(0)
            iteration(0, 1, None)
            with pe.Fori(1, IMAGES - 1) as f:
                iteration(f, f + 1, f - 1)
            iteration(IMAGES - 1, None, IMAGES - 2)
            project(IMAGES - 1)
            pair_conv(IMAGES - 1, L3, ring_d, D_L3, b3_copied, l3_done)
            out_tokens(IMAGES - 1)

        @block.scalar
        def _(act):
            act.wait_ge(cleared, len(cleared_tiles))
            for dst, src in loads[7::2]:
                act.dma_start(dst, src).then_inc(loaded, 16)
            act.wait_ge(prep_dve, marks["variances"])
            nc.scalar.activation(inv96[:, :], inv96[:, :], ACT.Sqrt).then_inc(prep_act, 1)
            nc.scalar.activation(invm[:, :, :], invm[:, :, :], ACT.Sqrt).then_inc(prep_act, 1)
            act.wait_ge(prep_dve, marks["all"])

            def scores_out(image):
                for n in range(4):
                    act.wait_ge(xt_done, 4 * image + n + 1)
                    nc.scalar.activation(xcm[0:C2, n * BANK:(n + 1) * BANK], ring_a.bank(A_XT + n)[0:C2, :], ACT.Copy)\
                        .then_inc(xcm_ready, 1)
                for n in range(8):
                    act.wait_ge(qk_done, 8 * image + n + 1)
                    src = ring_a.bank(A_QK + n)[:, 0:4 * C2].rearrange("p (m b s c) -> p m b s c", m=2, b=2, s=2)
                    for s, at in enumerate((Q_AT, K_AT)):
                        dst = columns(tok[:, :, :, :], 2 * n * TOK + at, [[TOK, 2], [RUN * TOK, 2], [1, C]])
                        nc.scalar.activation(dst, src[:, :, :, s, :], ACT.Square).then_inc(squared, 1)
                act.wait_ge(squared, 16 * image + 16)
                nc.scalar.activation(q4.rearrange("p (n c) -> p n c", c=C), tokens(Q_AT), ACT.Square).then_inc(q4_ready, 1)

            def root_of_q(image):
                act.wait_ge(norm_q, image + 1)
                nc.scalar.activation(s2[:, 0, :], s2[:, 0, :], ACT.Sqrt).then_inc(root_q, 1)

            def root_of_k(image):
                act.wait_ge(norm_k, image + 1)
                nc.scalar.activation(rk[:, :], rk[:, :], ACT.Sqrt, scale=float(TOKENS)).then_inc(root_k, 1)

            def conv1_slope(image):
                for k in range(CHUNKS + 1):
                    if k < CHUNKS:
                        act.wait_ge(xqt_done, CHUNKS * image + k + 1)
                        if k >= 2:
                            act.wait_ge(conv1_done, CHUNKS * image + k - 1)
                        nc.scalar.activation(xq[0:C2, k % 2, :], ring_a.bank(A_XQ + k)[0:C2, :], ACT.Copy).then_inc(xq_ready, 1)
                    if k > 0:
                        act.wait_ge(conv1_done, CHUNKS * image + k)
                        after(act, y1l_ready, CHUNKS * image + k - 2)
                        nc.scalar.activation(y1[:, (k - 1) % 2, :], ring_c.bank(C_1 + k - 1)[0:C2, :], ACT.Copy, scale=SLOPE)\
                            .then_inc(y1_slope, 1)

            def first_tap(image, n):
                _, dst, c, _ = unit(n)
                act.wait_ge(h1_ready, 14 * image + (6 if c else 14))
                at = Y_DW + c * TAPS
                nc.scalar.activation(dst, tap_input(n, 0), ACT.Identity, bias=dyn[:, Y_DWB + c:Y_DWB + c + 1],
                                     scale=dyn[:, at:at + 1]).then_inc(tap1_ready, 1)

            def finish_unit(image, n):
                _, dst, _, _ = unit(n)
                act.wait_ge(dw_ready, UNITS * image + n + 1)
                nc.scalar.activation(dst, dst, ACT.Relu).then_inc(h2_ready, 1)

            def conv2_slope(f, back):
                if back is not None:
                    for n in range(EARLY):
                        finish_unit(back, n)
                for k in range(CHUNKS + 1):
                    if k < CHUNKS:
                        act.wait_ge(conv2_done, CHUNKS * f + k + 1)
                        after(act, w3_done, PCHUNKS * f + k // 2 - 1)
                        nc.scalar.activation(y2[(k // 2) % 2][:, (k % 2) * BANK:(k % 2 + 1) * BANK],
                                             ring_c.bank(C_2 + k)[0:C2, :], ACT.Identity, bias=b2s[:, 0:1], scale=SLOPE)\
                            .then_inc(y2_slope, 1)
                    if back is not None:
                        for n in units_for(k + 1) if k < CHUNKS - 1 else ():
                            first_tap(back, n)
                        for n in units_for(k - 1) if k > 0 else ():
                            finish_unit(back, n)
                    if k >= 2 and k % 2 == 0:
                        m = k // 2 - 1
                        act.wait_ge(v_ready, PCHUNKS * f + m + 1)
                        high_part(a_h[L1], v, m).then_inc(ah1_ready, 1)

            def high_part(hi, src, m):
                return nc.scalar.activation(hi[:, m * ROWS + 1:(m + 1) * ROWS + 1, 1:W + 1],
                                            src[:, m % 2, :].rearrange("p (j w) -> p j w", w=W), ACT.Relu)

            def project_affine(b, l1_images):
                for m in range(PCHUNKS):
                    act.wait_ge(project_done, PCHUNKS * b + m + 1)
                    if m < 2:
                        act.wait_ge(al1_ready, PCHUNKS * l1_images + m - 1)
                    else:
                        act.wait_ge(al3_ready, PCHUNKS * b + m - 1)
                    nc.scalar.activation(v[:, m % 2, :], ring_d.bank(D_P + m)[0:C2, :], ACT.Identity,
                                         bias=dyn[0:C2, Y_B3:Y_B3 + 1], scale=inv96[:, L2:L2 + 1]).then_inc(v3_affine, 1)
                    act.wait_ge(v3_ready, PCHUNKS * b + m + 1)
                    high_part(a_h[L3], v, m).then_inc(ah3_ready, 1)

            def l1_out(f):
                for m in range(PCHUNKS):
                    act.wait_ge(l1_done, PCHUNKS * f + m + 1)
                    nc.scalar.activation(x2[:, m * BANK:(m + 1) * BANK], ring_b.bank(B_L1 + m)[0:C2, :], ACT.Identity,
                                         bias=conv_bias[:, 0:1], scale=inv96[:, L1:L1 + 1],
                                         accum_out=msum[:, m:m + 1]).then_inc(x2_ready, 1)

            def route(f):
                act.wait_ge(rwz_ready, f + 1)
                nc.scalar.activation(rw[:, :], rwz[:, :], ACT.Sigmoid).then_inc(rw_ready, 1)

            def l3_out(b):
                for m in range(PCHUNKS):
                    act.wait_ge(l3_done, PCHUNKS * b + m + 1)
                    nc.scalar.activation(outc[:, m * BANK:(m + 1) * BANK], ring_d.bank(D_L3 + m)[0:C2, :], ACT.Identity,
                                         bias=conv_bias[:, 1:2], scale=inv96[:, L3:L3 + 1]).then_inc(outc_ready, 1)

            def tokens_out(b):
                for n in range(4):
                    act.wait_ge(outt_done, 4 * b + n + 1)
                    src = ring_d.bank(D_OUT + n)[:, 0:4 * C2].rearrange("p (i b c) -> p b i c", b=2, c=C)
                    dst = columns(ot, 4 * n * C, [[RUN * C, 2], [C, 4], [1, C]])
                    nc.scalar.activation(dst, src, ACT.Copy).then_inc(ot_ready, 1)

            def expand_out(f):
                act.wait_ge(weight_chain.sem, weight_chain.each * (f + 1))
                bank = ring_b.bank(B_HALO)
                act.wait_ge(expand_done, 13 * f + 1)
                for n, (half, r) in enumerate(((slice(0, M2), PAIRS + 1), (slice(M2, M1), 0))):
                    nc.scalar.activation(h1b[half, r, 1:W + 1], bank[half, n * W:(n + 1) * W], ACT.Relu,
                                         bias=dyn[half, Y_B1 + 1:Y_B1 + 2], scale=invm[half, 1, 0:1]).then_inc(h1_ready, 1)
                for n in range(12):
                    c, dst_tile = (1, h1b) if n < 4 else (0, h1a)
                    par, g = n % 2, (n if n < 4 else n - 4) // 2
                    r0 = 1 + 2 * ROWS * g + par
                    act.wait_ge(expand_done, 13 * f + n + 2)
                    nc.scalar.activation(dst_tile[:, r0:r0 + 2 * ROWS - 1:2, 1:W + 1],
                                         ring_b.bank(B_E + n)[:, :].rearrange("p (j w) -> p j w", w=W), ACT.Relu,
                                         bias=dyn[:, Y_B1 + c:Y_B1 + c + 1], scale=invm[:, c, 0:1]).then_inc(h1_ready, 1)
                    if n == 3:
                        after(act, stored, 16 * WQ * f)
                        for n_tap in range(EARLY):
                            first_tap(f, n_tap)

            def iteration(f, attn, back):
                conv2_slope(f, back)
                if back is not None:
                    project_affine(back, f + 1)
                l1_out(f)
                if attn is not None:
                    scores_out(attn)
                route(f)
                if attn is not None:
                    root_of_q(attn)
                if back is not None:
                    l3_out(back)
                    tokens_out(back)
                if attn is not None:
                    root_of_k(attn)
                expand_out(f)
                for n in units_for(0):
                    first_tap(f, n)
                if attn is not None:
                    conv1_slope(attn)

            scores_out(0)
            root_of_q(0)
            root_of_k(0)
            conv1_slope(0)
            iteration(0, 1, None)
            with act.Fori(1, IMAGES - 1) as f:
                iteration(f, f + 1, f - 1)
            iteration(IMAGES - 1, None, IMAGES - 2)
            for n in range(EARLY):
                finish_unit(IMAGES - 1, n)
            for k in range(CHUNKS):
                for n in units_for(k + 1) if k < CHUNKS - 1 else ():
                    first_tap(IMAGES - 1, n)
                for n in units_for(k):
                    finish_unit(IMAGES - 1, n)
            project_affine(IMAGES - 1, IMAGES)
            l3_out(IMAGES - 1)
            tokens_out(IMAGES - 1)


def kernel(**inputs):
    import numpy as _np
    import concourse.bacc as _bacc
    from concourse import mybir as _mybir
    from concourse.bass_utils import run_bass_kernel_spmd as _run

    nc = _bacc.Bacc("TRN2", target_bir_lowering=False, num_devices=1)
    arrays, args = {}, {}
    for name, value in inputs.items():
        value = _np.ascontiguousarray(value)
        arrays[f"in_{name}_dram"] = value
        args[name] = nc.dram_tensor(f"in_{name}_dram", value.shape, _mybir.dt.from_np(value.dtype), kind="ExternalInput").ap()
    out = nc.dram_tensor("out_dram", (IMAGES, H, W, C), _mybir.dt.float32, kind="ExternalOutput").ap()
    conv_chain_kernel(nc, args, out)
    return _run(nc, [arrays], core_ids=[0]).results[0]["out_dram"]
```

```python
from contextlib import ExitStack

import concourse.bass as bass
from concourse import mybir

F32 = mybir.dt.float32
F32R = mybir.dt.float32r
ALU = mybir.AluOpType
ACT = mybir.ActivationFunctionType
AX = mybir.AxisListType

IMAGES, H, W, C = 8, 64, 64, 48
C2 = 2 * C
TOKENS = H * W
PAIRS = H // 2
HALF = TOKENS // 2
WQ = 4
RUN = W // WQ
EXPERTS = 4
M = 192
M1 = 128
M2 = M - M1
TAPS = 9
WP = W + 2
BANK = 512
CHUNKS = TOKENS // BANK
PCHUNKS = HALF // BANK
ROWS = BANK // W
Q_AT, X_AT, K_AT, TOK = 0, C, 2 * C, 3 * C + 1
SUMS = 2 * C + 1
BN_EPS = 1e-3
SLOPE = 0.2

T_VAR, T_GAMMA, T_MEAN, T_BETA = 0, 4, 8, 12
L0, L1, L3, L2 = 0, 1, 2, 3
T_BLN, T_B3, T_B2, T_DWB1, T_PWB1, T_DWB3, T_PWB3 = 16, 17, 18, 19, 20, 21, 22
T_S1, T_S3, T_BPWL = 23, 35, 47
T_ROWS = 51
U_VAR, U_GAMMA, U_MEAN, U_BETA, U_BPW, U_BDW, U_WDW = 0, 2, 4, 6, 8, 12, 16
U_ROWS = U_WDW + EXPERTS * TAPS
Y_DW, Y_DWB, Y_B1, Y_B3 = 0, 2 * TAPS, 2 * TAPS + 2, 2 * TAPS + 4
Y_ALL = Y_B3 + 1
E_BOTTOM, E_OTHER, E_ALL = M1, M1 + M2, M1 + 3 * M2


class Ring:

    def __init__(self, banks, readers):
        assert len(readers) % 2 == 0
        self.banks, self.readers = banks, readers

    def bank(self, k):
        return self.banks[k % 2]

    def take(self, pe, image, k):
        sem, each, nth = self.readers[k - 2]
        if k >= 2:
            pe.wait_ge(sem, image * each + nth)
        elif not isinstance(image, int) or image > 0:
            pe.wait_ge(sem, image * each)
        return self.banks[k % 2]


class Chain:

    def __init__(self, sem, each):
        self.sem, self.each = sem, each

    def begin(self, engine, image):
        self.engine, self.image, self.k = engine, image, 0

    def __call__(self, instruction):
        instruction.then_inc(self.sem, 1)
        self.k += 1
        self.engine.wait_ge(self.sem, self.image * self.each + self.k)

    def end(self):
        assert self.k == self.each, self.k


def columns(ap, offset, dims):
    return bass.AP(ap.tensor, ap.offset + offset, [list(ap.ap[0])] + [list(d) for d in dims])


def twice(row_ap):
    (rs, rn), (es, en) = row_ap.ap
    return bass.AP(row_ap.tensor, row_ap.offset, [[rs, rn], [0, 2], [es, en]])


def conv_chain_kernel(nc, a, out):
    ctx = ExitStack()
    with ctx:
        def sb(name, shape, dt=F32):
            return ctx.enter_context(nc.sbuf_tensor(name, shape, dt))

        def sem(name):
            return ctx.enter_context(nc.semaphore(name))

        def row(name):
            return a[name].rearrange("(o n) -> o n", o=1)

        tab96 = sb("tab96", [T_ROWS, C2])
        tab192 = sb("tab192", [U_ROWS, 2 * M1])
        col96 = sb("col96", [C2, T_ROWS])
        colm = sb("colm", [128, 2, U_ROWS])
        ident = sb("ident", [128, 128])
        ones = sb("ones", [128, 128])
        gram_mask = sb("gram_mask", [SUMS, C])
        mask_par = sb("mask_par", [C2, 2])
        mask_half = sb("mask_half", [128, 2])
        inv96, shift96 = sb("inv96", [C2, 4]), sb("shift96", [C2, 4])
        invm, shiftm = sb("invm", [128, 2, 2]), sb("shiftm", [128, 2, 2])
        inv0 = sb("inv0", [C + 1, 1])
        bn_fold = sb("bn_fold", [C + 1, C + 1])
        wqkv = sb("wqkv", [C + 1, 3 * C])
        wln, w1a, w1b = sb("wln", [C, C]), sb("w1a", [C, C2]), sb("w1b", [C + 1, C2])
        wqk = sb("wqk", [C + 1, C2])
        qk_mean = sb("qk_mean", [C + 1, 2])
        wv_t, p1, p1b = sb("wv_t", [C, C + 1]), sb("p1", [C, C + 1]), sb("p1b", [C, C + 1])
        wva, m1w = sb("wva", [C + 1, C2]), sb("m1w", [C + 1, C2])
        qkw = sb("qkw", [C2 + 1, 2 * C2])
        wva_aug = sb("wva_aug", [SUMS, C2])
        w1_cur = sb("w1_cur", [C2 + 1, C2])
        w2_h, w2_l = sb("w2_h", [C2, TAPS, C2], F32R), sb("w2_l", [C2, TAPS, C2], F32R)
        w3eo = sb("w3eo", [C2, 2, C2])
        b2s = sb("b2s", [C2, 1])
        pw = {L1: sb("pw1", [C2, 2, C]), L3: sb("pw3", [C2, 2, C])}
        wt_h = {n: sb(f"wt_h{n}", [C2, 3, 2, C2], F32R) for n in (L1, L3)}
        wt_l = {n: sb(f"wt_l{n}", [C2, 3, 2, C2], F32R) for n in (L1, L3)}
        conv_bias = sb("conv_bias", [C2, 2])
        wpw = sb("wpw", [C2, EXPERTS, E_ALL])
        wr, br = sb("wr", [C2, EXPERTS]), sb("br", [128, EXPERTS])
        wpl = sb("wpl", [128, EXPERTS, 2, C])
        lin, lin_const = sb("lin", [128, Y_ALL, EXPERTS]), sb("lin_const", [128, Y_ALL])
        s1, s2, u, r = (sb(n, [128, k, 2 * RUN]) for n, k in (("s1", 2), ("s2", 1), ("u", 2), ("r", 1)))
        gt, gm = sb("gt", [SUMS, C]), sb("gm", [SUMS, C])
        rk = sb("rk", [C, 1])
        msum, mean, mean_b = sb("msum", [C2, PCHUNKS]), sb("mean", [C2, 1]), sb("mean_b", [C2, 128])
        rwz, rw = sb("rwz", [128, EXPERTS]), sb("rw", [128, EXPERTS])
        prod, dyn = sb("prod", [128, Y_ALL, EXPERTS]), sb("dyn", [128, Y_ALL])
        wk, ew = sb("wk", [C2, E_ALL]), sb("ew", [C2, 2, E_ALL])
        pk = sb("pk", [128, 2, C])
        pc = sb("pc", [128, 3, 3 * C])
        tok = sb("tok", [128, 2, RUN, TOK])
        xcm = sb("xcm", [C2 + 1, RUN * 128])
        xq = sb("xq", [C2 + 1, 2, BANK])
        y1 = sb("y1", [C2, 2, BANK])
        y1_h, y1_l = sb("y1_h", [C2, H + 2, WP], F32R), sb("y1_l", [C2, H + 2, WP], F32R)
        y2 = [t[0:C2, :, :].rearrange("p a n -> p (a n)") for t in (xq, y1)]
        v = sb("v", [C2, 2, BANK])
        a_h = {n: sb(f"a_h{n}", [C2, PAIRS + 2, WP], F32R) for n in (L1, L3)}
        a_l = {n: sb(f"a_l{n}", [C2, PAIRS + 2, WP], F32R) for n in (L1, L3)}
        b_h, b_l = y1_h[:, 1:PAIRS + 1, :], y1_l[:, 1:PAIRS + 1, :]
        x2 = sb("x2", [C2, HALF])
        h1a = sb("h1a", [128, H + 2, WP])
        h1b = sb("h1b", [128, PAIRS + 2, WP])
        dwa = sb("dwa", [128, H, W])
        dwb = sb("dwb", [128, PAIRS, W])
        dwa_flat, dwb_flat = dwa[:, :, :].rearrange("p h w -> p (h w)"), dwb[:, :, :].rearrange("p h w -> p (h w)")
        outc = dwa_flat[0:C2, 0:HALF]
        q4 = dwa_flat[:, HALF:HALF + 2 * RUN * C]
        xa = q4
        ot = dwb_flat[:, 0:2 * RUN * C]
        h1a_flat = h1a[:, :, :].rearrange("p h w -> p (h w)")
        w2_f = h1a_flat[0:C2, 0:TAPS * C2]
        wt_f = h1a_flat[0:C2, TAPS * C2:(TAPS + 6) * C2]

        banks = [ctx.enter_context(nc.psum_tensor(f"bank{n}", [128, BANK], F32)) for n in range(8)]
        loaded, cleared, masks_ready = sem("loaded"), sem("cleared"), sem("masks_ready")
        prep_pe, prep_dve, prep_act, prep_dma = (sem(n) for n in ("prep_pe", "prep_dve", "prep_act", "prep_dma"))
        xa_loaded, x_loaded = sem("xa_loaded"), sem("x_loaded")
        xt_done, qk_done, g_done, m2_done, xqt_done = (sem(n) for n in ("xt_done", "qk_done", "g_done", "m2_done", "xqt_done"))
        conv1_done, conv2_done, w3_done, l1_done = (sem(n) for n in ("conv1_done", "conv2_done", "w3_done", "l1_done"))
        rw_done, expand_done, project_done, l3_done, outt_done = (sem(n) for n in ("rw_done", "expand_done", "project_done", "l3_done", "outt_done"))
        xcm_ready, squared, q4_ready, root_q, root_k = (sem(n) for n in ("xcm_ready", "squared", "q4_ready", "root_q", "root_k"))
        norm_q, norm_k = sem("norm_q"), sem("norm_k")
        u_ready, q_scaled, k_scaled = sem("u_ready"), sem("q_scaled"), sem("k_scaled")
        gt_ready, w1_ready = sem("gt_ready"), sem("w1_ready")
        xq_ready, y1_slope, y1_max, y1h_ready, y1l_ready = (sem(n) for n in ("xq_ready", "y1_slope", "y1_max", "y1h_ready", "y1l_ready"))
        y2_slope, y2_ready, v_ready, ah1_ready, al1_ready = (sem(n) for n in ("y2_slope", "y2_ready", "v_ready", "ah1_ready", "al1_ready"))
        b_copied = {n: (sem(f"b{n}_first_copied"), sem(f"b{n}_rest_copied")) for n in (L1, L3)}
        x2_ready, mean_ready, rwz_ready, rw_ready = (sem(n) for n in ("x2_ready", "mean_ready", "rwz_ready", "rw_ready"))
        h1_ready, tap1_ready, h2_ready = (sem(n) for n in ("h1_ready", "tap1_ready", "h2_ready"))
        v3_affine, v3_ready, ah3_ready, al3_ready = (sem(n) for n in ("v3_affine", "v3_ready", "ah3_ready", "al3_ready"))
        sync_waits = sem("sync_waits")
        outc_ready, ot_ready, stored = sem("outc_ready"), sem("ot_ready"), sem("stored")
        attn_chain, attn2_chain = Chain(sem("attn_chain"), 5), Chain(sem("attn2_chain"), 2)
        weight_chain = Chain(sem("weight_chain"), 8)
        rk_ready, mean_sum, pc_ready = sem("rk_ready"), sem("mean_sum"), sem("pc_ready")
        project_weight_chain = Chain(sem("project_weight_chain"), 4)
        tap_step = sem("tap_step")

        A_XT, A_QK, A_G, A_M2, A_XQ = 0, 4, 12, 13, 14
        ring_a = Ring(banks[0:2], [(xcm_ready, 4, n + 1) for n in range(4)]
                      + [(squared, 16, 2 * n + 2) for n in range(8)]
                      + [(gt_ready, 2, 2), (w1_ready, 1, 1)]
                      + [(xq_ready, CHUNKS, n + 1) for n in range(CHUNKS)])
        B_W3, B_L1, B_RW, B_HALO, B_E = 0, 4, 8, 9, 10
        ring_b = Ring(banks[2:4], [(v_ready, PCHUNKS, n + 1) for n in range(PCHUNKS)]
                      + [(x2_ready, PCHUNKS, n + 1) for n in range(PCHUNKS)]
                      + [(rwz_ready, 1, 1), (h1_ready, 14, 2)]
                      + [(h1_ready, 14, n + 3) for n in range(12)])
        C_1, C_2 = 0, 8
        ring_c = Ring(banks[4:6], [(y1_max, CHUNKS, n + 1) for n in range(CHUNKS)]
                      + [(y2_ready, CHUNKS, n + 1) for n in range(CHUNKS)])
        D_P, D_L3, D_OUT = 0, 4, 8
        ring_d = Ring(banks[6:8], [(v3_affine, PCHUNKS, n + 1) for n in range(PCHUNKS)]
                      + [(outc_ready, PCHUNKS, n + 1) for n in range(PCHUNKS)]
                      + [(ot_ready, 4, n + 1) for n in range(4)])

        UNIT_ROWS = 2 * ROWS
        OTHER_UNITS = PAIRS // UNIT_ROWS
        UNITS = OTHER_UNITS + H // UNIT_ROWS
        TAP_STEPS = UNITS * (TAPS - 1)
        BY_CONV1, BY_CONV2, BY_PROJECT = 0, CHUNKS, 2 * CHUNKS
        steps_at = (0, 0, 1, 1, 1, 1, 1, 0) + (8, 5, 4, 4, 4, 4, 4, 4) + (2, 1, 1, 2)
        assert sum(steps_at) == TAP_STEPS

        def unit(n):
            if n < OTHER_UNITS:
                r0 = n * UNIT_ROWS
                return h1b, dwb[:, r0:r0 + UNIT_ROWS, :], 1, r0
            r0 = (n - OTHER_UNITS) * UNIT_ROWS
            return h1a, dwa[:, r0:r0 + UNIT_ROWS, :], 0, r0

        def tap_input(n, t):
            src, _, _, r0 = unit(n)
            return src[:, r0 + t // 3:r0 + t // 3 + UNIT_ROWS, t % 3:t % 3 + W]

        def tap_of_step(s):
            pair, rest = divmod(s, 2 * (TAPS - 1))
            return 2 * pair + rest % 2, 1 + rest // 2

        def last_step(n):
            return 2 * (TAPS - 1) * (n // 2) + 2 * (TAPS - 2) + n % 2 + 1

        loads = []

        def load(dst, src):
            loads.append((dst, src))

        def flat2(name):
            return a[name]

        bn_names = {L0: ("L0_conv_bn_var", "L0_conv_bn_gamma", "L0_conv_bn_mean", "L0_conv_bn_beta"),
                    L1: ("L1_conv_moving_var", "L1_conv_gamma", "L1_conv_moving_mean", "L1_conv_beta"),
                    L3: ("L3_conv_moving_var", "L3_conv_gamma", "L3_conv_moving_mean", "L3_conv_beta"),
                    L2: ("L2_conv_v3", "L2_conv_g3", "L2_conv_m3", "L2_conv_b3")}

        def both(r0, rows, src):
            load(tab96[r0:r0 + rows, :].rearrange("r (a c) -> r a c", a=2), twice(src))

        load(wqkv[0:C, :], a["L0_conv_w_qkv"])
        load(wqkv[C:C + 1, :], row("L0_conv_b_qkv"))
        load(wln[:, :], a["L0_conv_w_ln"])
        w1_rows = a["L0_conv_w1"].rearrange("a b i o -> (a b i) o")
        load(w1a[:, :], w1_rows[0:C, :])
        load(w1b[0:C, :], w1_rows[C:C2, :])
        load(w1b[C:C + 1, :], row("L0_conv_b1"))
        for n, names in bn_names.items():
            for r0, name in zip((T_VAR, T_GAMMA, T_MEAN, T_BETA), names):
                both(r0 + n, 1, row(name))
        for r0, name in ((T_BLN, "L0_conv_b_ln"), (T_B3, "L0_conv_b3"), (T_DWB1, "L1_conv_dw_bias"),
                         (T_PWB1, "L1_conv_pw_bias"), (T_DWB3, "L3_conv_dw_bias"), (T_PWB3, "L3_conv_pw_bias")):
            both(r0, 1, row(name))
        load(tab96[T_B2:T_B2 + 1, :], row("L0_conv_b2"))
        both(T_BPWL, EXPERTS, a["L2_conv_bpwl"])
        for r0, name in ((T_S1, "L1_conv_dw_kernel"), (T_S3, "L3_conv_dw_kernel")):
            dw = a[name].rearrange("h w o c -> h (w o) c")
            for g, (even, odd) in enumerate(((1, 2), (0, 1), (None, 0), (2, None))):
                for par, kh in enumerate((even, odd)):
                    if kh is not None:
                        load(tab96[r0 + 3 * g:r0 + 3 * g + 3, par * C:(par + 1) * C], dw[kh])
        for r0, name in ((U_VAR, "L2_conv_v1"), (U_VAR + 1, "L2_conv_v2"), (U_GAMMA, "L2_conv_g1"),
                         (U_GAMMA + 1, "L2_conv_g2"), (U_MEAN, "L2_conv_m1"), (U_MEAN + 1, "L2_conv_m2"),
                         (U_BETA, "L2_conv_b1"), (U_BETA + 1, "L2_conv_b2")):
            load(tab192[r0:r0 + 1, 0:M], row(name))
            load(tab192[r0:r0 + 1, M:M + M2], row(name)[:, M1:M])
        for r0, rows, src in ((U_BPW, EXPERTS, a["L2_conv_bpw"]), (U_BDW, EXPERTS, a["L2_conv_bdw"]),
                              (U_WDW, EXPERTS * TAPS, a["L2_conv_Wdw"].rearrange("e h w m -> (e h w) m"))):
            load(tab192[r0:r0 + rows, 0:M], src)
            load(tab192[r0:r0 + rows, M:M + M2], src[:, M1:M])
        load(w2_f.rearrange("p (t o) -> p t o", t=TAPS), a["L0_conv_w2"].rearrange("h w i o -> i (h w) o"))
        w3_rows = a["L0_conv_w3"].rearrange("a b i o -> (a b i) o")
        for par in range(2):
            load(w3eo[:, par, par * C:(par + 1) * C], w3_rows)
            half = slice(par * C, (par + 1) * C)
            for n, name in ((L1, "L1_conv_pw_kernel"), (L3, "L3_conv_pw_kernel")):
                load(pw[n][half, :, :], twice(a[name].rearrange("a b i o -> (a b i) o")))
            wpw_src = a["L2_conv_Wpw"].rearrange("e c m -> c e m")
            load(wpw[half, :, 0:M1], wpw_src[:, :, 0:M1])
            load(wpw[half, :, E_OTHER:E_OTHER + M2], wpw_src[:, :, M1:M])
            load(wr[half, :], a["L2_conv_Wr"])
            wpl_src = a["L2_conv_Wpwl"].rearrange("e m f -> m e f")
            load(wpl[par * M2:(par + 1) * M2, :, 1, :], wpl_src[M1:M])
        load(wpl[:, :, 0, :], wpl_src[0:M1])
        br_row = row("L2_conv_br")
        load(br[:, :], bass.AP(br_row.tensor, br_row.offset, [[0, 128], [1, EXPERTS]]))

        cleared_tiles = [tab96, qkw, wva_aug, w3eo, wpw]
        placements = [
            (qkw[0:C, 0:C2], wqk[0:C, :]), (qkw[C:C2, C2:2 * C2], wqk[0:C, :]),
            (qkw[C2:C2 + 1, 0:C2], wqk[C:C + 1, :]), (qkw[C2:C2 + 1, C2:2 * C2], wqk[C:C + 1, :]),
            (wva_aug[0:C, :], wva[0:C, :]), (wva_aug[C2:C2 + 1, :], wva[C:C + 1, :]),
            (w1_cur[C:C2 + 1, :], m1w[:, :]),
        ]

        def y1_tokens(k):
            return columns(y1[:, :, :], (k % 2) * BANK, [[WQ, PAIRS], [1, WQ], [128, 4]])

        def y1_view(tile, k):
            par, i0 = k // 4, 4 * (k % 4)
            return columns(tile[:, :, :], (1 + par) * WP + 1 + i0, [[2 * WP, PAIRS], [RUN, WQ], [1, 4]])

        def tokens(at, outer=()):
            return columns(tok[:, :, :, :], at, [*outer, [TOK, 2 * RUN], [1, C]])

        def token(par, i, at, n):
            return tok[:, par, i, at:at + n]

        def after(engine, semaphore, value):
            if not isinstance(value, int) or value > 0:
                engine.wait_ge(semaphore, value)

        marks = {}
        H1_WRITES = 14

        BEFORE = -1
        expand_beside = {BEFORE: (0, 1), 0: (2,), 1: (3, 4), 7: (), 8: (10, 11), **{k: (k + 3,) for k in range(2, 7)}}

        block = ctx.enter_context(nc.Block())

        @block.vector
        def _(dve):
            for n, tile in enumerate(cleared_tiles):
                nc.vector.memset(tile[:], 0.0).then_inc(cleared, 1)
            steps = [0]

            def step(instruction, name=None):
                instruction.then_inc(prep_dve, 1)
                steps[0] += 1
                dve.wait_ge(prep_dve, steps[0])
                if name is not None:
                    marks[name] = steps[0]

            for tile in (pc, lin, lin_const):
                step(nc.vector.memset(tile[:], 0.0))
            for tile in (inv0, ones):
                step(nc.vector.memset(tile[:], 1.0))
            step(nc.vector.memset(tok[:, :, :, TOK - 1], 1.0))
            step(nc.vector.memset(xcm[C2:C2 + 1, :], 1.0))
            step(nc.vector.memset(xq[C2:C2 + 1, :, :], 1.0))
            step(nc.vector.memset(mask_par[:, 0:1], 0.0))
            step(nc.vector.memset(mask_par[0:C, 0:1], 1.0))
            step(nc.vector.tensor_scalar(mask_par[:, 1:2], mask_par[:, 0:1], -1.0, 1.0, ALU.mult, ALU.add))
            step(nc.vector.memset(mask_half[:, :], 0.0))
            for half in range(2):
                step(nc.vector.memset(mask_half[half * M2:(half + 1) * M2, half:half + 1], 1.0))
            for tile in (y1_h, y1_l, a_h[L1], a_l[L1], a_h[L3], a_l[L3], h1b):
                rows = tile.shape[1]
                edge = tile[:, :, :] if tile is h1b else tile[:, :, :].bitcast(F32)
                step(nc.vector.memset(edge[:, 0:rows:rows - 1, :], 0.0))
                step(nc.vector.memset(edge[:, :, 0:WP:WP - 1], 0.0))
            dve.wait_ge(prep_pe, 1)
            step(nc.vector.tensor_copy(col96[:, :], banks[0][0:C2, 0:T_ROWS]))
            dve.wait_ge(prep_pe, 3)
            step(nc.vector.tensor_copy(colm[:, :, :], banks[1][:, 0:2 * 64].rearrange("p (c u) -> p c u", c=2)[:, :, 0:U_ROWS]))
            step(nc.vector.tensor_scalar_add(inv96[:, :], col96[:, T_VAR:T_VAR + 4], BN_EPS))
            step(nc.vector.tensor_scalar_add(invm[:, :, :], colm[:, :, U_VAR:U_VAR + 2], BN_EPS), "variances")
            dve.wait_ge(prep_act, 2)
            step(nc.vector.reciprocal(inv96[:, :], inv96[:, :]))
            step(nc.vector.reciprocal(invm[:, :, :], invm[:, :, :]))
            for inv, shift, tab, g, m, b, n in ((inv96[:, :], shift96[:, :], col96[:, :], T_GAMMA, T_MEAN, T_BETA, 4),
                                                (invm[:, :, :], shiftm[:, :, :], colm[:, :, :], U_GAMMA, U_MEAN, U_BETA, 2)):
                step(nc.vector.tensor_tensor(inv, inv, tab[..., g:g + n], ALU.mult))
                step(nc.vector.tensor_tensor(shift, inv, tab[..., m:m + n], ALU.mult))
                step(nc.vector.tensor_tensor(shift, tab[..., b:b + n], shift, ALU.subtract))
            step(nc.vector.tensor_copy(inv0[0:C, :], inv96[0:C, L0:L0 + 1]))
            step(nc.vector.tensor_scalar(bn_fold[:, :], ident[0:C + 1, 0:C + 1], inv0[:, 0:1], None, ALU.mult))
            step(nc.vector.tensor_copy(bn_fold[0:C, C:C + 1], shift96[0:C, L0:L0 + 1]), "bn_fold")
            dve.wait_ge(prep_pe, 5)
            step(nc.vector.tensor_copy(wv_t[:, :], banks[3][0:C, 0:C + 1]), "wv_t")
            qk = banks[2][0:C + 1, 0:C2].rearrange("p (s c) -> p s c", s=2)
            step(nc.vector.tensor_reduce(qk_mean[:, :], qk, axis=AX.X, op=ALU.add))
            step(nc.vector.tensor_scalar(qk_mean[:, :], qk_mean[:, :], -1.0 / C, None, ALU.mult))
            step(nc.vector.tensor_tensor(wqk[:, :].rearrange("p (s c) -> p s c", s=2), qk,
                                         columns(qk_mean[:, :], 0, [[1, 2], [0, C]]), ALU.add))
            dve.wait_ge(prep_pe, 6)
            step(nc.vector.tensor_copy(p1[:, :], banks[4][0:C, 0:C + 1]))
            step(nc.vector.tensor_copy(p1b[:, :], p1[:, :]))
            step(nc.vector.tensor_tensor(p1b[:, C:C + 1], p1[:, C:C + 1], col96[0:C, T_BLN:T_BLN + 1], ALU.add), "p1")
            dve.wait_ge(prep_pe, 8)
            step(nc.vector.tensor_copy(wva[:, :], banks[5][0:C + 1, 0:C2]))
            step(nc.vector.tensor_copy(m1w[:, :], banks[6][0:C + 1, 0:C2]), "placed")
            step(nc.vector.tensor_scalar(b2s[:, :], col96[:, T_B2:T_B2 + 1], SLOPE, None, ALU.mult), "attention")
            w2_src = w2_f.rearrange("p (t o) -> p t o", t=TAPS)
            step(nc.vector.tensor_copy(w2_h[:, :, :], w2_src))
            step(nc.vector.tensor_tensor(w2_l[:, :, :], w2_src, w2_h[:, :, :].bitcast(F32), ALU.subtract))
            dve.wait_ge(prep_pe, 10)
            for n, (layer, s0, pwb) in enumerate(((L1, T_S1, T_PWB1), (L3, T_S3, T_PWB3))):
                step(nc.vector.scalar_tensor_tensor(out=conv_bias[:, n:n + 1], in0=banks[7][0:C2, n:n + 1],
                                                    scalar=col96[:, pwb:pwb + 1], in1=inv96[:, layer:layer + 1],
                                                    op0=ALU.add, op1=ALU.mult))
                step(nc.vector.tensor_tensor(conv_bias[:, n:n + 1], conv_bias[:, n:n + 1], shift96[:, layer:layer + 1], ALU.add))
                step(nc.vector.tensor_tensor(wt_f.rearrange("p (k g o) -> p k g o", k=3, g=4),
                                             columns(col96[:, :], s0, [[1, 3], [3, 4], [0, C]]),
                                             columns(pw[layer][:, :, :], 0, [[0, 3], [0, 4], [1, C]]), ALU.mult))
                flat = [t[layer][:, :, :, :].rearrange("p k b o -> p (k b o)") for t in (wt_h, wt_l)]
                step(nc.vector.tensor_copy(flat[0], wt_f))
                step(nc.vector.tensor_tensor(flat[1], wt_f, flat[0].bitcast(F32), ALU.subtract))
            for c in range(2):
                w_in = colm[:, c, U_WDW:U_ROWS].rearrange("p (e t) -> p t e", e=EXPERTS)
                step(nc.vector.tensor_scalar(lin[:, Y_DW + c * TAPS:Y_DW + (c + 1) * TAPS, :], w_in,
                                             invm[:, c, 1:2], None, ALU.mult))
                step(nc.vector.tensor_scalar(lin[:, Y_DWB + c, :], colm[:, c, U_BDW:U_BDW + EXPERTS], invm[:, c, 1:2], None, ALU.mult))
                step(nc.vector.tensor_scalar(lin[:, Y_B1 + c, :], colm[:, c, U_BPW:U_BPW + EXPERTS], invm[:, c, 0:1], None, ALU.mult))
                step(nc.vector.tensor_copy(lin_const[:, Y_DWB + c:Y_DWB + c + 1], shiftm[:, c, 1:2]))
                step(nc.vector.tensor_copy(lin_const[:, Y_B1 + c:Y_B1 + c + 1], shiftm[:, c, 0:1]))
            step(nc.vector.tensor_scalar(lin[0:C2, Y_B3, :], col96[:, T_BPWL:T_BPWL + EXPERTS], inv96[:, L2:L2 + 1], None, ALU.mult))
            step(nc.vector.tensor_copy(lin_const[0:C2, Y_B3:Y_B3 + 1], shift96[:, L2:L2 + 1]))
            step(nc.vector.memset(h1a[:, 0:H + 2:H + 1, :], 0.0))
            step(nc.vector.memset(h1a[:, :, 0:WP:WP - 1], 0.0), "all")

            def norms_begin(image):
                attn_chain.begin(dve, image)
                dve.wait_ge(squared, 16 * image + 16)
                attn_chain(nc.vector.tensor_reduce(s1[:, :, :], tokens(Q_AT, [[K_AT - Q_AT, 2]]), axis=AX.X, op=ALU.add))
                attn_chain(nc.vector.tensor_scalar_add(s1[:, :, :], s1[:, :, :], 1e-7))
                nc.vector.reciprocal(u[:, :, :], s1[:, :, :]).then_inc(u_ready, 1)
                dve.wait_ge(q4_ready, image + 1)
                dve.wait_ge(u_ready, image + 1)
                attn_chain(nc.vector.tensor_reduce(s2[:, 0, :], q4.rearrange("p (n c) -> p n c", c=C), axis=AX.X, op=ALU.add))
                attn_chain(nc.vector.tensor_tensor(s2[:, 0, :], s2[:, 0, :], u[:, 0, :], ALU.mult))
                attn_chain(nc.vector.tensor_tensor(s2[:, 0, :], s2[:, 0, :], u[:, 0, :], ALU.mult))
                nc.vector.tensor_scalar_max(s2[:, 0, :], s2[:, 0, :], 1e-12).then_inc(norm_q, 1)
                attn_chain.end()

            def norms_end(image):
                attn2_chain.begin(dve, image)
                dve.wait_ge(root_q, image + 1)
                attn2_chain(nc.vector.reciprocal(r[:, 0, :], s2[:, 0, :]))
                attn2_chain(nc.vector.tensor_tensor(r[:, 0, :], r[:, 0, :], u[:, 0, :], ALU.mult))
                q = tokens(Q_AT)
                nc.vector.tensor_tensor(q, q, columns(r[:, :, :], 0, [[1, 2 * RUN], [0, C]]), ALU.mult).then_inc(q_scaled, 1)
                attn2_chain.end()

            def sums_out(image):
                bank = ring_a.bank(A_G)
                dve.wait_ge(g_done, image + 1)
                nc.vector.tensor_copy(gt[:, :], bank[0:SUMS, 0:C]).then_inc(gt_ready, 1)
                nc.vector.tensor_tensor(gm[:, :], bank[0:SUMS, 0:C], gram_mask[:, :], ALU.mult).then_inc(gt_ready, 1)

            def conv1_weights(image):
                bank = ring_a.bank(A_M2)
                dve.wait_ge(m2_done, image + 1)
                nc.vector.tensor_scalar_max(rk[:, :], bank[0:C, C2:C2 + 1], 1e-12).then_inc(norm_k, 1)
                dve.wait_ge(root_k, image + 1)
                nc.vector.reciprocal(rk[:, :], rk[:, :]).then_inc(rk_ready, 1)
                dve.wait_ge(rk_ready, image + 1)
                nc.vector.tensor_scalar(w1_cur[0:C, :], bank[0:C, 0:C2], rk[:, 0:1], None, ALU.mult).then_inc(w1_ready, 1)

            def depthwise_at(image, place):
                if image is not None:
                    done = sum(steps_at[:place])
                    depthwise(image, done, done + steps_at[place])

            def depthwise(image, s0, s1):
                for s in range(s0, s1):
                    n, t = tap_of_step(s)
                    _, dst, c, _ = unit(n)
                    if t == 1:
                        dve.wait_ge(tap1_ready, UNITS * image + n + 1)
                    else:
                        dve.wait_ge(tap_step, TAP_STEPS * image + s - 1)
                    at = Y_DW + c * TAPS + t
                    nc.vector.scalar_tensor_tensor(out=dst, in0=tap_input(n, t), scalar=dyn[:, at:at + 1],
                                                   in1=dst, op0=ALU.mult, op1=ALU.add).then_inc(tap_step, 1)

            def conv1_out(image, f):
                after(dve, l3_done, PCHUNKS * (image - 1))
                for k in range(CHUNKS):
                    depthwise_at(f, BY_CONV1 + k)
                    dve.wait_ge(y1_slope, CHUNKS * image + k + 1)
                    bank = ring_c.bank(C_1 + k)
                    nc.vector.tensor_tensor(y1[:, k % 2, :], bank[0:C2, :], y1[:, k % 2, :], ALU.max).then_inc(y1_max, 1)
                    dve.wait_ge(y1_max, CHUNKS * image + k + 1)
                    nc.vector.tensor_copy(y1_view(y1_h, k), y1_tokens(k)).then_inc(y1h_ready, 1)

            def conv2_out(f, back):
                for k in range(CHUNKS):
                    depthwise_at(back, BY_CONV2 + k)
                    if k >= 3 and k % 2 == 1:
                        l1_low_part(f, k // 2 - 1)
                    dve.wait_ge(y2_slope, CHUNKS * f + k + 1)
                    dst = y2[(k // 2) % 2][:, (k % 2) * BANK:(k % 2 + 1) * BANK]
                    nc.vector.scalar_tensor_tensor(out=dst, in0=ring_c.bank(C_2 + k)[0:C2, :],
                                                   scalar=col96[:, T_B2:T_B2 + 1], in1=dst,
                                                   op0=ALU.add, op1=ALU.max).then_inc(y2_ready, 1)
                    if k >= 2 and k % 2 == 0:
                        w3_out(f, k // 2 - 1)

            def w3_out(f, m):
                dve.wait_ge(w3_done, PCHUNKS * f + m + 1)
                if m >= 2:
                    dve.wait_ge(ah1_ready, PCHUNKS * f + m - 1)
                x_in = columns(xcm[0:C2, :], m * ROWS * WQ, [[1, ROWS * WQ], [128, RUN]])
                nc.vector.scalar_tensor_tensor(
                    out=v[:, m % 2, :].rearrange("p (a b) -> p a b", b=RUN),
                    in0=ring_b.bank(B_W3 + m)[0:C2, :].rearrange("p (a b) -> p a b", b=RUN),
                    scalar=col96[:, T_B3:T_B3 + 1], in1=x_in, op0=ALU.add, op1=ALU.add).then_inc(v_ready, 1)

            def l1_low_part(f, m):
                dve.wait_ge(ah1_ready, PCHUNKS * f + m + 1)
                low_part(a_h[L1], a_l[L1], v, m).then_inc(al1_ready, 1)

            def low_part(hi, lo, src, m):
                rows = slice(m * ROWS + 1, (m + 1) * ROWS + 1)
                return nc.vector.scalar_tensor_tensor(
                    out=lo[:, rows, 1:W + 1], in0=src[:, m % 2, :].rearrange("p (j w) -> p j w", w=W), scalar=0.0,
                    in1=hi[:, rows, 1:W + 1].bitcast(F32), op0=ALU.max, op1=ALU.subtract)

            def project_out(b, m):
                dve.wait_ge(v3_affine, PCHUNKS * b + m + 1)
                nc.vector.tensor_tensor(v[:, m % 2, :], v[:, m % 2, :], x2[:, m * BANK:(m + 1) * BANK], ALU.add)\
                    .then_inc(v3_ready, 1)

            def l3_low_part(b, m):
                dve.wait_ge(ah3_ready, PCHUNKS * b + m + 1)
                low_part(a_h[L3], a_l[L3], v, m).then_inc(al3_ready, 1)

            def mean_out(f):
                dve.wait_ge(x2_ready, PCHUNKS * f + PCHUNKS)
                nc.vector.tensor_reduce(mean[:, :], msum[:, :], axis=AX.X, op=ALU.add).then_inc(mean_sum, 1)
                dve.wait_ge(mean_sum, f + 1)
                nc.vector.tensor_scalar(mean_b[:, :], ones[0:C2, :], mean[:, 0:1], 1.0 / TOKENS, ALU.mult, ALU.mult)\
                    .then_inc(mean_ready, 1)

            def route(f):
                dve.wait_ge(rw_done, f + 1)
                nc.vector.tensor_tensor(rwz[:, :], ring_b.bank(B_RW)[:, 0:EXPERTS], br[:, :], ALU.add).then_inc(rwz_ready, 1)

            def mix(chain, dst, src):
                chain(nc.vector.tensor_scalar(dst, src[:, 0, :], rw[0:dst.shape[0], 0:1], None, ALU.mult))
                for e in range(1, EXPERTS):
                    chain(nc.vector.scalar_tensor_tensor(out=dst, in0=src[:, e, :], scalar=rw[0:dst.shape[0], e:e + 1],
                                                         in1=dst, op0=ALU.mult, op1=ALU.add))

            def mix_weights(f):
                weight_chain.begin(dve, f)
                dve.wait_ge(rw_ready, f + 1)
                weight_chain(nc.vector.tensor_tensor(prod[:, :, :], lin[:, :, :], columns(rw[:, :], 0, [[0, Y_ALL], [1, EXPERTS]]), ALU.mult))
                weight_chain(nc.vector.tensor_reduce(dyn[:, :], prod[:, :, :], axis=AX.X, op=ALU.add))
                weight_chain(nc.vector.tensor_tensor(dyn[:, :], dyn[:, :], lin_const[:, :], ALU.add))
                mix(weight_chain, wk[:, :], wpw[:, :, :])
                nc.vector.tensor_scalar(ew[:, 0, :], wk[:, :], mask_par[:, 0:1], None, ALU.mult)
                weight_chain(nc.vector.tensor_scalar(ew[:, 1, :], wk[:, :], mask_par[:, 1:2], None, ALU.mult))
                weight_chain.end()
                project_weight_chain.begin(dve, f)
                mix(project_weight_chain, pk[:, :, :].rearrange("p c f -> p (c f)"),
                    wpl[:, :, :, :].rearrange("p e c f -> p e (c f)"))
                project_weight_chain.end()
                nc.vector.tensor_copy(pc[:, 0, C:C2], pk[:, 0, :]).then_inc(pc_ready, 1)
                for half in range(2):
                    nc.vector.tensor_scalar(pc[:, 1 + half, C:C2], pk[:, 1, :], mask_half[:, half:half + 1], None, ALU.mult)\
                        .then_inc(pc_ready, 1)

            def iteration(f, attn, back):
                conv2_out(f, back)
                if back is not None:
                    depthwise_at(back, BY_PROJECT)
                    project_out(back, 0)
                    depthwise_at(back, BY_PROJECT + 1)
                    l3_low_part(back, 0)
                w3_out(f, PCHUNKS - 1)
                depthwise_at(back, BY_PROJECT + 2)
                l1_low_part(f, PCHUNKS - 1)
                if back is not None:
                    project_out(back, 1)
                    l3_low_part(back, 1)
                    depthwise_at(back, BY_PROJECT + 3)
                    for m in (2, 3):
                        project_out(back, m)
                        l3_low_part(back, m)
                mean_out(f)
                route(f)
                if attn is not None:
                    norms_begin(attn)
                mix_weights(f)
                if attn is not None:
                    norms_end(attn)
                    sums_out(attn)
                    conv1_weights(attn)
                    conv1_out(attn, f)

            norms_begin(0)
            norms_end(0)
            sums_out(0)
            conv1_weights(0)
            conv1_out(0, None)
            iteration(0, 1, None)
            with dve.Fori(1, IMAGES - 1) as f:
                iteration(f, f + 1, f - 1)
            iteration(IMAGES - 1, None, IMAGES - 2)
            depthwise(IMAGES - 1, 0, TAP_STEPS)
            for m in range(PCHUNKS):
                project_out(IMAGES - 1, m)
                l3_low_part(IMAGES - 1, m)

        def wait(sp, semaphore, value):
            if not isinstance(value, int) or value > 0:
                sp.wait_ge(semaphore, value)
                sp.sem_inc(sync_waits, 1)

        def load_x(sp, image, transposed_images, projected_images):
            src = a["x"][image].rearrange("(j b) (q i) c -> b q j i c", b=2, q=WQ)
            wait(sp, project_done, PCHUNKS * projected_images)
            by_column = xa.rearrange("p (i b c) -> p b i c", b=2, c=C)
            for n in range(2 * WQ):
                par, q = n % 2, n // 2
                sp.dma_start(by_column[q::WQ, par], src[par, q]).then_inc(xa_loaded, 16)
            wait(sp, xqt_done, CHUNKS * transposed_images)
            for n in range(2 * WQ):
                par, q = n % 2, n // 2
                sp.dma_start(tok[q::WQ, par, :, X_AT:X_AT + C], src[par, q]).then_inc(x_loaded, 16)

        def copy_beside(sp, n, half):
            r0, rows = half * PAIRS // 2, PAIRS // 2
            for hi_or_lo in ((b_h, a_h[n]), (b_l, a_l[n])):
                dst, src = (t[:, :, :].bitcast(F32) for t in hi_or_lo)
                sp.dma_start(dst[0:C, r0:r0 + rows, :], src[0:C, r0 + 2:r0 + rows + 2, :]).then_inc(b_copied[n][half], 16)
                sp.dma_start(dst[C:C2, r0:r0 + rows, :], src[C:C2, r0:r0 + rows, :]).then_inc(b_copied[n][half], 16)

        def store(sp, image):
            wait(sp, ot_ready, 4 * image + 4)
            dst = out[image].rearrange("(j b) (q i) c -> q j b (i c)", b=2, q=WQ)
            for q in range(WQ):
                sp.dma_start(dst[q], ot[q::WQ, :].rearrange("p (b n) -> p b n", b=2)).then_inc(stored, 16)

        def beside_l1(sp, f):
            wait(sp, l3_done, PCHUNKS * (f - 1))
            for half in range(2):
                chunks = 3 + half
                wait(sp, ah1_ready, PCHUNKS * f + chunks)
                wait(sp, al1_ready, PCHUNKS * f + chunks)
                wait(sp, conv2_done, CHUNKS * f + 3 + 2 * half)
                copy_beside(sp, L1, half)

        def beside_l3(sp, b, l1_images):
            wait(sp, l1_done, PCHUNKS * l1_images)
            for half in range(2):
                chunks = 3 + half
                wait(sp, ah3_ready, PCHUNKS * b + chunks)
                wait(sp, al3_ready, PCHUNKS * b + chunks)
                copy_beside(sp, L3, half)

        @block.sync
        def _(sp):
            load_x(sp, 0, 0, 0)
            for dst, src in loads[0:6]:
                sp.dma_start(dst, src).then_inc(loaded, 16)
            sp.wait_ge(cleared, len(cleared_tiles))
            for dst, src in loads[6::2]:
                sp.dma_start(dst, src).then_inc(loaded, 16)
            sp.wait_ge(prep_dve, marks["placed"])
            for dst, src in placements:
                sp.dma_start(dst, src).then_inc(prep_dma, 16)

            def iteration(f, attn, back):
                beside_l1(sp, f)
                if attn is not None:
                    load_x(sp, attn, attn, f)
                if back is not None:
                    beside_l3(sp, back, f + 1)
                    store(sp, back)

            iteration(0, 1, None)
            with sp.Fori(1, IMAGES - 1) as f:
                iteration(f, f + 1, f - 1)
            iteration(IMAGES - 1, None, IMAGES - 2)
            beside_l3(sp, IMAGES - 1, IMAGES)
            store(sp, IMAGES - 1)
            sp.wait_ge(stored, 16 * WQ * IMAGES)

        @block.gpsimd
        def _(pool):
            nc.gpsimd.memset(ident[:, :], 0.0).then_inc(masks_ready, 1)
            nc.gpsimd.memset(gram_mask[:, :], 0.0).then_inc(masks_ready, 1)
            pool.wait_ge(masks_ready, 2)
            nc.gpsimd.affine_select(out=ident[:, :], in_=ident[:, :], compare_op=ALU.not_equal, fill=1.0,
                                    base=0, pattern=[[-1, 128]], channel_multiplier=1).then_inc(masks_ready, 1)
            nc.gpsimd.affine_select(out=gram_mask[:, :], in_=gram_mask[:, :], compare_op=ALU.not_equal, fill=1.0,
                                    base=-C, pattern=[[-1, C]], channel_multiplier=1).then_inc(masks_ready, 1)

            def scale_k(image):
                pool.wait_ge(squared, 16 * image + 16)
                pool.wait_ge(u_ready, image + 1)
                k = tokens(K_AT)
                nc.gpsimd.tensor_tensor(k, k, columns(u[:, :, :], 2 * RUN, [[1, 2 * RUN], [0, C]]), ALU.mult).then_inc(k_scaled, 1)

            def split_y1(image):
                for k in range(CHUNKS):
                    pool.wait_ge(y1h_ready, CHUNKS * image + k + 1)
                    nc.gpsimd.tensor_tensor(y1_view(y1_l, k), y1_tokens(k), y1_view(y1_h, k).bitcast(F32),
                                            ALU.subtract).then_inc(y1l_ready, 1)

            scale_k(0)
            split_y1(0)
            with pool.Fori(1, IMAGES) as image:
                scale_k(image)
                split_y1(image)

        @block.tensor
        def _(pe):
            pe.wait_ge(loaded, 16 * len(loads))
            pe.wait_ge(masks_ready, 4)
            nc.tensor.transpose(banks[0][0:C2, 0:T_ROWS], tab96[:, :], ident[0:T_ROWS, 0:T_ROWS]).then_inc(prep_pe, 1)
            for c in range(2):
                nc.tensor.transpose(banks[1][:, c * 64:c * 64 + U_ROWS], tab192[:, c * M1:(c + 1) * M1],
                                    ident[0:U_ROWS, 0:U_ROWS]).then_inc(prep_pe, 1)
            pe.wait_ge(prep_dve, marks["bn_fold"])
            nc.tensor.matmul(banks[2][0:C + 1, 0:3 * C], bn_fold[:, :], wqkv[:, :], start=True, stop=True).then_inc(prep_pe, 1)
            nc.tensor.matmul(banks[3][0:C, 0:C + 1], wqkv[:, 2 * C:3 * C], bn_fold[:, :], start=True, stop=True).then_inc(prep_pe, 1)
            pe.wait_ge(prep_dve, marks["wv_t"])
            nc.tensor.matmul(banks[4][0:C, 0:C + 1], wln[:, :], wv_t[:, :], start=True, stop=True).then_inc(prep_pe, 1)
            pe.wait_ge(prep_dve, marks["p1"])
            nc.tensor.matmul(banks[5][0:C + 1, 0:C2], p1[:, :], w1a[:, :], start=True, stop=True).then_inc(prep_pe, 1)
            nc.tensor.matmul(banks[6][0:C + 1, 0:C2], p1b[:, :], w1a[:, :], start=True, stop=False)
            nc.tensor.matmul(banks[6][0:C + 1, 0:C2], ident[0:C + 1, 0:C + 1], w1b[:, :], start=False, stop=True).then_inc(prep_pe, 1)
            for n, (layer, t) in enumerate(((L1, T_DWB1), (L3, T_DWB3))):
                nc.tensor.matmul(banks[7][0:C2, n:n + 1], pw[layer][0:C, :, :].rearrange("p a c -> p (a c)"), col96[0:C, t:t + 1], start=True, stop=True).then_inc(prep_pe, 1)
            pe.wait_ge(prep_dve, marks["all"])
            pe.wait_ge(prep_dma, 16 * len(placements))

            def attention_scores(image):
                pe.wait_ge(xa_loaded, 32 * WQ * (image + 1))
                for n in range(4):
                    bank = ring_a.take(pe, image, A_XT + n)
                    for m in range(4):
                        i = 4 * n + m
                        last = nc.tensor.transpose(bank[0:C2, m * 128:(m + 1) * 128],
                                                   xa[:, i * C2:(i + 1) * C2], ident[:, :])
                    last.then_inc(xt_done, 1)
                for n in range(8):
                    bank = ring_a.take(pe, image, A_QK + n)
                    if n % 2 == 0:
                        pe.wait_ge(xcm_ready, 4 * image + n // 2 + 1)
                    for m in range(2):
                        i = 2 * n + m
                        last = nc.tensor.matmul(bank[:, m * 2 * C2:(m + 1) * 2 * C2], xcm[:, i * 128:(i + 1) * 128],
                                                qkw[:, :], start=True, stop=True)
                    last.then_inc(qk_done, 1)

            def attention_sums(image):
                bank = ring_a.take(pe, image, A_G)
                pe.wait_ge(x_loaded, 32 * WQ * (image + 1))
                pe.wait_ge(k_scaled, image + 1)
                for par in range(2):
                    for i in range(RUN):
                        first, final = par == 0 and i == 0, par == 1 and i == RUN - 1
                        last = nc.tensor.matmul(bank[0:SUMS, 0:C], token(par, i, X_AT, SUMS), token(par, i, K_AT, C),
                                                start=first, stop=final)
                last.then_inc(g_done, 1)

            def attention_weights(image):
                bank = ring_a.take(pe, image, A_M2)
                pe.wait_ge(gt_ready, 2 * image + 2)
                nc.tensor.matmul(bank[0:C, 0:C2], gt[:, :], wva_aug[:, :], start=True, stop=True)
                nc.tensor.matmul(bank[0:C, C2:C2 + 1], gm[:, :], ones[0:SUMS, 0:1], start=True, stop=True).then_inc(m2_done, 1)

            def conv1(image, f):
                for k in range(BEFORE, CHUNKS + 1):
                    if image is not None and 0 <= k < CHUNKS:
                        if k == 0:
                            pe.wait_ge(q_scaled, image + 1)
                        par, i0 = k // 4, 4 * (k % 4)
                        bank = ring_a.take(pe, image, A_XQ + k)
                        for m in range(4):
                            last = nc.tensor.transpose(bank[0:C2, m * 128:(m + 1) * 128],
                                                       token(par, i0 + m, Q_AT, C2), ident[:, :])
                        last.then_inc(xqt_done, 1)
                    if image is not None and k > 0:
                        if k == 1:
                            pe.wait_ge(w1_ready, image + 1)
                        bank = ring_c.take(pe, image, C_1 + k - 1)
                        pe.wait_ge(xq_ready, CHUNKS * image + k)
                        nc.tensor.matmul(bank[0:C2, :], w1_cur[:, :], xq[:, (k - 1) % 2, :], start=True, stop=True)\
                            .then_inc(conv1_done, 1)
                    for n in expand_beside[k] if f is not None else ():
                        expand(f, n)

            def conv2(image):
                for k in range(CHUNKS):
                    bank = ring_c.take(pe, image, C_2 + k)
                    for n, (wgt, src, ready) in enumerate(((w2_h, y1_h, y1h_ready), (w2_l, y1_h, y1h_ready),
                                                           (w2_h, y1_l, y1l_ready))):
                        if k == 0 and n != 1:
                            pe.wait_ge(ready, CHUNKS * image + CHUNKS)
                        for t in range(TAPS):
                            rows, cols = slice(k * ROWS + t // 3, k * ROWS + t // 3 + ROWS), slice(t % 3, t % 3 + W)
                            last = nc.tensor.matmul(bank[0:C2, :], wgt[:, t, :], src[:, rows, cols],
                                                    start=t + n == 0, stop=t == TAPS - 1 and n == 2)
                    last.then_inc(conv2_done, 1)
                    if k >= 2 and k % 2 == 0:
                        w3(image, k // 2 - 1)

            def w3(image, m):
                bank = ring_b.take(pe, image, B_W3 + m)
                pe.wait_ge(y2_ready, CHUNKS * image + 2 * m + 2)
                rows = y2[m % 2].rearrange("p (j b w) -> p j b w", b=2, w=W)
                for par in range(2):
                    last = nc.tensor.matmul(bank[0:C2, :], w3eo[:, par, :], rows[:, :, par, :], start=par == 0, stop=par == 1)
                last.then_inc(w3_done, 1)

            def pair_conv(image, layer, ring, first, done, chunks):
                for m in chunks:
                    bank = ring.take(pe, image, first + m)
                    n = 0
                    for beside in range(2):
                        if beside == 1 and m % 2 == 0:
                            pe.wait_ge(b_copied[layer][m // 2], 64 * (image + 1))
                        hi, lo = ((a_h[layer], a_l[layer]), (b_h, b_l))[beside]
                        r0 = m * ROWS + 1 - beside
                        for kw in range(3):
                            for wgt, src in ((wt_h, hi), (wt_l, hi), (wt_h, lo)):
                                last = nc.tensor.matmul(bank[0:C2, :], wgt[layer][:, kw, beside, :],
                                                        src[:, r0:r0 + ROWS, kw:kw + W], start=n == 0, stop=n == 17)
                                n += 1
                    last.then_inc(done, 1)

            def routing(image):
                bank = ring_b.take(pe, image, B_RW)
                pe.wait_ge(mean_ready, image + 1)
                nc.tensor.matmul(bank[:, 0:EXPERTS], mean_b[:, :], wr[:, :], start=True, stop=True).then_inc(rw_done, 1)

            def expand_halo(image):
                pe.wait_ge(weight_chain.sem, weight_chain.each * (image + 1))
                x2_rows = x2[:, :].rearrange("p (j w) -> p j w", w=W)
                bank = ring_b.take(pe, image, B_HALO)
                nc.tensor.matmul(bank[:, 0:W], ew[:, 0, E_OTHER:E_OTHER + M1], x2_rows[:, PAIRS // 2, :], start=True, stop=True)
                nc.tensor.matmul(bank[:, W:2 * W], ew[:, 1, E_BOTTOM:E_BOTTOM + M1], x2_rows[:, PAIRS // 2 - 1, :],
                                 start=True, stop=True).then_inc(expand_done, 1)

            def expand(image, n):
                x2_rows = x2[:, :].rearrange("p (j w) -> p j w", w=W)
                bank = ring_b.take(pe, image, B_E + n)
                par, g = n % 2, (n if n < 4 else n - 4) // 2
                parts = (((E_OTHER, g), (E_BOTTOM, g + 2)) if n < 4 else ((0, g),))
                for part, (at, g) in enumerate(parts):
                    last = nc.tensor.matmul(bank[:, :], ew[:, par, at:at + M1], x2_rows[:, g * ROWS:(g + 1) * ROWS, :],
                                            start=part == 0, stop=part == len(parts) - 1)
                last.then_inc(expand_done, 1)

            def project(image, chunks):
                for m in chunks:
                    bank = ring_d.take(pe, image, D_P + m)
                    if m == 0:
                        pe.wait_ge(pc_ready, 3 * image + 3)
                    pe.wait_ge(h2_ready, UNITS * image + OTHER_UNITS + m + 1)
                    first = dwa[:, :, :].rearrange("p (j b) w -> p j b w", b=2)[:, m * ROWS:(m + 1) * ROWS]
                    m2 = m % 2
                    other = dwb[:, :, :].rearrange("p (j b) w -> p j b w", b=2)[:, m2 * ROWS:(m2 + 1) * ROWS]
                    for par in range(2):
                        cols = slice(C - C * par, 3 * C - C * par)
                        nc.tensor.matmul(bank[0:C2, :], pc[:, 0, cols], first[:, :, par, :], start=par == 0, stop=False)
                        last = nc.tensor.matmul(bank[0:C2, :], pc[:, 1 + m // 2, cols], other[:, :, par, :],
                                                start=False, stop=par == 1)
                    last.then_inc(project_done, 1)

            def out_tokens(image):
                for n in range(4):
                    bank = ring_d.take(pe, image, D_OUT + n)
                    if n == 0:
                        pe.wait_ge(outc_ready, PCHUNKS * image + PCHUNKS)
                    for m in range(4):
                        i = 4 * n + m
                        last = nc.tensor.transpose(bank[:, m * C2:(m + 1) * C2], outc[:, i::RUN], ident[0:C2, 0:C2])
                    last.then_inc(outt_done, 1)

            def l1(image, chunks):
                pair_conv(image, L1, ring_b, B_L1, l1_done, chunks)

            def l3(image):
                pair_conv(image, L3, ring_d, D_L3, l3_done, range(PCHUNKS))

            def iteration(f, attn, back):
                conv2(f)
                if back is not None:
                    project(back, (0,))
                w3(f, PCHUNKS - 1)
                if back is not None:
                    project(back, (1,))
                l1(f, (0, 1))
                if back is not None:
                    project(back, (2, 3))
                l1(f, (2, 3))
                if attn is not None:
                    attention_scores(attn)
                routing(f)
                if back is not None:
                    l3(back)
                if attn is not None:
                    attention_sums(attn)
                if back is not None:
                    out_tokens(back)
                if attn is not None:
                    attention_weights(attn)
                expand_halo(f)
                conv1(attn, f)

            attention_scores(0)
            attention_sums(0)
            attention_weights(0)
            conv1(0, None)
            iteration(0, 1, None)
            with pe.Fori(1, IMAGES - 1) as f:
                iteration(f, f + 1, f - 1)
            iteration(IMAGES - 1, None, IMAGES - 2)
            project(IMAGES - 1, range(PCHUNKS))
            l3(IMAGES - 1)
            out_tokens(IMAGES - 1)

        @block.scalar
        def _(act):
            act.wait_ge(cleared, len(cleared_tiles))
            for dst, src in loads[7::2]:
                act.dma_start(dst, src).then_inc(loaded, 16)
            act.wait_ge(prep_dve, marks["variances"])
            nc.scalar.activation(inv96[:, :], inv96[:, :], ACT.Sqrt).then_inc(prep_act, 1)
            nc.scalar.activation(invm[:, :, :], invm[:, :, :], ACT.Sqrt).then_inc(prep_act, 1)
            act.wait_ge(prep_dve, marks["all"])

            def scores_out(image):
                for n in range(4):
                    act.wait_ge(xt_done, 4 * image + n + 1)
                    nc.scalar.activation(xcm[0:C2, n * BANK:(n + 1) * BANK], ring_a.bank(A_XT + n)[0:C2, :], ACT.Copy)\
                        .then_inc(xcm_ready, 1)
                for n in range(8):
                    act.wait_ge(qk_done, 8 * image + n + 1)
                    src = ring_a.bank(A_QK + n)[:, 0:4 * C2].rearrange("p (m b s c) -> p m b s c", m=2, b=2, s=2)
                    for s, at in enumerate((Q_AT, K_AT)):
                        dst = columns(tok[:, :, :, :], 2 * n * TOK + at, [[TOK, 2], [RUN * TOK, 2], [1, C]])
                        nc.scalar.activation(dst, src[:, :, :, s, :], ACT.Square).then_inc(squared, 1)

            def fourth_powers(image):
                act.wait_ge(squared, 16 * image + 16)
                nc.scalar.activation(q4.rearrange("p (n c) -> p n c", c=C), tokens(Q_AT), ACT.Square).then_inc(q4_ready, 1)

            def root_of_q(image):
                act.wait_ge(norm_q, image + 1)
                nc.scalar.activation(s2[:, 0, :], s2[:, 0, :], ACT.Sqrt).then_inc(root_q, 1)

            def root_of_k(image):
                act.wait_ge(norm_k, image + 1)
                nc.scalar.activation(rk[:, :], rk[:, :], ACT.Sqrt, scale=float(TOKENS)).then_inc(root_k, 1)

            def conv1_slope(image, f):
                begun = {2: (0, 1), CHUNKS: (2, 3)}
                for k in range(BEFORE, CHUNKS + 1):
                    if image is not None and 0 <= k < CHUNKS:
                        act.wait_ge(xqt_done, CHUNKS * image + k + 1)
                        if k >= 2:
                            act.wait_ge(conv1_done, CHUNKS * image + k - 1)
                        nc.scalar.activation(xq[0:C2, k % 2, :], ring_a.bank(A_XQ + k)[0:C2, :], ACT.Copy).then_inc(xq_ready, 1)
                    if image is not None and k > 0:
                        act.wait_ge(conv1_done, CHUNKS * image + k)
                        after(act, y1l_ready, CHUNKS * image + k - 2)
                        nc.scalar.activation(y1[:, (k - 1) % 2, :], ring_c.bank(C_1 + k - 1)[0:C2, :], ACT.Copy, scale=SLOPE)\
                            .then_inc(y1_slope, 1)
                    if f is not None:
                        for n in expand_beside[k]:
                            h1_rows(f, n)
                        for n in begun.get(k, ()):
                            first_tap(f, n)

            def first_tap(image, n):
                _, dst, c, _ = unit(n)
                if n == 0:
                    after(act, stored, 16 * WQ * image)
                    act.wait_ge(h1_ready, H1_WRITES * image + 6)
                if n == OTHER_UNITS:
                    act.wait_ge(h1_ready, H1_WRITES * image + H1_WRITES)
                nc.scalar.activation(dst, tap_input(n, 0), ACT.Identity, bias=dyn[:, Y_DWB + c:Y_DWB + c + 1],
                                     scale=dyn[:, Y_DW + c * TAPS:Y_DW + c * TAPS + 1]).then_inc(tap1_ready, 1)

            def finish_unit(image, n):
                _, dst, _, _ = unit(n)
                act.wait_ge(tap_step, TAP_STEPS * image + last_step(n))
                nc.scalar.activation(dst, dst, ACT.Relu).then_inc(h2_ready, 1)

            def conv2_slope(f, back):
                finished = {1: (0, 1), 5: (2, 3)}
                begun = {3: (4,), 4: (5,)}
                for k in range(CHUNKS):
                    act.wait_ge(conv2_done, CHUNKS * f + k + 1)
                    after(act, w3_done, PCHUNKS * f + k // 2 - 1)
                    nc.scalar.activation(y2[(k // 2) % 2][:, (k % 2) * BANK:(k % 2 + 1) * BANK],
                                         ring_c.bank(C_2 + k)[0:C2, :], ACT.Identity, bias=b2s[:, 0:1], scale=SLOPE)\
                        .then_inc(y2_slope, 1)
                    if back is not None:
                        for n in begun.get(k, ()):
                            first_tap(back, n)
                        for n in finished.get(k, ()):
                            finish_unit(back, n)
                    if k >= 2 and k % 2 == 0:
                        l1_high_part(f, k // 2 - 1)

            def l1_high_part(f, m):
                act.wait_ge(v_ready, PCHUNKS * f + m + 1)
                high_part(a_h[L1], v, m).then_inc(ah1_ready, 1)

            def high_part(hi, src, m):
                return nc.scalar.activation(hi[:, m * ROWS + 1:(m + 1) * ROWS + 1, 1:W + 1],
                                            src[:, m % 2, :].rearrange("p (j w) -> p j w", w=W), ACT.Relu)

            def project_affine(b, l1_images, m):
                act.wait_ge(project_done, PCHUNKS * b + m + 1)
                if m < 2:
                    act.wait_ge(al1_ready, PCHUNKS * l1_images + m - 1)
                else:
                    act.wait_ge(al3_ready, PCHUNKS * b + m - 1)
                nc.scalar.activation(v[:, m % 2, :], ring_d.bank(D_P + m)[0:C2, :], ACT.Identity,
                                     bias=dyn[0:C2, Y_B3:Y_B3 + 1], scale=inv96[:, L2:L2 + 1]).then_inc(v3_affine, 1)
                act.wait_ge(v3_ready, PCHUNKS * b + m + 1)
                high_part(a_h[L3], v, m).then_inc(ah3_ready, 1)

            def l1_out(f, chunks):
                for m in chunks:
                    act.wait_ge(l1_done, PCHUNKS * f + m + 1)
                    nc.scalar.activation(x2[:, m * BANK:(m + 1) * BANK], ring_b.bank(B_L1 + m)[0:C2, :], ACT.Identity,
                                         bias=conv_bias[:, 0:1], scale=inv96[:, L1:L1 + 1],
                                         accum_out=msum[:, m:m + 1]).then_inc(x2_ready, 1)

            def route(f):
                act.wait_ge(rwz_ready, f + 1)
                nc.scalar.activation(rw[:, :], rwz[:, :], ACT.Sigmoid).then_inc(rw_ready, 1)

            def l3_out(b, chunks):
                for m in chunks:
                    act.wait_ge(l3_done, PCHUNKS * b + m + 1)
                    nc.scalar.activation(outc[:, m * BANK:(m + 1) * BANK], ring_d.bank(D_L3 + m)[0:C2, :], ACT.Identity,
                                         bias=conv_bias[:, 1:2], scale=inv96[:, L3:L3 + 1]).then_inc(outc_ready, 1)

            def tokens_out(b):
                for n in range(4):
                    act.wait_ge(outt_done, 4 * b + n + 1)
                    src = ring_d.bank(D_OUT + n)[:, 0:4 * C2].rearrange("p (i b c) -> p b i c", b=2, c=C)
                    dst = columns(ot, 4 * n * C, [[RUN * C, 2], [C, 4], [1, C]])
                    nc.scalar.activation(dst, src, ACT.Copy).then_inc(ot_ready, 1)

            def halo_out(f):
                act.wait_ge(weight_chain.sem, weight_chain.each * (f + 1))
                bank = ring_b.bank(B_HALO)
                act.wait_ge(expand_done, 13 * f + 1)
                for n, (half, r) in enumerate(((slice(0, M2), PAIRS + 1), (slice(M2, M1), 0))):
                    nc.scalar.activation(h1b[half, r, 1:W + 1], bank[half, n * W:(n + 1) * W], ACT.Relu,
                                         bias=dyn[half, Y_B1 + 1:Y_B1 + 2], scale=invm[half, 1, 0:1]).then_inc(h1_ready, 1)

            def h1_rows(f, n):
                c, dst_tile = (1, h1b) if n < 4 else (0, h1a)
                par, g = n % 2, (n if n < 4 else n - 4) // 2
                r0 = 1 + 2 * ROWS * g + par
                act.wait_ge(expand_done, 13 * f + n + 2)
                nc.scalar.activation(dst_tile[:, r0:r0 + 2 * ROWS - 1:2, 1:W + 1],
                                     ring_b.bank(B_E + n)[:, :].rearrange("p (j w) -> p j w", w=W), ACT.Relu,
                                     bias=dyn[:, Y_B1 + c:Y_B1 + c + 1], scale=invm[:, c, 0:1]).then_inc(h1_ready, 1)

            def iteration(f, attn, back):
                conv2_slope(f, back)
                if back is not None:
                    project_affine(back, f + 1, 0)
                l1_high_part(f, PCHUNKS - 1)
                if back is not None:
                    project_affine(back, f + 1, 1)
                l1_out(f, (0,))
                if back is not None:
                    finish_unit(back, 4)
                    finish_unit(back, 5)
                l1_out(f, (1,))
                if back is not None:
                    project_affine(back, f + 1, 2)
                    project_affine(back, f + 1, 3)
                l1_out(f, (2, 3))
                if attn is not None:
                    scores_out(attn)
                route(f)
                if attn is not None:
                    fourth_powers(attn)
                if back is not None:
                    l3_out(back, (0, 1))
                if attn is not None:
                    root_of_q(attn)
                if back is not None:
                    l3_out(back, (2, 3))
                    tokens_out(back)
                if attn is not None:
                    root_of_k(attn)
                halo_out(f)
                conv1_slope(attn, f)

            scores_out(0)
            fourth_powers(0)
            root_of_q(0)
            root_of_k(0)
            conv1_slope(0, None)
            iteration(0, 1, None)
            with act.Fori(1, IMAGES - 1) as f:
                iteration(f, f + 1, f - 1)
            iteration(IMAGES - 1, None, IMAGES - 2)
            for n in range(UNITS - 2, UNITS):
                first_tap(IMAGES - 1, n)
            for n in range(UNITS):
                finish_unit(IMAGES - 1, n)
            for m in range(PCHUNKS):
                project_affine(IMAGES - 1, IMAGES, m)
            l3_out(IMAGES - 1, range(PCHUNKS))
            tokens_out(IMAGES - 1)


def kernel(**inputs):
    import numpy as _np
    import concourse.bacc as _bacc
    from concourse import mybir as _mybir
    from concourse.bass_utils import run_bass_kernel_spmd as _run

    nc = _bacc.Bacc("TRN2", target_bir_lowering=False, num_devices=1)
    arrays, args = {}, {}
    for name, value in inputs.items():
        value = _np.ascontiguousarray(value)
        arrays[f"in_{name}_dram"] = value
        args[name] = nc.dram_tensor(f"in_{name}_dram", value.shape, _mybir.dt.from_np(value.dtype), kind="ExternalInput").ap()
    out = nc.dram_tensor("out_dram", (IMAGES, H, W, C), _mybir.dt.float32, kind="ExternalOutput").ap()
    conv_chain_kernel(nc, args, out)
    return _run(nc, [arrays], core_ids=[0]).results[0]["out_dram"]
```

```python
from contextlib import ExitStack

import concourse.bass as bass
from concourse import mybir

F32 = mybir.dt.float32
F32R = mybir.dt.float32r
ALU = mybir.AluOpType
ACT = mybir.ActivationFunctionType
AX = mybir.AxisListType

IMAGES, H, W, C = 8, 64, 64, 48
C2 = 2 * C
TOKENS = H * W
PAIRS = H // 2
HALF = TOKENS // 2
WQ = 4
RUN = W // WQ
EXPERTS = 4
M = 192
M1 = 128
M2 = M - M1
TAPS = 9
WP = W + 2
BANK = 512
CHUNKS = TOKENS // BANK
PCHUNKS = HALF // BANK
ROWS = BANK // W
Q_AT, X_AT, K_AT, TOK = 0, C, 2 * C, 3 * C + 1
SUMS = 2 * C + 1
BN_EPS = 1e-3
SLOPE = 0.2

L0, L1, L3, L2 = 0, 1, 2, 3
Z_VAR, Z_GAMMA, Z_MEAN, Z_BETA, Z_BLN, Z_B3, Z_B2 = range(7)
Z_ROWS = 7
T_VAR, T_GAMMA, T_MEAN, T_BETA = 0, 3, 6, 9
T_DWB1, T_PWB1, T_DWB3, T_PWB3 = 12, 13, 14, 15
T_S1, T_S3, T_BPWL = 16, 28, 40
T_ROWS = 44
U_VAR, U_GAMMA, U_MEAN, U_BETA, U_BPW, U_BDW, U_WDW = 0, 2, 4, 6, 8, 12, 16
U_ROWS = U_WDW + EXPERTS * TAPS
Y_DW, Y_DWB, Y_B1, Y_B3 = 0, 2 * TAPS, 2 * TAPS + 2, 2 * TAPS + 4
Y_ALL = Y_B3 + 1
E_BOTTOM, E_OTHER, E_ALL = M1, M1 + M2, M1 + 3 * M2


BEHIND = 128 - C2
APART = C2 - BEHIND
B_COPIES, WT_COPIES, X2_COPIES = 7, 16, 4
Y1_BUFFERS = 3


class Ring:

    def __init__(self, banks, readers, first_free=False):
        assert len(readers) % 2 == 0
        self.banks, self.readers, self.first_free = banks, readers, first_free

    def bank(self, k):
        return self.banks[k % 2]

    def take(self, pe, image, k):
        sem, each, nth = self.readers[k - 2]
        if k >= 2:
            pe.wait_ge(sem, image * each + nth)
        elif not self.first_free and (not isinstance(image, int) or image > 0):
            pe.wait_ge(sem, image * each)
        return self.banks[k % 2]


class Chain:

    def __init__(self, sem, each):
        self.sem, self.each = sem, each

    def begin(self, engine, image):
        self.engine, self.image, self.k = engine, image, 0

    def __call__(self, instruction):
        instruction.then_inc(self.sem, 1)
        self.k += 1
        self.engine.wait_ge(self.sem, self.image * self.each + self.k)

    def end(self):
        assert self.k == self.each, self.k


def columns(ap, offset, dims):
    return bass.AP(ap.tensor, ap.offset + offset, [list(ap.ap[0])] + [list(d) for d in dims])


def twice(row_ap):
    (rs, rn), (es, en) = row_ap.ap
    return bass.AP(row_ap.tensor, row_ap.offset, [[rs, rn], [0, 2], [es, en]])


def conv_chain_kernel(nc, a, out):
    ctx = ExitStack()
    with ctx:
        def sb(name, shape, dt=F32):
            return ctx.enter_context(nc.sbuf_tensor(name, shape, dt))

        def sem(name):
            return ctx.enter_context(nc.semaphore(name))

        def row(name):
            return a[name].rearrange("(o n) -> o n", o=1)

        col0, col96 = sb("col0", [C2, Z_ROWS]), sb("col96", [C2, T_ROWS])
        colm = sb("colm", [128, 2, U_ROWS])
        ident = sb("ident", [128, 128])
        ones = sb("ones", [128, 128])
        gram_mask = sb("gram_mask", [SUMS, C])
        pick = sb("pick", [C2, 3 * C], F32R)
        mask_token = sb("mask_token", [C2 + 1, 2])
        mask_half = sb("mask_half", [128, 2])
        inv96, shift96 = sb("inv96", [C2, 4]), sb("shift96", [C2, 4])
        invm, shiftm = sb("invm", [128, 2, 2]), sb("shiftm", [128, 2, 2])
        inv0 = sb("inv0", [C + 1, 1])
        qk_mean = sb("qk_mean", [C2 + 1, 2])
        qkw = sb("qkw", [C2 + 1, 2 * C2])
        wva_aug = sb("wva_aug", [SUMS, C2])
        w1_cur = sb("w1_cur", [C2 + 1, C2])
        w2_h, w2_l = sb("w2_h", [C2, TAPS, C2], F32R), sb("w2_l", [C2, TAPS, C2], F32R)
        w3eo = sb("w3eo", [C2, 2, C2])
        b2s = sb("b2s", [C2, 1])
        wt_h, wt_l = ({n: sb(f"wt_{part}{n}", [128, 5, C2], F32R) for n in (L1, L3)} for part in "hl")
        conv_bias = sb("conv_bias", [C2, 2])
        wpw = sb("wpw", [C2, EXPERTS, M])
        wr, br = sb("wr", [C2, EXPERTS]), sb("br", [128, EXPERTS])
        wpl = sb("wpl", [128, EXPERTS, 2, C])
        lin, lin_const = sb("lin", [128, Y_ALL, EXPERTS]), sb("lin_const", [128, Y_ALL])
        s1, s2, u, r = (sb(n, [128, k, 2 * RUN]) for n, k in (("s1", 2), ("s2", 1), ("u", 2), ("r", 1)))
        gt, gm = sb("gt", [SUMS, C]), sb("gm", [SUMS, C])
        rk = sb("rk", [C, 1])
        msum, mean, mean_b = sb("msum", [C2, PCHUNKS]), sb("mean", [C2, 1]), sb("mean_b", [C2, 128])
        rwz, rw = sb("rwz", [128, EXPERTS]), sb("rw", [128, EXPERTS])
        prod, dyn = sb("prod", [128, Y_ALL, EXPERTS]), sb("dyn", [128, Y_ALL])
        wk = sb("wk", [C2, M])
        ew_h, ew_l = sb("ew_h", [C2, E_ALL], F32R), sb("ew_l", [C, E_ALL], F32R)
        pk = sb("pk", [128, 2, C])
        pc = sb("pc", [128, 3, 3 * C])
        tok = sb("tok", [128, 2, RUN, TOK])
        xcm = sb("xcm", [C2 + 1, RUN * 128])
        xq = sb("xq", [C2 + 1, 2, BANK])
        y1 = sb("y1", [C2, Y1_BUFFERS, BANK])
        y1_parts = sb("y1_parts", [128, 2, H + 2, WP], F32R)
        y1_h, y1_l = (y1_parts[0:C2, part, :, :] for part in range(2))
        y2 = [t[0:C2, 0:2, :].rearrange("p a n -> p (a n)") for t in (xq, y1)]
        v = sb("v", [C2, 2, BANK])
        a_parts = {n: sb(f"a_parts{n}", [128, 2, PAIRS + 2, WP], F32R) for n in (L1, L3)}
        a_h, a_l = ({n: a_parts[n][0:C2, part, :, :] for n in (L1, L3)} for part in range(2))
        b_parts = y1_parts[:, :, 1:PAIRS + 1, :]
        x2 = [sb(f"x2_{name}", [C2, HALF], F32R) for name in ("even", "odd")]
        x2_h, x2_l = y1_h[:, PAIRS + 1:H + 1, 1:W + 1], y1_l[:, PAIRS + 1:H + 1, 1:W + 1]
        h1a = sb("h1a", [128, H + 2, WP])
        h1b = sb("h1b", [128, PAIRS + 2, WP])
        dwa = sb("dwa", [128, H, W])
        dwb = sb("dwb", [128, PAIRS, W])
        dwa_flat, dwb_flat = dwa[:, :, :].rearrange("p h w -> p (h w)"), dwb[:, :, :].rearrange("p h w -> p (h w)")
        outc = dwa_flat[0:C2, HALF:2 * HALF]
        q4 = dwa_flat[:, 0:2 * RUN * C]
        xa = q4
        ot = dwb_flat[:, 0:2 * RUN * C]
        h1a_flat = h1a[:, :, :].rearrange("p h w -> p (h w)")
        scratch_used = [0]

        def scratch(partitions, width):
            at = scratch_used[0]
            scratch_used[0] += width
            assert scratch_used[0] <= (H + 2) * WP
            return h1a_flat[0:partitions, at:at + width]

        tab0, tab96, tab192 = scratch(Z_ROWS, C2), scratch(T_ROWS, C2), scratch(U_ROWS, M)
        wqkv, wln, w1a, w1b = scratch(C + 1, 3 * C), scratch(C, C), scratch(C, C2), scratch(C2 + 1, C2)
        bn_fold = scratch(C + 1, C2 + 1)
        wqk = scratch(C2 + 1, C2)
        wv_t, p1, p1b = scratch(C, C + 1), scratch(C, C2 + 1), scratch(C, C2 + 1)
        pw = {L1: scratch(C2, C2), L3: scratch(C2, C2)}
        norm3, norm1 = scratch(C, C), scratch(M1, M)
        wt_beside = {n: [ot[0:C2, (2 * k + part) * 3 * C2:(2 * k + part + 1) * 3 * C2].rearrange("p (k o) -> p k o", k=3)
                         for part in range(2)] for k, n in enumerate((L1, L3))}
        w2_f, wt_f = scratch(C2, TAPS * C2), scratch(C2, 6 * C2)

        banks = [ctx.enter_context(nc.psum_tensor(f"bank{n}", [128, BANK], F32)) for n in range(8)]
        norm_loaded = sem("norm_loaded")
        first_loaded, w2_loaded, loaded = sem("first_loaded"), sem("w2_loaded"), sem("loaded")
        wt_placed = sem("wt_placed")
        cleared, masks_ready = sem("cleared"), sem("masks_ready")
        prep_pe, prep_dve, prep_act = (sem(n) for n in ("prep_pe", "prep_dve", "prep_act"))
        xa_loaded, x_loaded = sem("xa_loaded"), sem("x_loaded")
        xt_done, qk_done, g_done, m2_done, xqt_done = (sem(n) for n in ("xt_done", "qk_done", "g_done", "m2_done", "xqt_done"))
        conv1_done, conv2_done, w3_done, l1_done = (sem(n) for n in ("conv1_done", "conv2_done", "w3_done", "l1_done"))
        rw_done, expand_done, project_done, l3_done, outt_done = (sem(n) for n in ("rw_done", "expand_done", "project_done", "l3_done", "outt_done"))
        xcm_ready, squared, q4_ready, root_q, root_k = (sem(n) for n in ("xcm_ready", "squared", "q4_ready", "root_q", "root_k"))
        norm_q, norm_k = sem("norm_q"), sem("norm_k")
        u_ready, q_scaled, k_scaled = sem("u_ready"), sem("q_scaled"), sem("k_scaled")
        gt_ready, w1_ready = sem("gt_ready"), sem("w1_ready")
        xq_ready, y1_slope, y1_max, y1h_ready, y1l_ready = (sem(n) for n in ("xq_ready", "y1_slope", "y1_max", "y1h_ready", "y1l_ready"))
        y2_slope, y2_ready, v_ready, ah1_ready, al1_ready = (sem(n) for n in ("y2_slope", "y2_ready", "v_ready", "ah1_ready", "al1_ready"))
        b_copied = {n: (sem(f"b{n}_first_copied"), sem(f"b{n}_rest_copied")) for n in (L1, L3)}
        x2_ready, x2h_ready, x2l_ready, x2_copied = (sem(n) for n in ("x2_ready", "x2h_ready", "x2l_ready", "x2_copied"))
        mean_ready, rwz_ready, rw_ready = (sem(n) for n in ("mean_ready", "rwz_ready", "rw_ready"))
        tap1_ready = sem("tap1_ready")
        diag_ready, taps_done = sem("diag_ready"), sem("taps_done")
        h1b_ready, h1a_ready, h2_ready = (sem(n) for n in ("h1b_ready", "h1a_ready", "h2_ready"))
        v3_ready, ah3_ready, al3_ready = (sem(n) for n in ("v3_ready", "ah3_ready", "al3_ready"))
        sync_waits = sem("sync_waits")
        outc_ready, ot_ready, stored = sem("outc_ready"), sem("ot_ready"), sem("stored")
        attn_chain, attn2_chain = Chain(sem("attn_chain"), 5), Chain(sem("attn2_chain"), 2)
        weight_chain = Chain(sem("weight_chain"), 11)
        rk_ready, mean_sum, pc_ready = sem("rk_ready"), sem("mean_sum"), sem("pc_ready")
        project_weight_chain = Chain(sem("project_weight_chain"), 4)
        tap_step = sem("tap_step")

        A_XT, A_QK, A_G, A_M2, A_XQ = 0, 4, 12, 13, 14
        ring_a = Ring(banks[0:2], [(xcm_ready, 4, n + 1) for n in range(4)]
                      + [(squared, 16, 2 * n + 2) for n in range(8)]
                      + [(gt_ready, 2, 2), (w1_ready, 1, 1)]
                      + [(xq_ready, CHUNKS, n + 1) for n in range(CHUNKS)])
        B_W3, B_L1, B_RW, B_HALO, B_E = 0, 4, 8, 9, 10
        ring_b = Ring(banks[2:4], [(v_ready, PCHUNKS, n + 1) for n in range(PCHUNKS)]
                      + [(x2_ready, PCHUNKS, n + 1) for n in range(PCHUNKS)]
                      + [(rwz_ready, 1, 1), (h1b_ready, 6, 2)]
                      + [(h1b_ready, 6, n + 3) for n in range(4)] + [(h1a_ready, 8, n + 1) for n in range(8)])
        C_1, C_2 = 0, 8
        ring_c = Ring(banks[4:6], [(y1_max, CHUNKS, n + 1) for n in range(CHUNKS)]
                      + [(y2_ready, CHUNKS, n + 1) for n in range(CHUNKS)])
        D_P, D_L3, D_OUT = 0, 4, 8
        ring_d = Ring(banks[6:8], [(ah3_ready, PCHUNKS, n + 1) for n in range(PCHUNKS)]
                      + [(outc_ready, PCHUNKS, n + 1) for n in range(PCHUNKS)]
                      + [(ot_ready, 4, n + 1) for n in range(4)], first_free=True)

        UNIT_ROWS = 2 * ROWS
        OTHER_UNITS = PAIRS // UNIT_ROWS
        UNITS = OTHER_UNITS + H // UNIT_ROWS
        FIRST_STEPS, PAIR_STEPS = 2 * TAPS, 2 * (TAPS - 1)
        TAP_STEPS = FIRST_STEPS + (UNITS - 2) // 2 * PAIR_STEPS
        BY_CONV1, BY_CONV2, BY_PROJECT = 0, CHUNKS, 2 * CHUNKS
        steps_at = (0, 1, 1, 1, 0, 1, 0, 0) + (8, 5, 5, 5, 5, 4, 4, 4) + (1, 1, 1, 3)
        assert sum(steps_at) == TAP_STEPS

        def unit(n):
            if n < OTHER_UNITS:
                r0 = n * UNIT_ROWS
                return h1b, dwb[:, r0:r0 + UNIT_ROWS, :], 1, r0
            r0 = (n - OTHER_UNITS) * UNIT_ROWS
            return h1a, dwa[:, r0:r0 + UNIT_ROWS, :], 0, r0

        def tap_input(n, t):
            src, _, _, r0 = unit(n)
            return src[:, r0 + t // 3:r0 + t // 3 + UNIT_ROWS, t % 3:t % 3 + W]

        def tap_of_step(s):
            if s < FIRST_STEPS:
                return s % 2, s // 2
            pair, rest = divmod(s - FIRST_STEPS, PAIR_STEPS)
            return 2 + 2 * pair + rest % 2, 1 + rest // 2

        def last_step(n):
            return FIRST_STEPS + n // 2 * PAIR_STEPS - 1 + n % 2

        def finished_at(place):
            done = sum(steps_at[:place])
            return [n for n in range(UNITS) if done < last_step(n) <= done + steps_at[place]]

        PE_UNITS = (2, 3)
        PE_CHUNKS = len(PE_UNITS) * UNIT_ROWS * W // BANK
        PE_BANKS = (0, 1, 4, 5)
        tap_diag = tok[:, :, :, :].rearrange("p b i c -> p (b i c)")[:, 0:TAPS * 128]

        loads, first_loads = [], []

        def load(dst, src):
            loads.append((dst, src))

        def both(table, r0, rows, src):
            return table[r0:r0 + rows, :].rearrange("r (a c) -> r a c", a=2), twice(src)

        for r0, name in ((Z_VAR, "bn_var"), (Z_GAMMA, "bn_gamma"), (Z_MEAN, "bn_mean"), (Z_BETA, "bn_beta"),
                         (Z_BLN, "b_ln"), (Z_B3, "b3")):
            first_loads.append(both(tab0, r0, 1, row("L0_conv_" + name)))
        w1_rows = a["L0_conv_w1"].rearrange("a b i o -> (a b i) o")
        first_loads += [
            (tab0[Z_B2:Z_B2 + 1, :], row("L0_conv_b2")),
            (wqkv[0:C, :], a["L0_conv_w_qkv"]), (wqkv[C:C + 1, :], row("L0_conv_b_qkv")),
            (wln[:, :], a["L0_conv_w_ln"]), (w1a[:, :], w1_rows[0:C, :]),
            (w1b[C:C2, :], w1_rows[C:C2, :]), (w1b[C2:C2 + 1, :], row("L0_conv_b1")),
        ]
        NORM_LOADS = 9
        norms = {L1: ("L1_conv_moving_var", "L1_conv_gamma", "L1_conv_moving_mean", "L1_conv_beta"),
                 L3: ("L3_conv_moving_var", "L3_conv_gamma", "L3_conv_moving_mean", "L3_conv_beta"),
                 L2: ("L2_conv_v3", "L2_conv_g3", "L2_conv_m3", "L2_conv_b3")}
        for n, names in norms.items():
            for r0, name in zip((T_VAR, T_GAMMA, T_MEAN, T_BETA), names):
                load(*both(tab96, r0 + n - L1, 1, row(name)))
        for r0, name in ((T_DWB1, "L1_conv_dw_bias"), (T_PWB1, "L1_conv_pw_bias"),
                         (T_DWB3, "L3_conv_dw_bias"), (T_PWB3, "L3_conv_pw_bias")):
            load(*both(tab96, r0, 1, row(name)))
        load(*both(tab96, T_BPWL, EXPERTS, a["L2_conv_bpwl"]))
        for r0, name in ((T_S1, "L1_conv_dw_kernel"), (T_S3, "L3_conv_dw_kernel")):
            dw = a[name].rearrange("h w o c -> h (w o) c")
            for g, (even, odd) in enumerate(((1, 2), (0, 1), (None, 0), (2, None))):
                for par, kh in enumerate((even, odd)):
                    if kh is not None:
                        load(tab96[r0 + 3 * g:r0 + 3 * g + 3, par * C:(par + 1) * C], dw[kh])
        w3_rows = a["L0_conv_w3"].rearrange("a b i o -> (a b i) o")
        for par in range(2):
            load(w3eo[:, par, par * C:(par + 1) * C], w3_rows)
            half = slice(par * C, (par + 1) * C)
            for n, name in ((L1, "L1_conv_pw_kernel"), (L3, "L3_conv_pw_kernel")):
                load(pw[n][half, :].rearrange("p (a c) -> p a c", a=2), twice(a[name].rearrange("a b i o -> (a b i) o")))
            wpw_src = a["L2_conv_Wpw"].rearrange("e c m -> c e m")
            load(wpw[half, :, :], wpw_src)
            load(wr[half, :], a["L2_conv_Wr"])
            wpl_src = a["L2_conv_Wpwl"].rearrange("e m f -> m e f")
            load(wpl[par * M2:(par + 1) * M2, :, 1, :], wpl_src[M1:M])
        load(wpl[:, :, 0, :], wpl_src[0:M1])
        br_row = row("L2_conv_br")
        load(br[:, :], bass.AP(br_row.tensor, br_row.offset, [[0, 128], [1, EXPERTS]]))
        for r0, name in ((U_VAR, "L2_conv_v1"), (U_VAR + 1, "L2_conv_v2"), (U_GAMMA, "L2_conv_g1"),
                         (U_GAMMA + 1, "L2_conv_g2"), (U_MEAN, "L2_conv_m1"), (U_MEAN + 1, "L2_conv_m2"),
                         (U_BETA, "L2_conv_b1"), (U_BETA + 1, "L2_conv_b2")):
            load(tab192[r0:r0 + 1, :], row(name))
        for r0, rows, src in ((U_BPW, EXPERTS, a["L2_conv_bpw"]), (U_BDW, EXPERTS, a["L2_conv_bdw"]),
                              (U_WDW, EXPERTS * TAPS, a["L2_conv_Wdw"].rearrange("e h w m -> (e h w) m"))):
            load(tab192[r0:r0 + rows, :], src)

        cleared_tiles = [w1b, tab96, w3eo]

        def y1_tokens(k):
            return columns(y1[:, :, :], (k % Y1_BUFFERS) * BANK, [[WQ, PAIRS], [1, WQ], [128, 4]])

        def y1_view(tile, k):
            par, i0 = k // 4, 4 * (k % 4)
            return columns(tile[:, :, :], (1 + par) * WP + 1 + i0, [[2 * WP, PAIRS], [RUN, WQ], [1, 4]])

        def tokens(at, outer=()):
            return columns(tok[:, :, :, :], at, [*outer, [TOK, 2 * RUN], [1, C]])

        def token(par, i, at, n):
            return tok[:, par, i, at:at + n]

        def after(engine, semaphore, value):
            if not isinstance(value, int) or value > 0:
                engine.wait_ge(semaphore, value)

        marks = {}
        H1B_WRITES, H1A_WRITES = 6, 8

        BEFORE = -1
        expand_beside = {BEFORE: (0, 1), 0: (2,), 1: (3, 4), 7: (), 8: (10, 11), **{k: (k + 3,) for k in range(2, 7)}}

        block = ctx.enter_context(nc.Block())

        @block.vector
        def _(dve):
            for n, tile in enumerate(cleared_tiles):
                nc.vector.memset(tile[:], 0.0).then_inc(cleared, 1)
            steps = [0]

            def step(instruction, name=None):
                instruction.then_inc(prep_dve, 1)
                steps[0] += 1
                dve.wait_ge(prep_dve, steps[0])
                if name is not None:
                    marks[name] = steps[0]

            step(nc.vector.memset(inv0[:], 1.0))
            for tile in (p1, p1b):
                step(nc.vector.memset(tile[:], 0.0))
            step(nc.vector.memset(mask_token[:, :], 1.0))
            step(nc.vector.memset(mask_token[0:C, 1:2], 0.0))
            step(nc.vector.tensor_scalar(mask_token[0:C2, 0:1], mask_token[0:C2, 1:2], -1.0, 1.0, ALU.mult, ALU.add))
            step(nc.vector.memset(tok[:, :, :, TOK - 1], 1.0))
            step(nc.vector.memset(xcm[C2:C2 + 1, :], 1.0))
            step(nc.vector.memset(xq[C2:C2 + 1, :, :], 1.0))
            step(nc.vector.memset(ones[:], 1.0))

            def fold_norm(inv, shift, gamma, mean, beta):
                step(nc.vector.reciprocal(inv, inv))
                step(nc.vector.tensor_tensor(inv, inv, gamma, ALU.mult))
                step(nc.vector.tensor_tensor(shift, inv, mean, ALU.mult))
                step(nc.vector.tensor_tensor(shift, beta, shift, ALU.subtract))

            dve.wait_ge(prep_pe, 1)
            step(nc.vector.tensor_copy(col0[:, :], banks[0][0:C2, 0:Z_ROWS]))
            step(nc.vector.tensor_scalar_add(inv96[:, L0:L0 + 1], col0[:, Z_VAR:Z_VAR + 1], BN_EPS), "variance")
            dve.wait_ge(prep_act, 1)
            fold_norm(inv96[:, L0:L0 + 1], shift96[:, L0:L0 + 1], *(col0[:, z:z + 1] for z in (Z_GAMMA, Z_MEAN, Z_BETA)))
            step(nc.vector.tensor_copy(inv0[0:C, :], inv96[0:C, L0:L0 + 1]))
            for at in (0, C):
                step(nc.vector.tensor_scalar(bn_fold[:, at:at + C], ident[0:C + 1, 0:C], inv0[:, 0:1], None, ALU.mult))
            step(nc.vector.tensor_copy(bn_fold[:, C2:C2 + 1], ident[0:C + 1, C:C + 1]))
            step(nc.vector.tensor_copy(bn_fold[0:C, C2:C2 + 1], shift96[0:C, L0:L0 + 1]), "bn_fold")
            dve.wait_ge(prep_pe, 3)
            step(nc.vector.tensor_copy(wv_t[:, :], banks[3][0:C, 0:C + 1]), "wv_t")
            qk = banks[2][0:C2 + 1, 0:C2].rearrange("p (s c) -> p s c", s=2)
            step(nc.vector.tensor_reduce(qk_mean[:, :], qk, axis=AX.X, op=ALU.add))
            step(nc.vector.tensor_scalar(qk_mean[:, :], qk_mean[:, :], -1.0 / C, None, ALU.mult))
            step(nc.vector.tensor_tensor(wqk[:, :].rearrange("p (s c) -> p s c", s=2), qk,
                                         columns(qk_mean[:, :], 0, [[1, 2], [0, C]]), ALU.add))
            for par in range(2):
                step(nc.vector.tensor_scalar(qkw[:, par * C2:(par + 1) * C2], wqk[:, :], mask_token[:, par:par + 1], None, ALU.mult))
            dve.wait_ge(prep_pe, 4)
            step(nc.vector.tensor_copy(p1[:, 0:C], banks[4][0:C, 0:C]))
            step(nc.vector.tensor_copy(p1[:, C2:C2 + 1], banks[4][0:C, C:C + 1]))
            step(nc.vector.tensor_copy(p1b[:, C:C2], banks[4][0:C, 0:C]))
            step(nc.vector.tensor_tensor(p1b[:, C2:C2 + 1], banks[4][0:C, C:C + 1], col0[0:C, Z_BLN:Z_BLN + 1], ALU.add), "p1")
            dve.wait_ge(prep_pe, 6)
            step(nc.vector.tensor_copy(wva_aug[:, :], banks[5][0:SUMS, 0:C2]))
            step(nc.vector.tensor_copy(w1_cur[:, :], banks[6][0:C2 + 1, 0:C2]))
            step(nc.vector.tensor_scalar(b2s[:, :], col0[:, Z_B2:Z_B2 + 1], SLOPE, None, ALU.mult), "attention")

            def prepare_conv2():
                dve.wait_ge(w2_loaded, 16)
                w2_src = w2_f.rearrange("p (t o) -> p t o", t=TAPS)
                step(nc.vector.tensor_copy(w2_h[:, :, :], w2_src))
                step(nc.vector.tensor_tensor(w2_l[:, :, :], w2_src, w2_h[:, :, :].bitcast(F32), ALU.subtract))
                for tile, rows in ((y1_parts, H + 2), (a_parts[L1], PAIRS + 2), (a_parts[L3], PAIRS + 2)):
                    edge = tile[:, :, :, :].bitcast(F32)
                    step(nc.vector.memset(edge[:, :, 0:rows:rows - 1, :], 0.0))
                    step(nc.vector.memset(edge[:, :, :, 0:WP:WP - 1], 0.0))
                step(nc.vector.memset(h1b[:, 0:PAIRS + 2:PAIRS + 1, :], 0.0))
                step(nc.vector.memset(h1b[:, :, 0:WP:WP - 1], 0.0))
                marks["conv2"] = steps[0]

            def prepare_norms():
                dve.wait_ge(prep_pe, 10)
                step(nc.vector.tensor_copy(col96[:, :], banks[7][0:C2, 0:T_ROWS]))
                step(nc.vector.tensor_copy(colm[:, :, :], banks[6][:, 0:2 * 64].rearrange("p (c u) -> p c u", c=2)[:, :, 0:U_ROWS]), "columns")
                step(nc.vector.tensor_scalar_add(inv96[:, L1:], col96[:, T_VAR:T_VAR + 3], BN_EPS))
                step(nc.vector.tensor_scalar_add(invm[:, :, :], colm[:, :, U_VAR:U_VAR + 2], BN_EPS), "variances")

            def prepare_pairs():
                dve.wait_ge(prep_act, 3)
                fold_norm(inv96[:, L1:], shift96[:, L1:], *(col96[:, t:t + 3] for t in (T_GAMMA, T_MEAN, T_BETA)))
                fold_norm(invm[:, :, :], shiftm[:, :, :], *(colm[:, :, t:t + 2] for t in (U_GAMMA, U_MEAN, U_BETA)))
                step(nc.vector.tensor_scalar(norm1[:, 0:M1], ident[:, :], invm[:, 0, 0:1], None, ALU.mult))
                step(nc.vector.tensor_scalar(norm1[0:M2, M1:M], ident[0:M2, 0:M2], invm[0:M2, 1, 0:1], None, ALU.mult))
                step(nc.vector.tensor_scalar(norm3[:, :], ident[0:C, 0:C], inv96[0:C, L2:L2 + 1], None, ALU.mult))
                dve.wait_ge(prep_pe, 12)
                for n, (layer, s0, pwb) in enumerate(((L1, T_S1, T_PWB1), (L3, T_S3, T_PWB3))):
                    step(nc.vector.scalar_tensor_tensor(out=conv_bias[:, n:n + 1], in0=banks[7][0:C2, 64 + n:65 + n],
                                                        scalar=col96[:, pwb:pwb + 1], in1=inv96[:, layer:layer + 1],
                                                        op0=ALU.add, op1=ALU.mult))
                    step(nc.vector.tensor_tensor(conv_bias[:, n:n + 1], conv_bias[:, n:n + 1], shift96[:, layer:layer + 1], ALU.add))
                    step(nc.vector.tensor_tensor(wt_f.rearrange("p (k g o) -> p k g o", k=3, g=4),
                                                 columns(col96[:, :], s0, [[1, 3], [3, 4], [0, C]]),
                                                 columns(pw[layer][:, :], 0, [[0, 3], [0, 4], [1, C]]), ALU.mult))
                    own, beside = (wt_f.rearrange("p (k b o) -> p k b o", k=3, b=2)[:, :, b, :] for b in range(2))
                    for src, (hi, lo) in ((own, (wt_h[layer][0:C2, 0:3, :], wt_l[layer][0:C2, 0:3, :])),
                                          (beside, [t[:, :, :].bitcast(F32R) for t in wt_beside[layer]])):
                        step(nc.vector.tensor_copy(hi, src))
                        step(nc.vector.tensor_tensor(lo, src, hi.bitcast(F32), ALU.subtract))
                marks["pairs"] = steps[0]

            def prepare_experts():
                for tile in (pc, lin, lin_const):
                    step(nc.vector.memset(tile[:], 0.0))
                for tile in (pick, ew_h, ew_l):
                    step(nc.vector.memset(tile[:, :].bitcast(F32), 0.0))
                step(nc.vector.tensor_tensor(pick[:, C:C2], ident[0:C2, 0:C], ident[0:C2, C:C2], ALU.add))
                dve.wait_ge(prep_pe, 15)
                step(nc.vector.tensor_tensor(wpw[:, :, :], wpw[:, :, :], columns(banks[7][0:C2, :], 192, [[0, EXPERTS], [1, M]]), ALU.mult))
                step(nc.vector.tensor_tensor(wpl[:, :, :, :].rearrange("p e c f -> p (e c) f"),
                                             wpl[:, :, :, :].rearrange("p e c f -> p (e c) f"),
                                             columns(banks[7][:, :], 128, [[0, 2 * EXPERTS], [1, C]]), ALU.mult))
                step(nc.vector.memset(mask_half[:, :], 0.0))
                for half in range(2):
                    step(nc.vector.memset(mask_half[half * M2:(half + 1) * M2, half:half + 1], 1.0))
                for c in range(2):
                    w_in = colm[:, c, U_WDW:U_ROWS].rearrange("p (e t) -> p t e", e=EXPERTS)
                    step(nc.vector.tensor_scalar(lin[:, Y_DW + c * TAPS:Y_DW + (c + 1) * TAPS, :], w_in,
                                                 invm[:, c, 1:2], None, ALU.mult))
                    step(nc.vector.tensor_scalar(lin[:, Y_DWB + c, :], colm[:, c, U_BDW:U_BDW + EXPERTS], invm[:, c, 1:2], None, ALU.mult))
                    step(nc.vector.tensor_scalar(lin[:, Y_B1 + c, :], colm[:, c, U_BPW:U_BPW + EXPERTS], invm[:, c, 0:1], None, ALU.mult))
                    step(nc.vector.tensor_copy(lin_const[:, Y_DWB + c:Y_DWB + c + 1], shiftm[:, c, 1:2]))
                    step(nc.vector.tensor_copy(lin_const[:, Y_B1 + c:Y_B1 + c + 1], shiftm[:, c, 0:1]))
                step(nc.vector.tensor_scalar(lin[0:C2, Y_B3, :], col96[:, T_BPWL:T_BPWL + EXPERTS], inv96[:, L2:L2 + 1], None, ALU.mult))
                step(nc.vector.tensor_copy(lin_const[0:C2, Y_B3:Y_B3 + 1], shift96[:, L2:L2 + 1]))
                step(nc.vector.memset(h1a[:, 0:H + 2:H + 1, :], 0.0))
                step(nc.vector.memset(h1a[:, :, 0:WP:WP - 1], 0.0))

            def norms_begin(image):
                attn_chain.begin(dve, image)
                dve.wait_ge(squared, 16 * image + 16)
                attn_chain(nc.vector.tensor_reduce(s1[:, :, :], tokens(Q_AT, [[K_AT - Q_AT, 2]]), axis=AX.X, op=ALU.add))
                attn_chain(nc.vector.tensor_scalar_add(s1[:, :, :], s1[:, :, :], 1e-7))
                nc.vector.reciprocal(u[:, :, :], s1[:, :, :]).then_inc(u_ready, 1)
                dve.wait_ge(q4_ready, image + 1)
                dve.wait_ge(u_ready, image + 1)
                attn_chain(nc.vector.tensor_reduce(s2[:, 0, :], q4.rearrange("p (n c) -> p n c", c=C), axis=AX.X, op=ALU.add))
                attn_chain(nc.vector.tensor_tensor(s2[:, 0, :], s2[:, 0, :], u[:, 0, :], ALU.mult))
                attn_chain(nc.vector.tensor_tensor(s2[:, 0, :], s2[:, 0, :], u[:, 0, :], ALU.mult))
                nc.vector.tensor_scalar_max(s2[:, 0, :], s2[:, 0, :], 1e-12).then_inc(norm_q, 1)
                attn_chain.end()

            def norms_end(image):
                attn2_chain.begin(dve, image)
                dve.wait_ge(root_q, image + 1)
                attn2_chain(nc.vector.reciprocal(r[:, 0, :], s2[:, 0, :]))
                attn2_chain(nc.vector.tensor_tensor(r[:, 0, :], r[:, 0, :], u[:, 0, :], ALU.mult))
                q = tokens(Q_AT)
                nc.vector.tensor_tensor(q, q, columns(r[:, :, :], 0, [[1, 2 * RUN], [0, C]]), ALU.mult).then_inc(q_scaled, 1)
                attn2_chain.end()

            def sums_out(image):
                bank = ring_a.bank(A_G)
                dve.wait_ge(g_done, image + 1)
                nc.vector.tensor_copy(gt[:, :], bank[0:SUMS, 0:C]).then_inc(gt_ready, 1)
                nc.vector.tensor_tensor(gm[:, :], bank[0:SUMS, 0:C], gram_mask[:, :], ALU.mult).then_inc(gt_ready, 1)

            def conv1_weights(image):
                bank = ring_a.bank(A_M2)
                dve.wait_ge(m2_done, image + 1)
                nc.vector.tensor_scalar_max(rk[:, :], bank[0:C, C2:C2 + 1], 1e-12).then_inc(norm_k, 1)
                dve.wait_ge(root_k, image + 1)
                nc.vector.reciprocal(rk[:, :], rk[:, :]).then_inc(rk_ready, 1)
                dve.wait_ge(rk_ready, image + 1)
                nc.vector.tensor_scalar(w1_cur[0:C, :], bank[0:C, 0:C2], rk[:, 0:1], None, ALU.mult).then_inc(w1_ready, 1)

            def depthwise_at(image, place, steps=slice(None)):
                if image is not None:
                    done = sum(steps_at[:place])
                    chosen = range(done, done + steps_at[place])[steps]
                    depthwise(image, chosen.start, chosen.stop)

            def depthwise(image, s0, s1, skipped=0):
                for s in range(s0, s1):
                    n, t = tap_of_step(s)
                    _, dst, c, _ = unit(n)
                    weight = dyn[:, Y_DW + c * TAPS + t:Y_DW + c * TAPS + t + 1]
                    if s == 0:
                        after(dve, stored, 16 * WQ * image)
                        dve.wait_ge(h1b_ready, H1B_WRITES * (image + 1))
                    if n >= 2 and t == 1:
                        dve.wait_ge(tap1_ready, (UNITS - 2) * image + n - 1 - (len(PE_UNITS) if skipped else 0))
                    if t == 0:
                        nc.vector.tensor_scalar(dst, tap_input(n, 0), weight, dyn[:, Y_DWB + c:Y_DWB + c + 1],
                                                ALU.mult, ALU.add).then_inc(tap_step, 1)
                    else:
                        dve.wait_ge(tap_step, TAP_STEPS * image + s - 1 - skipped)
                        nc.vector.scalar_tensor_tensor(out=dst, in0=tap_input(n, t), scalar=weight,
                                                       in1=dst, op0=ALU.mult, op1=ALU.add).then_inc(tap_step, 1)

            def halo_out(f):
                bank = ring_b.bank(B_HALO)
                dve.wait_ge(expand_done, 13 * f + 1)
                for n, (half, r) in enumerate(((slice(0, M2), PAIRS + 1), (slice(M2, M1), 0))):
                    nc.vector.tensor_scalar(h1b[half, r, 1:W + 1], bank[half, n * W:(n + 1) * W],
                                            dyn[half, Y_B1 + 1:Y_B1 + 2], 0.0, ALU.add, ALU.max).then_inc(h1b_ready, 1)

            def h1b_rows(f, n):
                par, g = n % 2, n // 2
                r0 = 1 + 2 * ROWS * g + par
                dve.wait_ge(expand_done, 13 * f + n + 2)
                nc.vector.tensor_scalar(h1b[:, r0:r0 + 2 * ROWS - 1:2, 1:W + 1],
                                        ring_b.bank(B_E + n)[:, :].rearrange("p (j w) -> p j w", w=W),
                                        dyn[:, Y_B1 + 1:Y_B1 + 2], 0.0, ALU.add, ALU.max).then_inc(h1b_ready, 1)

            def conv1_out(image, f):
                if image is not None:
                    after(dve, l3_done, PCHUNKS * (image - 1))
                    after(dve, x2_copied, 16 * X2_COPIES * image)
                if f is not None:
                    halo_out(f)
                for k in range(BEFORE, CHUNKS + 1):
                    for n in expand_beside[k] if f is not None else ():
                        if n < 4:
                            h1b_rows(f, n)
                    if k < 1 or image is None:
                        continue
                    depthwise_at(f, BY_CONV1 + k - 1)
                    dve.wait_ge(y1_slope, CHUNKS * image + k)
                    bank = ring_c.bank(C_1 + k - 1)
                    buffer = (k - 1) % Y1_BUFFERS
                    nc.vector.tensor_tensor(y1[:, buffer, :], bank[0:C2, :], y1[:, buffer, :], ALU.max).then_inc(y1_max, 1)
                    dve.wait_ge(y1_max, CHUNKS * image + k)
                    nc.vector.tensor_copy(y1_view(y1_h, k - 1), y1_tokens(k - 1)).then_inc(y1h_ready, 1)

            def conv2_out(f, back):
                for k in range(CHUNKS):
                    low = k // 2 - 1 if k >= 3 and k % 2 == 1 else None
                    if low is None:
                        depthwise_at(back, BY_CONV2 + k)
                    else:
                        depthwise_at(back, BY_CONV2 + k, steps=slice(0, 1))
                        l1_low_part(f, low)
                        depthwise_at(back, BY_CONV2 + k, steps=slice(1, None))
                    dve.wait_ge(y2_slope, CHUNKS * f + k + 1)
                    dst = y2[(k // 2) % 2][:, (k % 2) * BANK:(k % 2 + 1) * BANK]
                    nc.vector.scalar_tensor_tensor(out=dst, in0=ring_c.bank(C_2 + k)[0:C2, :],
                                                   scalar=col0[:, Z_B2:Z_B2 + 1], in1=dst,
                                                   op0=ALU.add, op1=ALU.max).then_inc(y2_ready, 1)
                    if k >= 2 and k % 2 == 0:
                        w3_out(f, k // 2 - 1)

            def w3_out(f, m):
                dve.wait_ge(w3_done, PCHUNKS * f + m + 1)
                if m >= 2:
                    dve.wait_ge(ah1_ready, PCHUNKS * f + m - 1)
                x_in = columns(xcm[0:C2, :], m * ROWS * WQ, [[1, ROWS * WQ], [128, RUN]])
                nc.vector.scalar_tensor_tensor(
                    out=v[:, m % 2, :].rearrange("p (a b) -> p a b", b=RUN),
                    in0=ring_b.bank(B_W3 + m)[0:C2, :].rearrange("p (a b) -> p a b", b=RUN),
                    scalar=col0[:, Z_B3:Z_B3 + 1], in1=x_in, op0=ALU.add, op1=ALU.add).then_inc(v_ready, 1)

            def l1_low_part(f, m):
                dve.wait_ge(ah1_ready, PCHUNKS * f + m + 1)
                low_part(a_h[L1], a_l[L1], v, m).then_inc(al1_ready, 1)

            def low_part(hi, lo, src, m):
                rows = slice(m * ROWS + 1, (m + 1) * ROWS + 1)
                return nc.vector.scalar_tensor_tensor(
                    out=lo[:, rows, 1:W + 1], in0=src[:, m % 2, :].rearrange("p (j w) -> p j w", w=W), scalar=0.0,
                    in1=hi[:, rows, 1:W + 1].bitcast(F32), op0=ALU.max, op1=ALU.subtract)

            def l3_low_part(b, m):
                dve.wait_ge(v3_ready, PCHUNKS * b + m + 1)
                dve.wait_ge(ah3_ready, PCHUNKS * b + m + 1)
                low_part(a_h[L3], a_l[L3], v, m).then_inc(al3_ready, 1)

            def x2_low_part(f, m):
                dve.wait_ge(x2h_ready, PCHUNKS * f + m + 1)
                rows = slice(m * ROWS, (m + 1) * ROWS)
                nc.vector.tensor_tensor(x2_l[:, rows, :], y1[:, m % 2, :].rearrange("p (j w) -> p j w", w=W),
                                        x2_h[:, rows, :].bitcast(F32), ALU.subtract).then_inc(x2l_ready, 1)

            def mean_out(f):
                dve.wait_ge(x2_ready, PCHUNKS * f + PCHUNKS)
                nc.vector.tensor_reduce(mean[:, :], msum[:, :], axis=AX.X, op=ALU.add).then_inc(mean_sum, 1)
                dve.wait_ge(mean_sum, f + 1)
                nc.vector.tensor_scalar(mean_b[:, :], ones[0:C2, :], mean[:, 0:1], 1.0 / TOKENS, ALU.mult, ALU.mult)\
                    .then_inc(mean_ready, 1)

            def route(f):
                dve.wait_ge(rw_done, f + 1)
                nc.vector.tensor_tensor(rwz[:, :], ring_b.bank(B_RW)[:, 0:EXPERTS], br[:, :], ALU.add).then_inc(rwz_ready, 1)

            def mix(chain, dst, src):
                chain(nc.vector.tensor_scalar(dst, src[:, 0, :], rw[0:dst.shape[0], 0:1], None, ALU.mult))
                for e in range(1, EXPERTS):
                    chain(nc.vector.scalar_tensor_tensor(out=dst, in0=src[:, e, :], scalar=rw[0:dst.shape[0], e:e + 1],
                                                         in1=dst, op0=ALU.mult, op1=ALU.add))

            def mix_weights(f):
                weight_chain.begin(dve, f)
                dve.wait_ge(rw_ready, f + 1)
                weight_chain(nc.vector.tensor_tensor(prod[:, :, :], lin[:, :, :], columns(rw[:, :], 0, [[0, Y_ALL], [1, EXPERTS]]), ALU.mult))
                weight_chain(nc.vector.tensor_reduce(dyn[:, :], prod[:, :, :], axis=AX.X, op=ALU.add))
                weight_chain(nc.vector.tensor_tensor(dyn[:, :], dyn[:, :], lin_const[:, :], ALU.add))
                mix(weight_chain, wk[:, :], wpw[:, :, :])
                parts = ((slice(0, M1), slice(0, M1)), (slice(E_OTHER, E_OTHER + M2), slice(M1, M)))
                for dst, src in parts:
                    weight_chain(nc.vector.tensor_copy(ew_h[:, dst], wk[:, src]))
                for dst, src in parts:
                    weight_chain(nc.vector.tensor_tensor(ew_l[:, dst], wk[0:C, src], ew_h[0:C, dst].bitcast(F32), ALU.subtract))
                weight_chain.end()
                project_weight_chain.begin(dve, f)
                mix(project_weight_chain, pk[:, :, :].rearrange("p c f -> p (c f)"),
                    wpl[:, :, :, :].rearrange("p e c f -> p e (c f)"))
                project_weight_chain.end()
                nc.vector.tensor_copy(pc[:, 0, C:C2], pk[:, 0, :]).then_inc(pc_ready, 1)
                for half in range(2):
                    nc.vector.tensor_scalar(pc[:, 1 + half, C:C2], pk[:, 1, :], mask_half[:, half:half + 1], None, ALU.mult)\
                        .then_inc(pc_ready, 1)

            def iteration(f, attn, back):
                conv2_out(f, back)
                depthwise_at(back, BY_PROJECT)
                if back is not None:
                    l3_low_part(back, 0)
                depthwise_at(back, BY_PROJECT + 1)
                w3_out(f, PCHUNKS - 1)
                depthwise_at(back, BY_PROJECT + 2)
                l1_low_part(f, PCHUNKS - 1)
                if back is not None:
                    l3_low_part(back, 1)
                    depthwise_at(back, BY_PROJECT + 3)
                else:
                    prepare_experts()
                x2_low_part(f, 0)
                x2_low_part(f, 1)
                if back is not None:
                    l3_low_part(back, 2)
                    l3_low_part(back, 3)
                x2_low_part(f, 2)
                mean_out(f)
                x2_low_part(f, 3)
                route(f)
                if attn is not None:
                    norms_begin(attn)
                mix_weights(f)
                if attn is not None:
                    norms_end(attn)
                    sums_out(attn)
                    conv1_weights(attn)
                conv1_out(attn, f)
                if attn is None:
                    depthwise(f, 0, FIRST_STEPS)
                    depthwise(f, FIRST_STEPS + PAIR_STEPS, TAP_STEPS, skipped=PAIR_STEPS)

            prepare_conv2()
            norms_begin(0)
            norms_end(0)
            sums_out(0)
            conv1_weights(0)
            conv1_out(0, None)
            prepare_norms()
            prepare_pairs()
            iteration(0, 1, None)
            with dve.Fori(1, IMAGES - 1) as f:
                iteration(f, f + 1, f - 1)
            iteration(IMAGES - 1, None, IMAGES - 2)
            for m in range(PCHUNKS):
                l3_low_part(IMAGES - 1, m)

        def wait(sp, semaphore, value):
            if not isinstance(value, int) or value > 0:
                sp.wait_ge(semaphore, value)
                sp.sem_inc(sync_waits, 1)

        def x_rows(image):
            return a["x"][image].rearrange("(j b) (q i) c -> b q j i c", b=2, q=WQ)

        def load_xa(sp, image, projected):
            src = x_rows(image)
            wait(sp, project_done, projected)
            by_column = xa.rearrange("p (i b c) -> p b i c", b=2, c=C)
            for n in range(2 * WQ):
                par, q = n % 2, n // 2
                sp.dma_start(by_column[q::WQ, par], src[par, q]).then_inc(xa_loaded, 16)

        def load_x(sp, image):
            src = x_rows(image)
            wait(sp, xqt_done, CHUNKS * image)
            for n in range(2 * WQ):
                par, q = n % 2, n // 2
                sp.dma_start(tok[q::WQ, par, :, X_AT:X_AT + C], src[par, q]).then_inc(x_loaded, 16)

        def copy_beside(sp, n, half):
            r0, rows = half * PAIRS // 2, PAIRS // 2
            rest = C - BEHIND
            below, above = slice(r0 + 2, r0 + rows + 2), slice(r0, r0 + rows)
            here, behind = slice(r0, r0 + rows), slice(r0 + 1, r0 + rows + 1)
            own, dst = a_parts[n][:, :, :, :].bitcast(F32), b_parts.bitcast(F32)
            for to, frm in ((own[C2:128, :, behind, :], own[0:BEHIND, :, below, :]),
                            (dst[0:rest, :, here, :], own[BEHIND:C, :, below, :]),
                            (dst[rest:APART, :, here, :], own[C:C2, :, above, :])):
                to, frm = (t.rearrange("p a h w -> p a (h w)") for t in (to, frm))
                sp.dma_start(to, frm).then_inc(b_copied[n][half], 16)
            for part in range(2):
                for to, frm in ((dst[APART:APART + rest, part, here, 1:W + 1], own[BEHIND:C, part, below, 0:W]),
                                (dst[APART + rest:128, part, here, 1:W + 1], own[C:C2, part, above, 0:W])):
                    sp.dma_start(to, frm).then_inc(b_copied[n][half], 16)

        def copy_x2(sp, f):
            wait(sp, x2h_ready, PCHUNKS * f + PCHUNKS)
            wait(sp, x2l_ready, PCHUNKS * f + PCHUNKS)
            wait(sp, project_done, PCHUNKS * f)
            for par in range(2):
                for n, src in enumerate((x2_h, x2_l)):
                    sp.dma_start(x2[par][n * C:(n + 1) * C, :].bitcast(F32).rearrange("p (j w) -> p j w", w=W),
                                 src[par * C:(par + 1) * C, :, :].bitcast(F32)).then_inc(x2_copied, 16)

        def store(sp, image):
            wait(sp, ot_ready, 4 * image + 4)
            dst = out[image].rearrange("(j b) (q i) c -> q j b (i c)", b=2, q=WQ)
            for q in range(WQ):
                sp.dma_start(dst[q], ot[q::WQ, :].rearrange("p (b n) -> p b n", b=2)).then_inc(stored, 16)

        def beside_l1(sp, f):
            for half in range(2):
                chunks = 3 + half
                wait(sp, ah1_ready, PCHUNKS * f + chunks)
                wait(sp, al1_ready, PCHUNKS * f + chunks)
                wait(sp, conv2_done, CHUNKS * f + 3 + 2 * half)
                copy_beside(sp, L1, half)

        def beside_l3(sp, b, l1_images):
            for half in range(2):
                wait(sp, l1_done, PCHUNKS * l1_images - 2 + 2 * half)
                chunks = 3 + half
                wait(sp, ah3_ready, PCHUNKS * b + chunks)
                wait(sp, al3_ready, PCHUNKS * b + chunks)
                copy_beside(sp, L3, half)

        @block.sync
        def _(sp):
            for dst, src in first_loads[0:NORM_LOADS]:
                sp.dma_start(dst, src).then_inc(norm_loaded, 16)
            sp.wait_ge(cleared, len(cleared_tiles))
            for dst, src in first_loads[NORM_LOADS:]:
                sp.dma_start(dst, src).then_inc(first_loaded, 16)
            load_xa(sp, 0, 0)
            load_x(sp, 0)
            sp.dma_start(w2_f.rearrange("p (t o) -> p t o", t=TAPS), a["L0_conv_w2"].rearrange("h w i o -> i (h w) o"))\
                .then_inc(w2_loaded, 16)
            for dst, src in loads:
                sp.dma_start(dst, src).then_inc(loaded, 16)

            sp.wait_ge(xt_done, 4)
            sp.wait_ge(norm_q, 1)
            load_xa(sp, 1, 0)
            sp.wait_ge(prep_dve, marks["pairs"])
            for n in (L1, L3):
                for src, tile in zip(wt_beside[n], (wt_h[n], wt_l[n])):
                    dst = tile[:, :, :].bitcast(F32)
                    for to, frm in ((dst[C2:128, 0:3, :], src[0:BEHIND, :, :]), (dst[0:APART, 3, :], src[BEHIND:C2, 1, :]),
                                    (dst[APART:128, 3, :], src[BEHIND:C2, 0, :]), (dst[0:APART, 4, :], src[BEHIND:C2, 2, :])):
                        sp.dma_start(to, frm).then_inc(wt_placed, 16)

            def iteration(f, attn, back):
                beside_l1(sp, f)
                if attn is not None and back is not None:
                    load_xa(sp, attn, PCHUNKS * (f - 1) + 2)
                if back is not None:
                    beside_l3(sp, back, f + 1)
                if attn is not None:
                    load_x(sp, attn)
                copy_x2(sp, f)
                if back is not None:
                    store(sp, back)

            iteration(0, 1, None)
            with sp.Fori(1, IMAGES - 1) as f:
                iteration(f, f + 1, f - 1)
            iteration(IMAGES - 1, None, IMAGES - 2)
            beside_l3(sp, IMAGES - 1, IMAGES)
            store(sp, IMAGES - 1)
            sp.wait_ge(stored, 16 * WQ * IMAGES)

        @block.gpsimd
        def _(pool):
            nc.gpsimd.memset(ident[:, :], 0.0).then_inc(masks_ready, 1)
            nc.gpsimd.memset(gram_mask[:, :], 0.0).then_inc(masks_ready, 1)
            pool.wait_ge(masks_ready, 2)
            nc.gpsimd.affine_select(out=ident[:, :], in_=ident[:, :], compare_op=ALU.not_equal, fill=1.0,
                                    base=0, pattern=[[-1, 128]], channel_multiplier=1).then_inc(masks_ready, 1)
            nc.gpsimd.affine_select(out=gram_mask[:, :], in_=gram_mask[:, :], compare_op=ALU.not_equal, fill=1.0,
                                    base=-C, pattern=[[-1, C]], channel_multiplier=1).then_inc(masks_ready, 1)

            def scale_k(image):
                pool.wait_ge(squared, 16 * image + 16)
                pool.wait_ge(u_ready, image + 1)
                k = tokens(K_AT)
                nc.gpsimd.tensor_tensor(k, k, columns(u[:, :, :], 2 * RUN, [[1, 2 * RUN], [0, C]]), ALU.mult).then_inc(k_scaled, 1)

            def split_y1(image):
                for k in range(CHUNKS):
                    pool.wait_ge(y1h_ready, CHUNKS * image + k + 1)
                    nc.gpsimd.tensor_tensor(y1_view(y1_l, k), y1_tokens(k), y1_view(y1_h, k).bitcast(F32),
                                            ALU.subtract).then_inc(y1l_ready, 1)

            scale_k(0)
            split_y1(0)
            with pool.Fori(1, IMAGES) as image:
                scale_k(image)
                split_y1(image)

        @block.tensor
        def _(pe):
            pe.wait_ge(norm_loaded, 16 * NORM_LOADS)
            pe.wait_ge(masks_ready, 4)
            nc.tensor.transpose(banks[0][0:C2, 0:Z_ROWS], tab0[:, :], ident[0:Z_ROWS, 0:Z_ROWS]).then_inc(prep_pe, 1)
            pe.wait_ge(prep_dve, marks["bn_fold"])
            nc.tensor.matmul(banks[2][0:C2 + 1, 0:3 * C], bn_fold[:, :], wqkv[:, :], start=True, stop=True).then_inc(prep_pe, 1)
            nc.tensor.matmul(banks[3][0:C, 0:C + 1], wqkv[:, 2 * C:3 * C], bn_fold[:, C:], start=True, stop=True).then_inc(prep_pe, 1)
            pe.wait_ge(prep_dve, marks["wv_t"])
            pe.wait_ge(first_loaded, 16 * (len(first_loads) - NORM_LOADS))
            nc.tensor.matmul(banks[4][0:C, 0:C + 1], wln[:, :], wv_t[:, :], start=True, stop=True).then_inc(prep_pe, 1)
            pe.wait_ge(prep_dve, marks["p1"])
            nc.tensor.matmul(banks[5][0:SUMS, 0:C2], p1[:, :], w1a[:, :], start=True, stop=True).then_inc(prep_pe, 1)
            nc.tensor.matmul(banks[6][0:C2 + 1, 0:C2], p1b[:, :], w1a[:, :], start=True, stop=False)
            nc.tensor.matmul(banks[6][0:C2 + 1, 0:C2], ident[0:C2 + 1, 0:C2 + 1], w1b[:, :], start=False, stop=True).then_inc(prep_pe, 1)
            pe.wait_ge(prep_dve, marks["attention"])

            def prepare_columns():
                pe.wait_ge(loaded, 16 * len(loads))
                nc.tensor.transpose(banks[7][0:C2, 0:T_ROWS], tab96[:, :], ident[0:T_ROWS, 0:T_ROWS]).then_inc(prep_pe, 1)
                nc.tensor.transpose(banks[6][:, 0:U_ROWS], tab192[:, 0:M1], ident[0:U_ROWS, 0:U_ROWS]).then_inc(prep_pe, 1)
                for half in range(2):
                    nc.tensor.matmul(banks[6][half * M2:(half + 1) * M2, 64:64 + U_ROWS], tab192[:, M1:M],
                                     ident[0:U_ROWS, 0:U_ROWS], start=True, stop=True).then_inc(prep_pe, 1)

            def prepare_biases():
                pe.wait_ge(prep_dve, marks["columns"])
                for n, (layer, t) in enumerate(((L1, T_DWB1), (L3, T_DWB3))):
                    nc.tensor.matmul(banks[7][0:C2, 64 + n:65 + n], pw[layer][0:C, :], col96[0:C, t:t + 1],
                                     start=True, stop=True).then_inc(prep_pe, 1)

            def transpose_x(image, chunks):
                for n in chunks:
                    if n == 0:
                        pe.wait_ge(xa_loaded, 32 * WQ * (image + 1))
                    bank = ring_a.take(pe, image, A_XT + n)
                    for m in range(4):
                        i = 4 * n + m
                        last = nc.tensor.transpose(bank[0:C2, m * 128:(m + 1) * 128],
                                                   xa[:, i * C2:(i + 1) * C2], ident[:, :])
                    last.then_inc(xt_done, 1)

            def attention_scores(image):
                for n in range(8):
                    bank = ring_a.take(pe, image, A_QK + n)
                    if n % 2 == 0:
                        pe.wait_ge(xcm_ready, 4 * image + n // 2 + 1)
                    for m in range(2):
                        i = 2 * n + m
                        last = nc.tensor.matmul(bank[:, m * 2 * C2:(m + 1) * 2 * C2], xcm[:, i * 128:(i + 1) * 128],
                                                qkw[:, :], start=True, stop=True)
                    last.then_inc(qk_done, 1)

            def attention_sums(image):
                bank = ring_a.take(pe, image, A_G)
                pe.wait_ge(x_loaded, 32 * WQ * (image + 1))
                pe.wait_ge(k_scaled, image + 1)
                for par in range(2):
                    for i in range(RUN):
                        first, final = par == 0 and i == 0, par == 1 and i == RUN - 1
                        last = nc.tensor.matmul(bank[0:SUMS, 0:C], token(par, i, X_AT, SUMS), token(par, i, K_AT, C),
                                                start=first, stop=final)
                last.then_inc(g_done, 1)

            def attention_weights(image):
                bank = ring_a.take(pe, image, A_M2)
                pe.wait_ge(gt_ready, 2 * image + 2)
                nc.tensor.matmul(bank[0:C, 0:C2], gt[:, :], wva_aug[:, :], start=True, stop=True)
                nc.tensor.matmul(bank[0:C, C2:C2 + 1], gm[:, :], ones[0:SUMS, 0:1], start=True, stop=True).then_inc(m2_done, 1)

            def conv1(image, f):
                for k in range(BEFORE, CHUNKS + 1):
                    if image is not None and 0 <= k < CHUNKS:
                        if k == 0:
                            pe.wait_ge(q_scaled, image + 1)
                        par, i0 = k // 4, 4 * (k % 4)
                        bank = ring_a.take(pe, image, A_XQ + k)
                        for m in range(4):
                            last = nc.tensor.transpose(bank[0:C2, m * 128:(m + 1) * 128],
                                                       token(par, i0 + m, Q_AT, C2), ident[:, :])
                        last.then_inc(xqt_done, 1)
                    if image is not None and k > 0:
                        if k == 1:
                            pe.wait_ge(w1_ready, image + 1)
                        bank = ring_c.take(pe, image, C_1 + k - 1)
                        pe.wait_ge(xq_ready, CHUNKS * image + k)
                        nc.tensor.matmul(bank[0:C2, :], w1_cur[:, :], xq[:, (k - 1) % 2, :], start=True, stop=True)\
                            .then_inc(conv1_done, 1)
                    for n in expand_beside[k] if f is not None else ():
                        expand(f, n)

            def conv2(image):
                for k in range(CHUNKS):
                    bank = ring_c.take(pe, image, C_2 + k)
                    for n, (wgt, src, ready) in enumerate(((w2_h, y1_h, y1h_ready), (w2_l, y1_h, y1h_ready),
                                                           (w2_h, y1_l, y1l_ready))):
                        if k == 0 and n != 1:
                            pe.wait_ge(ready, CHUNKS * image + CHUNKS)
                        for t in range(TAPS):
                            rows, cols = slice(k * ROWS + t // 3, k * ROWS + t // 3 + ROWS), slice(t % 3, t % 3 + W)
                            last = nc.tensor.matmul(bank[0:C2, :], wgt[:, t, :], src[:, rows, cols],
                                                    start=t + n == 0, stop=t == TAPS - 1 and n == 2)
                    last.then_inc(conv2_done, 1)
                    if k >= 2 and k % 2 == 0:
                        w3(image, k // 2 - 1)

            def w3(image, m):
                bank = ring_b.take(pe, image, B_W3 + m)
                pe.wait_ge(y2_ready, CHUNKS * image + 2 * m + 2)
                rows = y2[m % 2].rearrange("p (j b w) -> p j b w", b=2, w=W)
                for par in range(2):
                    last = nc.tensor.matmul(bank[0:C2, :], w3eo[:, par, :], rows[:, :, par, :], start=par == 0, stop=par == 1)
                last.then_inc(w3_done, 1)

            def pair_conv(image, layer, ring, first, done, chunks):
                for m in chunks:
                    bank = ring.take(pe, image, first + m)
                    if m % 2 == 0:
                        pe.wait_ge(b_copied[layer][m // 2], 16 * B_COPIES * (image + 1))
                    rows = slice(m * ROWS, (m + 1) * ROWS)
                    for n, (wgt, part) in enumerate(((wt_h, 0), (wt_l, 0), (wt_h, 1))):
                        own, beside = a_parts[layer][:, part, 1:PAIRS + 1, :], b_parts[:, part, :, :]
                        for kw in range(3):
                            nc.tensor.matmul(bank[0:C2, :], wgt[layer][:, kw, :], own[:, rows, kw:kw + W],
                                             start=n + kw == 0, stop=False)
                        nc.tensor.matmul(bank[0:C2, :], wgt[layer][:, 3, :], beside[:, rows, 1:W + 1], start=False, stop=False)
                        last = nc.tensor.matmul(bank[0:C2, :], wgt[layer][0:APART, 4, :], beside[0:APART, rows, 2:W + 2],
                                                start=False, stop=n == 2)
                    last.then_inc(done, 1)

            def routing(image):
                bank = ring_b.take(pe, image, B_RW)
                pe.wait_ge(mean_ready, image + 1)
                nc.tensor.matmul(bank[:, 0:EXPERTS], mean_b[:, :], wr[:, :], start=True, stop=True).then_inc(rw_done, 1)

            def expand_rows(out_ap, at, par, rows, start, stop):
                src = x2[par][:, rows.start * W:rows.stop * W]
                nc.tensor.matmul(out_ap, ew_h[:, at:at + M1], src, start=start, stop=False)
                return nc.tensor.matmul(out_ap, ew_l[:, at:at + M1], src[0:C, :], start=False, stop=stop)

            def expand_halo(image):
                pe.wait_ge(weight_chain.sem, weight_chain.each * (image + 1))
                pe.wait_ge(x2_copied, 16 * X2_COPIES * (image + 1))
                bank = ring_b.take(pe, image, B_HALO)
                half = PAIRS // 2
                expand_rows(bank[:, 0:W], E_OTHER, 0, slice(half, half + 1), True, True)
                expand_rows(bank[:, W:2 * W], E_BOTTOM, 1, slice(half - 1, half), True, True).then_inc(expand_done, 1)

            def expand(image, n):
                bank = ring_b.take(pe, image, B_E + n)
                par, g = n % 2, (n if n < 4 else n - 4) // 2
                parts = (((E_OTHER, g), (E_BOTTOM, g + 2)) if n < 4 else ((0, g),))
                for part, (at, g) in enumerate(parts):
                    last = expand_rows(bank[:, :], at, par, slice(g * ROWS, (g + 1) * ROWS), part == 0, part == len(parts) - 1)
                last.then_inc(expand_done, 1)

            def last_taps(image):
                pe.wait_ge(diag_ready, TAPS)
                for n, b in enumerate(PE_BANKS):
                    pe.wait_ge(h1a_ready, H1A_WRITES * image + 2 * (((n + 1) * ROWS + 1) // (2 * ROWS) + 1))
                    for t in range(TAPS):
                        r0 = n * ROWS + t // 3
                        last = nc.tensor.matmul(banks[b][:, :], tap_diag[:, t * 128:(t + 1) * 128],
                                                h1a[:, r0:r0 + ROWS, t % 3:t % 3 + W], start=t == 0, stop=t == TAPS - 1)
                    last.then_inc(taps_done, 1)

            def project(image, chunks, last_image=False):
                for m in chunks:
                    bank = ring_d.take(pe, image, D_P + m)
                    if m == 0:
                        pe.wait_ge(pc_ready, 3 * image + 3)
                    if last_image:
                        by_pe = len(PE_UNITS)
                        finished = OTHER_UNITS + (PE_CHUNKS // by_pe * (m + 1) if m < by_pe else PE_CHUNKS + m - by_pe + 1)
                    else:
                        finished = OTHER_UNITS + m + 1
                    pe.wait_ge(h2_ready, UNITS * image + finished)
                    first = dwa[:, :, :].rearrange("p (j b) w -> p j b w", b=2)[:, m * ROWS:(m + 1) * ROWS]
                    m2 = m % 2
                    other = dwb[:, :, :].rearrange("p (j b) w -> p j b w", b=2)[:, m2 * ROWS:(m2 + 1) * ROWS]
                    for par in range(2):
                        cols = slice(C - C * par, 3 * C - C * par)
                        nc.tensor.matmul(bank[0:C2, :], pick[:, cols], x2[par][:, m * BANK:(m + 1) * BANK], start=par == 0, stop=False)
                        nc.tensor.matmul(bank[0:C2, :], pc[:, 0, cols], first[:, :, par, :], start=False, stop=False)
                        last = nc.tensor.matmul(bank[0:C2, :], pc[:, 1 + m // 2, cols], other[:, :, par, :],
                                                start=False, stop=par == 1)
                    last.then_inc(project_done, 1)

            def out_tokens(image):
                for n in range(4):
                    bank = ring_d.take(pe, image, D_OUT + n)
                    if n == 0:
                        pe.wait_ge(outc_ready, PCHUNKS * image + PCHUNKS)
                    for m in range(4):
                        i = 4 * n + m
                        last = nc.tensor.transpose(bank[:, m * C2:(m + 1) * C2], outc[:, i::RUN], ident[0:C2, 0:C2])
                    last.then_inc(outt_done, 1)

            def l1(image, chunks):
                pair_conv(image, L1, ring_b, B_L1, l1_done, chunks)

            def l3(image):
                pair_conv(image, L3, ring_d, D_L3, l3_done, range(PCHUNKS))

            def iteration(f, attn, back):
                conv2(f)
                if back is not None:
                    project(back, (0,))
                w3(f, PCHUNKS - 1)
                if back is not None:
                    project(back, (1,))
                else:
                    pe.wait_ge(prep_dve, marks["pairs"])
                    pe.wait_ge(wt_placed, 16 * WT_COPIES)
                    nc.tensor.matmul(banks[7][:, 128:128 + C], ones[0:C, :], norm3[:, :], start=True, stop=True).then_inc(prep_pe, 1)
                    for n in range(2):
                        rows, cols = slice(0, (M1, M2)[n]), slice(n * M1, (M1, M)[n])
                        nc.tensor.matmul(banks[7][0:C2, 192 + cols.start:192 + cols.stop], ones[rows, 0:C2], norm1[rows, cols],
                                         start=True, stop=True).then_inc(prep_pe, 1)
                l1(f, (0, 1))
                if back is not None:
                    project(back, (2, 3))
                if attn is not None:
                    transpose_x(attn, (0, 1))
                l1(f, (2,))
                if attn is not None:
                    transpose_x(attn, (2, 3))
                l1(f, (3,))
                if attn is not None:
                    attention_scores(attn)
                routing(f)
                if back is not None:
                    l3(back)
                if attn is not None:
                    attention_sums(attn)
                if back is not None:
                    out_tokens(back)
                if attn is not None:
                    attention_weights(attn)
                expand_halo(f)
                conv1(attn, f)

            transpose_x(0, range(4))
            attention_scores(0)
            attention_sums(0)
            attention_weights(0)
            conv1(0, None)
            prepare_columns()
            prepare_biases()
            iteration(0, 1, None)
            with pe.Fori(1, IMAGES - 1) as f:
                iteration(f, f + 1, f - 1)
            iteration(IMAGES - 1, None, IMAGES - 2)
            last_taps(IMAGES - 1)
            project(IMAGES - 1, range(PCHUNKS), last_image=True)
            l3(IMAGES - 1)
            out_tokens(IMAGES - 1)

        @block.scalar
        def _(act):
            act.wait_ge(prep_dve, marks["variance"])
            nc.scalar.activation(inv96[:, L0:L0 + 1], inv96[:, L0:L0 + 1], ACT.Sqrt).then_inc(prep_act, 1)
            act.wait_ge(prep_dve, marks["attention"])

            def x_out(image, chunks):
                for n in chunks:
                    act.wait_ge(xt_done, 4 * image + n + 1)
                    nc.scalar.activation(xcm[0:C2, n * BANK:(n + 1) * BANK], ring_a.bank(A_XT + n)[0:C2, :], ACT.Copy)\
                        .then_inc(xcm_ready, 1)

            def scores_out(image):
                for n in range(8):
                    act.wait_ge(qk_done, 8 * image + n + 1)
                    src = ring_a.bank(A_QK + n)[:, 0:4 * C2].rearrange("p (m b s c) -> p m b s c", m=2, b=2, s=2)
                    for s, at in enumerate((Q_AT, K_AT)):
                        dst = columns(tok[:, :, :, :], 2 * n * TOK + at, [[TOK, 2], [RUN * TOK, 2], [1, C]])
                        nc.scalar.activation(dst, src[:, :, :, s, :], ACT.Square).then_inc(squared, 1)

            def fourth_powers(image):
                act.wait_ge(squared, 16 * image + 16)
                nc.scalar.activation(q4.rearrange("p (n c) -> p n c", c=C), tokens(Q_AT), ACT.Square).then_inc(q4_ready, 1)

            def root_of_q(image):
                act.wait_ge(norm_q, image + 1)
                nc.scalar.activation(s2[:, 0, :], s2[:, 0, :], ACT.Sqrt).then_inc(root_q, 1)

            def root_of_k(image):
                act.wait_ge(norm_k, image + 1)
                nc.scalar.activation(rk[:, :], rk[:, :], ACT.Sqrt, scale=float(TOKENS)).then_inc(root_k, 1)

            def conv1_slope(image, f):
                for k in range(BEFORE, CHUNKS + 1):
                    if image is not None and 0 <= k < CHUNKS:
                        act.wait_ge(xqt_done, CHUNKS * image + k + 1)
                        if k >= 2:
                            act.wait_ge(conv1_done, CHUNKS * image + k - 1)
                        nc.scalar.activation(xq[0:C2, k % 2, :], ring_a.bank(A_XQ + k)[0:C2, :], ACT.Copy).then_inc(xq_ready, 1)
                    if image is not None and k > 0:
                        act.wait_ge(conv1_done, CHUNKS * image + k)
                        after(act, y1l_ready, CHUNKS * image + k - Y1_BUFFERS)
                        nc.scalar.activation(y1[:, (k - 1) % Y1_BUFFERS, :], ring_c.bank(C_1 + k - 1)[0:C2, :], ACT.Copy, scale=SLOPE)\
                            .then_inc(y1_slope, 1)
                    if f is not None:
                        for n in expand_beside[k]:
                            if n >= 4:
                                h1a_rows(f, n)

            def first_tap(image, n):
                _, dst, c, _ = unit(n)
                if n == PE_UNITS[0]:
                    act.wait_ge(h1a_ready, H1A_WRITES * (image + 1))
                nc.scalar.activation(dst, tap_input(n, 0), ACT.Identity, bias=dyn[:, Y_DWB + c:Y_DWB + c + 1],
                                     scale=dyn[:, Y_DW + c * TAPS:Y_DW + c * TAPS + 1]).then_inc(tap1_ready, 1)

            def finish_unit(image, n, skipped=0):
                _, dst, _, _ = unit(n)
                act.wait_ge(tap_step, TAP_STEPS * image + last_step(n) - skipped)
                nc.scalar.activation(dst, dst, ACT.Relu).then_inc(h2_ready, 1)

            def conv2_slope(f, back):
                if back is not None:
                    first_tap(back, 2)
                    first_tap(back, 3)
                for k in range(CHUNKS):
                    act.wait_ge(conv2_done, CHUNKS * f + k + 1)
                    after(act, w3_done, PCHUNKS * f + k // 2 - 1)
                    nc.scalar.activation(y2[(k // 2) % 2][:, (k % 2) * BANK:(k % 2 + 1) * BANK],
                                         ring_c.bank(C_2 + k)[0:C2, :], ACT.Identity, bias=b2s[:, 0:1], scale=SLOPE)\
                        .then_inc(y2_slope, 1)
                    if back is not None:
                        for n in {2: (4,), 3: (5,)}.get(k, ()):
                            first_tap(back, n)
                        for n in finished_at(BY_CONV2 + k):
                            finish_unit(back, n)
                    if k >= 2 and k % 2 == 0:
                        l1_high_part(f, k // 2 - 1)

            def l1_high_part(f, m):
                act.wait_ge(v_ready, PCHUNKS * f + m + 1)
                high_part(a_h[L1], v, m).then_inc(ah1_ready, 1)

            def high_part(hi, src, m):
                return nc.scalar.activation(hi[:, m * ROWS + 1:(m + 1) * ROWS + 1, 1:W + 1],
                                            src[:, m % 2, :].rearrange("p (j w) -> p j w", w=W), ACT.Relu)

            def project_affine(b, l1_images, m):
                act.wait_ge(project_done, PCHUNKS * b + m + 1)
                if m < 2:
                    act.wait_ge(al1_ready, PCHUNKS * l1_images + m - 1)
                else:
                    act.wait_ge(al3_ready, PCHUNKS * b + m - 1)
                src, bias = ring_d.bank(D_P + m)[0:C2, :], dyn[0:C2, Y_B3:Y_B3 + 1]
                nc.scalar.activation(v[:, m % 2, :], src, ACT.Relu, bias=bias).then_inc(v3_ready, 1)
                nc.scalar.activation(a_h[L3][:, m * ROWS + 1:(m + 1) * ROWS + 1, 1:W + 1],
                                     src.rearrange("p (j w) -> p j w", w=W), ACT.Relu, bias=bias).then_inc(ah3_ready, 1)

            def l1_out(f, chunks):
                for m in chunks:
                    act.wait_ge(l1_done, PCHUNKS * f + m + 1)
                    if m >= 2:
                        act.wait_ge(x2l_ready, PCHUNKS * f + m - 1)
                    x2_m = y1[:, m % 2, :]
                    nc.scalar.activation(x2_m, ring_b.bank(B_L1 + m)[0:C2, :], ACT.Identity,
                                         bias=conv_bias[:, 0:1], scale=inv96[:, L1:L1 + 1],
                                         accum_out=msum[:, m:m + 1]).then_inc(x2_ready, 1)
                    act.wait_ge(x2_ready, PCHUNKS * f + m + 1)
                    nc.scalar.activation(x2_h[:, m * ROWS:(m + 1) * ROWS, :], x2_m.rearrange("p (j w) -> p j w", w=W), ACT.Copy)\
                        .then_inc(x2h_ready, 1)

            def route(f):
                act.wait_ge(rwz_ready, f + 1)
                nc.scalar.activation(rw[:, :], rwz[:, :], ACT.Sigmoid).then_inc(rw_ready, 1)

            def l3_out(b, chunks):
                for m in chunks:
                    act.wait_ge(l3_done, PCHUNKS * b + m + 1)
                    nc.scalar.activation(outc[:, m * BANK:(m + 1) * BANK], ring_d.bank(D_L3 + m)[0:C2, :], ACT.Identity,
                                         bias=conv_bias[:, 1:2], scale=inv96[:, L3:L3 + 1]).then_inc(outc_ready, 1)

            def tokens_out(b):
                for n in range(4):
                    act.wait_ge(outt_done, 4 * b + n + 1)
                    src = ring_d.bank(D_OUT + n)[:, 0:4 * C2].rearrange("p (i b c) -> p b i c", b=2, c=C)
                    dst = columns(ot, 4 * n * C, [[RUN * C, 2], [C, 4], [1, C]])
                    nc.scalar.activation(dst, src, ACT.Copy).then_inc(ot_ready, 1)

            def h1a_rows(f, n):
                par, g = n % 2, (n - 4) // 2
                r0 = 1 + 2 * ROWS * g + par
                act.wait_ge(expand_done, 13 * f + n + 2)
                nc.scalar.activation(h1a[:, r0:r0 + 2 * ROWS - 1:2, 1:W + 1],
                                     ring_b.bank(B_E + n)[:, :].rearrange("p (j w) -> p j w", w=W), ACT.Relu,
                                     bias=dyn[:, Y_B1:Y_B1 + 1]).then_inc(h1a_ready, 1)

            def iteration(f, attn, back):
                conv2_slope(f, back)
                if back is not None:
                    project_affine(back, f + 1, 0)
                l1_high_part(f, PCHUNKS - 1)
                if back is not None:
                    project_affine(back, f + 1, 1)
                l1_out(f, (0,))
                if back is not None:
                    finish_unit(back, 4)
                    finish_unit(back, 5)
                l1_out(f, (1,))
                if back is not None:
                    project_affine(back, f + 1, 2)
                    project_affine(back, f + 1, 3)
                if attn is not None:
                    x_out(attn, (0, 1))
                l1_out(f, (2,))
                if attn is not None:
                    x_out(attn, (2, 3))
                l1_out(f, (3,))
                if attn is not None:
                    scores_out(attn)
                route(f)
                if attn is not None:
                    fourth_powers(attn)
                if back is not None:
                    l3_out(back, (0, 1))
                if attn is not None:
                    root_of_q(attn)
                if back is not None:
                    l3_out(back, (2, 3))
                    tokens_out(back)
                if attn is not None:
                    root_of_k(attn)
                act.wait_ge(weight_chain.sem, weight_chain.each * (f + 1))
                for t in range(TAPS) if attn is None else ():
                    nc.scalar.activation(tap_diag[:, t * 128:(t + 1) * 128], ident[:, :], ACT.Copy,
                                         scale=dyn[:, Y_DW + t:Y_DW + t + 1]).then_inc(diag_ready, 1)
                conv1_slope(attn, f)

            x_out(0, range(4))
            scores_out(0)
            fourth_powers(0)
            root_of_q(0)
            root_of_k(0)
            conv1_slope(0, None)
            act.wait_ge(prep_dve, marks["variances"])
            nc.scalar.activation(inv96[:, L1:], inv96[:, L1:], ACT.Sqrt).then_inc(prep_act, 1)
            nc.scalar.activation(invm[:, :, :], invm[:, :, :], ACT.Sqrt).then_inc(prep_act, 1)
            act.wait_ge(prep_dve, marks["pairs"])
            iteration(0, 1, None)
            with act.Fori(1, IMAGES - 1) as f:
                iteration(f, f + 1, f - 1)
            iteration(IMAGES - 1, None, IMAGES - 2)
            act.wait_ge(h1a_ready, H1A_WRITES * IMAGES)
            for n in range(OTHER_UNITS + len(PE_UNITS), UNITS):
                first_tap(IMAGES - 1, n)
            for n in range(OTHER_UNITS):
                finish_unit(IMAGES - 1, n)
            for n, b in enumerate(PE_BANKS):
                act.wait_ge(taps_done, n + 1)
                nc.scalar.activation(dwa[:, n * ROWS:(n + 1) * ROWS, :], banks[b][:, :].rearrange("p (j w) -> p j w", w=W),
                                     ACT.Relu, bias=dyn[:, Y_DWB:Y_DWB + 1]).then_inc(h2_ready, 1)
            for n in range(OTHER_UNITS + len(PE_UNITS), UNITS):
                finish_unit(IMAGES - 1, n, skipped=PAIR_STEPS)
            for m in range(PCHUNKS):
                project_affine(IMAGES - 1, IMAGES, m)
            l3_out(IMAGES - 1, range(PCHUNKS))
            tokens_out(IMAGES - 1)


def kernel(**inputs):
    import numpy as _np
    import concourse.bacc as _bacc
    from concourse import mybir as _mybir
    from concourse.bass_utils import run_bass_kernel_spmd as _run

    nc = _bacc.Bacc("TRN2", target_bir_lowering=False, num_devices=1)
    arrays, args = {}, {}
    for name, value in inputs.items():
        value = _np.ascontiguousarray(value)
        arrays[f"in_{name}_dram"] = value
        args[name] = nc.dram_tensor(f"in_{name}_dram", value.shape, _mybir.dt.from_np(value.dtype), kind="ExternalInput").ap()
    out = nc.dram_tensor("out_dram", (IMAGES, H, W, C), _mybir.dt.float32, kind="ExternalOutput").ap()
    conv_chain_kernel(nc, args, out)
    return _run(nc, [arrays], core_ids=[0]).results[0]["out_dram"]
```
